# Optimizing a Trainium2 kernel written in Bass

```python
import numpy as np
import jax
import jax.numpy as jnp

def _softmax(x, axis=-1):
    return jax.nn.softmax(x, axis=axis)

def _gelu(x):
    return jax.nn.gelu(x, approximate=True)

def _silu(x):
    return jax.nn.silu(x)

def _sigmoid(x):
    return jax.nn.sigmoid(x)

def _layernorm(x, axis=-1, eps=1e-05):
    m = jnp.mean(x, axis=axis, keepdims=True)
    v = jnp.var(x, axis=axis, keepdims=True)
    return (x - m) / jnp.sqrt(v + eps)

def _scatter_add(tgt, idx, src, axis=0):
    return tgt.at[idx].add(src)

def _segment_sum(src, seg, n):
    return jax.ops.segment_sum(src, seg, n)
kernel_name = 'mk_seq_preln_d2_jaxref_r8_af05df'

def setup_inputs(seed: int=0):
    np.random.seed(seed)
    _w = jnp.asarray

    def _L0_attn_setup():
        import jax, jax.numpy as jnp
        import numpy as np
        B, S, HID = (2, 256, 256)
        NH, NKV, HD = (16, 4, 128)
        KV_DIM = NKV * HD
        key = jax.random.key(seed)
        ks = jax.random.split(key, 7)
        sc = 0.02
        return {'hidden_states': jax.random.normal(ks[0], (B, S, HID), dtype=jnp.float32), 'Wq': jax.random.normal(ks[1], (NH * HD, HID), dtype=jnp.float32) * sc, 'Wk': jax.random.normal(ks[2], (KV_DIM, HID), dtype=jnp.float32) * sc, 'Wv': jax.random.normal(ks[3], (KV_DIM, HID), dtype=jnp.float32) * sc, 'Wo': jax.random.normal(ks[4], (HID, NH * HD), dtype=jnp.float32) * sc, 'bo': jnp.zeros((HID,), dtype=jnp.float32)}
    _L0_attn_in = _L0_attn_setup()

    def _L0_ffn_setup():
        import jax, jax.numpy as jnp
        import numpy as np
        import math
        GOLDEN_CENTER = 1.0 / math.e
        GOLDEN_LOWER = 0.5 - math.log(4.0 / 3.0)
        GOLDEN_UPPER = 0.5
        B, T, D = (4, 128, 256)
        E = 8
        F = 1024 // (E // 2)
        R = 64
        NL = 2

        def _router_weights(x, Wr, temperature):
            logits = jnp.einsum('btd,de->bte', x, Wr)
            inhibition = jax.nn.sigmoid(logits / temperature)
            in_zone = (inhibition >= GOLDEN_LOWER) & (inhibition <= GOLDEN_UPPER)
            distance = jnp.abs(inhibition - GOLDEN_CENTER)
            w = jnp.exp(-distance / 0.1) * in_zone.astype(x.dtype)
            wsum = w.sum(axis=-1, keepdims=True)
            no_expert = wsum < 1e-08
            fb = jnp.exp(-distance / 0.3)
            _, top2 = jax.lax.top_k(fb, 2)
            fb_mask = jax.nn.one_hot(top2, E, dtype=x.dtype).sum(axis=-2)
            fb_w = fb * fb_mask
            fb_w = fb_w / jnp.clip(fb_w.sum(axis=-1, keepdims=True), 1e-08)
            w = jnp.where(no_expert, fb_w, w)
            return w / jnp.clip(w.sum(axis=-1, keepdims=True), 1e-08)
        key = jax.random.key(seed)
        ks = jax.random.split(key, 13)
        s = 0.02
        x = jax.random.normal(ks[0], (B, T, D), dtype=jnp.float32)
        Wg = jax.random.normal(ks[1], (E, D, F), dtype=jnp.float32) * s
        Wu = jax.random.normal(ks[2], (E, D, F), dtype=jnp.float32) * s
        Wd = jax.random.normal(ks[3], (E, F, D), dtype=jnp.float32) * s
        Ga = jax.random.normal(ks[4], (NL, D, R), dtype=jnp.float32) * s
        Gb = jax.random.normal(ks[5], (NL, R, F), dtype=jnp.float32) * s
        Ua = jax.random.normal(ks[6], (NL, D, R), dtype=jnp.float32) * s
        Ub = jax.random.normal(ks[7], (NL, R, F), dtype=jnp.float32) * s
        Da = jax.random.normal(ks[8], (NL, F, R), dtype=jnp.float32) * s
        Db = jax.random.normal(ks[9], (NL, R, D), dtype=jnp.float32) * s
        Wr = jax.random.normal(ks[10], (D, E), dtype=jnp.float32) * s
        temperature = jnp.ones((1,), dtype=jnp.float32)
        return {'x': x, 'Wg': Wg, 'Wu': Wu, 'Wd': Wd, 'Ga': Ga, 'Gb': Gb, 'Ua': Ua, 'Ub': Ub, 'Da': Da, 'Db': Db, 'Wr': Wr, 'temperature': temperature}
    _L0_ffn_in = _L0_ffn_setup()

    def _L1_attn_setup():
        import jax, jax.numpy as jnp
        import numpy as np
        B, T, HIDDEN = (2, 512, 256)
        NUM_HEADS, HEAD_K, HEAD_V = (6, 32, 64)
        KEY_DIM, VALUE_DIM = (NUM_HEADS * HEAD_K, NUM_HEADS * HEAD_V)
        CONV_K, CHUNK, EPS = (4, 64, 1e-05)

        def short_conv(x, w):
            K = w.shape[1]
            xp = jnp.pad(x, ((0, 0), (K - 1, 0), (0, 0)))
            y = sum((xp[:, i:i + x.shape[1], :] * w[:, i] for i in range(K)))
            return jax.nn.silu(y)

        def l2norm(x):
            return x * jax.lax.rsqrt(jnp.sum(x * x, -1, keepdims=True))

        def _step(S, xs):
            qt, kt, vt, gt, bt = xs
            S = S * jnp.exp(gt)[..., None, None]
            pred = jnp.einsum('bhk,bhkv->bhv', kt, S)
            delta = (vt - pred) * bt[..., None]
            S = S + jnp.einsum('bhk,bhv->bhkv', kt, delta)
            return (S, jnp.einsum('bhk,bhkv->bhv', qt, S))

        def _chunk(S, xs):
            return jax.lax.scan(_step, S, xs)
        _chunk_ckpt = jax.checkpoint(_chunk)

        def gated_delta_rule(q, k, v, g, beta):
            b, t, h, dk = q.shape
            dv = v.shape[-1]
            q = l2norm(q) * dk ** (-0.5)
            k = l2norm(k)
            nc = t // CHUNK

            def to_scan(x):
                x = x.reshape(b, nc, CHUNK, *x.shape[2:])
                return jnp.moveaxis(x, 0, 2)
            xs = tuple(map(to_scan, (q, k, v, g, beta)))
            S0 = jnp.zeros((b, h, dk, dv), q.dtype)
            _, o = jax.lax.scan(_chunk_ckpt, S0, xs)
            return jnp.moveaxis(o, 2, 0).reshape(b, t, h, dv)
        key = jax.random.key(seed)
        ks = jax.random.split(key, 14)

        def lin(k, fi, fo):
            return jax.random.normal(k, (fi, fo), jnp.float32) / np.sqrt(fi)
        A = jax.random.uniform(ks[11], (NUM_HEADS,), minval=0.001, maxval=16.0)
        dt = jnp.exp(jax.random.uniform(ks[12], (NUM_HEADS,)) * (np.log(0.1) - np.log(0.001)) + np.log(0.001))
        dt = jnp.clip(dt, 0.0001)
        return {'hidden_states': jax.random.normal(ks[0], (B, T, HIDDEN), jnp.float32), 'Wq': lin(ks[1], HIDDEN, KEY_DIM), 'Wk': lin(ks[2], HIDDEN, KEY_DIM), 'Wv': lin(ks[3], HIDDEN, VALUE_DIM), 'Wa': lin(ks[4], HIDDEN, NUM_HEADS), 'Wb': lin(ks[5], HIDDEN, NUM_HEADS), 'Wg': lin(ks[6], HIDDEN, VALUE_DIM), 'Wo': lin(ks[7], VALUE_DIM, HIDDEN), 'conv_wq': jax.random.normal(ks[8], (KEY_DIM, CONV_K), jnp.float32) / np.sqrt(CONV_K), 'conv_wk': jax.random.normal(ks[9], (KEY_DIM, CONV_K), jnp.float32) / np.sqrt(CONV_K), 'conv_wv': jax.random.normal(ks[10], (VALUE_DIM, CONV_K), jnp.float32) / np.sqrt(CONV_K), 'A_log': jnp.log(A), 'dt_bias': dt + jnp.log(-jnp.expm1(-dt)), 'norm_weight': jnp.ones((HEAD_V,), jnp.float32)}
    _L1_attn_in = _L1_attn_setup()

    def _L1_ffn_setup():
        import jax, jax.numpy as jnp
        import numpy as np
        D_MODEL = 256
        D_FF = 176
        N_EXPERTS = 6
        TOP_K = 2
        B, S = (8, 512)
        key = jax.random.key(seed)
        ks = jax.random.split(key, 6)
        x = jax.random.normal(ks[0], (B, S, D_MODEL), dtype=jnp.float32)
        W1 = jax.random.normal(ks[1], (N_EXPERTS, D_MODEL, D_FF), dtype=jnp.float32) * 0.02
        b1 = jax.random.normal(ks[2], (N_EXPERTS, D_FF), dtype=jnp.float32) * 0.02
        W2 = jax.random.normal(ks[3], (N_EXPERTS, D_FF, D_MODEL), dtype=jnp.float32) * 0.02
        b2 = jax.random.normal(ks[4], (N_EXPERTS, D_MODEL), dtype=jnp.float32) * 0.02
        gate_W = jax.random.normal(ks[5], (N_EXPERTS, D_MODEL), dtype=jnp.float32) * 0.02
        return {'x': x, 'gate_W': gate_W, 'W1': W1, 'b1': b1, 'W2': W2, 'b2': b2}
    _L1_ffn_in = _L1_ffn_setup()
    _d = {'L0_attn_hidden_states': _L0_attn_in['hidden_states'], 'L0_attn_Wq': _L0_attn_in['Wq'], 'L0_attn_Wk': _L0_attn_in['Wk'], 'L0_attn_Wv': _L0_attn_in['Wv'], 'L0_attn_Wo': _L0_attn_in['Wo'], 'L0_attn_bo': _L0_attn_in['bo'], 'L0_ffn_Wg': _L0_ffn_in['Wg'], 'L0_ffn_Wu': _L0_ffn_in['Wu'], 'L0_ffn_Wd': _L0_ffn_in['Wd'], 'L0_ffn_Ga': _L0_ffn_in['Ga'], 'L0_ffn_Gb': _L0_ffn_in['Gb'], 'L0_ffn_Ua': _L0_ffn_in['Ua'], 'L0_ffn_Ub': _L0_ffn_in['Ub'], 'L0_ffn_Da': _L0_ffn_in['Da'], 'L0_ffn_Db': _L0_ffn_in['Db'], 'L0_ffn_Wr': _L0_ffn_in['Wr'], 'L0_ffn_temperature': _L0_ffn_in['temperature'], 'L1_attn_Wq': _L1_attn_in['Wq'], 'L1_attn_Wk': _L1_attn_in['Wk'], 'L1_attn_Wv': _L1_attn_in['Wv'], 'L1_attn_Wa': _L1_attn_in['Wa'], 'L1_attn_Wb': _L1_attn_in['Wb'], 'L1_attn_Wg': _L1_attn_in['Wg'], 'L1_attn_Wo': _L1_attn_in['Wo'], 'L1_attn_conv_wq': _L1_attn_in['conv_wq'], 'L1_attn_conv_wk': _L1_attn_in['conv_wk'], 'L1_attn_conv_wv': _L1_attn_in['conv_wv'], 'L1_attn_A_log': _L1_attn_in['A_log'], 'L1_attn_dt_bias': _L1_attn_in['dt_bias'], 'L1_attn_norm_weight': _L1_attn_in['norm_weight'], 'L1_ffn_gate_W': _L1_ffn_in['gate_W'], 'L1_ffn_W1': _L1_ffn_in['W1'], 'L1_ffn_b1': _L1_ffn_in['b1'], 'L1_ffn_W2': _L1_ffn_in['W2'], 'L1_ffn_b2': _L1_ffn_in['b2']}
    _x0 = _d['L0_attn_hidden_states']
    _d['L0_attn_hidden_states'] = jax.random.normal(jax.random.fold_in(jax.random.key(seed), 1), (8, 256, 256), dtype=_x0.dtype)
    del _x0
    return _d

def reference(L0_attn_hidden_states, L0_attn_Wq, L0_attn_Wk, L0_attn_Wv, L0_attn_Wo, L0_attn_bo, L0_ffn_Wg, L0_ffn_Wu, L0_ffn_Wd, L0_ffn_Ga, L0_ffn_Gb, L0_ffn_Ua, L0_ffn_Ub, L0_ffn_Da, L0_ffn_Db, L0_ffn_Wr, L0_ffn_temperature, L1_attn_Wq, L1_attn_Wk, L1_attn_Wv, L1_attn_Wa, L1_attn_Wb, L1_attn_Wg, L1_attn_Wo, L1_attn_conv_wq, L1_attn_conv_wk, L1_attn_conv_wv, L1_attn_A_log, L1_attn_dt_bias, L1_attn_norm_weight, L1_ffn_gate_W, L1_ffn_W1, L1_ffn_b1, L1_ffn_W2, L1_ffn_b2):

    def _L0_attn_ref(hidden_states, Wq, Wk, Wv, Wo, bo):
        import jax, jax.numpy as jnp
        import numpy as np
        B, S, HID = (2, 256, 256)
        NH, NKV, HD = (16, 4, 128)
        KV_DIM = NKV * HD
        b, s, _ = hidden_states.shape
        q = (hidden_states @ Wq.T).reshape(b, s, NH, HD).transpose(0, 2, 1, 3)
        k = (hidden_states @ Wk.T).reshape(b, s, NKV, HD).transpose(0, 2, 1, 3)
        v = (hidden_states @ Wv.T).reshape(b, s, NKV, HD).transpose(0, 2, 1, 3)
        g = NH // NKV
        k_rep = jnp.repeat(k, g, axis=1)
        v_rep = jnp.repeat(v, g, axis=1)
        qf = q.astype(jnp.float32)
        kf = k_rep.astype(jnp.float32)
        scores = jnp.einsum('bhqd,bhkd->bhqk', qf, kf)
        causal = jnp.tril(jnp.ones((s, s), dtype=bool))[None, None]
        neg = jnp.finfo(scores.dtype).min
        scores = jnp.where(causal, scores, neg)
        attn = jax.nn.softmax(scores, axis=-1).astype(v.dtype)
        out = jnp.einsum('bhqk,bhkd->bhqd', attn, v_rep)
        out = out.transpose(0, 2, 1, 3).reshape(b, s, NH * HD)
        return out @ Wo.T + bo

    def _L0_ffn_ref(x, Wg, Wu, Wd, Ga, Gb, Ua, Ub, Da, Db, Wr, temperature):
        import jax, jax.numpy as jnp
        import numpy as np
        import math
        GOLDEN_CENTER = 1.0 / math.e
        GOLDEN_LOWER = 0.5 - math.log(4.0 / 3.0)
        GOLDEN_UPPER = 0.5
        B, T, D = (4, 128, 256)
        E = 8
        F = 1024 // (E // 2)
        R = 64
        NL = 2

        def _router_weights(x, Wr, temperature):
            logits = jnp.einsum('btd,de->bte', x, Wr)
            inhibition = jax.nn.sigmoid(logits / temperature)
            in_zone = (inhibition >= GOLDEN_LOWER) & (inhibition <= GOLDEN_UPPER)
            distance = jnp.abs(inhibition - GOLDEN_CENTER)
            w = jnp.exp(-distance / 0.1) * in_zone.astype(x.dtype)
            wsum = w.sum(axis=-1, keepdims=True)
            no_expert = wsum < 1e-08
            fb = jnp.exp(-distance / 0.3)
            _, top2 = jax.lax.top_k(fb, 2)
            fb_mask = jax.nn.one_hot(top2, E, dtype=x.dtype).sum(axis=-2)
            fb_w = fb * fb_mask
            fb_w = fb_w / jnp.clip(fb_w.sum(axis=-1, keepdims=True), 1e-08)
            w = jnp.where(no_expert, fb_w, w)
            return w / jnp.clip(w.sum(axis=-1, keepdims=True), 1e-08)
        weights = _router_weights(x, Wr, temperature)
        gate = jnp.einsum('btd,edf->ebtf', x, Wg)
        up = jnp.einsum('btd,edf->ebtf', x, Wu)
        gate = gate.at[:NL].add(jnp.einsum('btd,edr,erf->ebtf', x, Ga, Gb))
        up = up.at[:NL].add(jnp.einsum('btd,edr,erf->ebtf', x, Ua, Ub))
        mid = jax.nn.silu(gate) * up
        out = jnp.einsum('ebtf,efd->ebtd', mid, Wd)
        out = out.at[:NL].add(jnp.einsum('ebtf,efr,erd->ebtd', mid[:NL], Da, Db))
        return jnp.einsum('bte,ebtd->btd', weights, out)

    def _L1_attn_ref(hidden_states, Wq, Wk, Wv, Wa, Wb, Wg, Wo, conv_wq, conv_wk, conv_wv, A_log, dt_bias, norm_weight):
        import jax, jax.numpy as jnp
        import numpy as np
        B, T, HIDDEN = (2, 512, 256)
        NUM_HEADS, HEAD_K, HEAD_V = (6, 32, 64)
        KEY_DIM, VALUE_DIM = (NUM_HEADS * HEAD_K, NUM_HEADS * HEAD_V)
        CONV_K, CHUNK, EPS = (4, 64, 1e-05)

        def short_conv(x, w):
            K = w.shape[1]
            xp = jnp.pad(x, ((0, 0), (K - 1, 0), (0, 0)))
            y = sum((xp[:, i:i + x.shape[1], :] * w[:, i] for i in range(K)))
            return jax.nn.silu(y)

        def l2norm(x):
            return x * jax.lax.rsqrt(jnp.sum(x * x, -1, keepdims=True))

        def _step(S, xs):
            qt, kt, vt, gt, bt = xs
            S = S * jnp.exp(gt)[..., None, None]
            pred = jnp.einsum('bhk,bhkv->bhv', kt, S)
            delta = (vt - pred) * bt[..., None]
            S = S + jnp.einsum('bhk,bhv->bhkv', kt, delta)
            return (S, jnp.einsum('bhk,bhkv->bhv', qt, S))

        def _chunk(S, xs):
            return jax.lax.scan(_step, S, xs)
        _chunk_ckpt = jax.checkpoint(_chunk)

        def gated_delta_rule(q, k, v, g, beta):
            b, t, h, dk = q.shape
            dv = v.shape[-1]
            q = l2norm(q) * dk ** (-0.5)
            k = l2norm(k)
            nc = t // CHUNK

            def to_scan(x):
                x = x.reshape(b, nc, CHUNK, *x.shape[2:])
                return jnp.moveaxis(x, 0, 2)
            xs = tuple(map(to_scan, (q, k, v, g, beta)))
            S0 = jnp.zeros((b, h, dk, dv), q.dtype)
            _, o = jax.lax.scan(_chunk_ckpt, S0, xs)
            return jnp.moveaxis(o, 2, 0).reshape(b, t, h, dv)
        b, t, _ = hidden_states.shape
        q = short_conv(hidden_states @ Wq, conv_wq).reshape(b, t, NUM_HEADS, HEAD_K)
        k = short_conv(hidden_states @ Wk, conv_wk).reshape(b, t, NUM_HEADS, HEAD_K)
        v = short_conv(hidden_states @ Wv, conv_wv).reshape(b, t, NUM_HEADS, HEAD_V)
        beta = jax.nn.sigmoid(hidden_states @ Wb)
        g = -jnp.exp(A_log) * jax.nn.softplus(hidden_states @ Wa + dt_bias)
        o = gated_delta_rule(q, k, v, g, beta)
        gate = (hidden_states @ Wg).reshape(b, t, NUM_HEADS, HEAD_V)
        o = o * jax.lax.rsqrt(jnp.mean(o * o, -1, keepdims=True) + EPS) * norm_weight
        o = o * jax.nn.silu(gate)
        return o.reshape(b, t, VALUE_DIM) @ Wo

    def _L1_ffn_ref(x, gate_W, W1, b1, W2, b2):
        import jax, jax.numpy as jnp
        import numpy as np
        D_MODEL = 256
        D_FF = 176
        N_EXPERTS = 6
        TOP_K = 2
        B, S = (8, 512)
        gate_logits = jnp.einsum('bd,ed->be', x.mean(axis=1), gate_W)
        gate_probs = jax.nn.softmax(gate_logits, axis=-1)
        topk_vals, topk_idx = jax.lax.top_k(gate_probs, TOP_K)
        topk_vals = topk_vals / topk_vals.sum(axis=-1, keepdims=True)
        W1g = W1[topk_idx]
        b1g = b1[topk_idx]
        W2g = W2[topk_idx]
        b2g = b2[topk_idx]
        h = jnp.einsum('bsd,bkdf->bksf', x, W1g) + b1g[:, :, None, :]
        h = jax.nn.gelu(h, approximate=False)
        eo = jnp.einsum('bksf,bkfd->bksd', h, W2g) + b2g[:, :, None, :]
        return jnp.einsum('bk,bksd->bsd', topk_vals, eo)
    x = L0_attn_hidden_states
    x = x + _L0_attn_ref(_layernorm(x, axis=-1), L0_attn_Wq, L0_attn_Wk, L0_attn_Wv, L0_attn_Wo, L0_attn_bo)
    x = x + _L0_ffn_ref(_layernorm(x, axis=-1), L0_ffn_Wg, L0_ffn_Wu, L0_ffn_Wd, L0_ffn_Ga, L0_ffn_Gb, L0_ffn_Ua, L0_ffn_Ub, L0_ffn_Da, L0_ffn_Db, L0_ffn_Wr, L0_ffn_temperature)
    x = x + _L1_attn_ref(_layernorm(x, axis=-1), L1_attn_Wq, L1_attn_Wk, L1_attn_Wv, L1_attn_Wa, L1_attn_Wb, L1_attn_Wg, L1_attn_Wo, L1_attn_conv_wq, L1_attn_conv_wk, L1_attn_conv_wv, L1_attn_A_log, L1_attn_dt_bias, L1_attn_norm_weight)
    x = x + _L1_ffn_ref(_layernorm(x, axis=-1), L1_ffn_gate_W, L1_ffn_W1, L1_ffn_b1, L1_ffn_W2, L1_ffn_b2)
    return x

_drawn_inputs = setup_inputs


def setup_inputs(seed=0):
    import zlib

    import numpy as np

    out = dict(_drawn_inputs(seed))
    spreads = {'L0_attn_bo': (0.0, 0.1), 'L1_attn_norm_weight': (1.0, 0.6)}
    factors = {'L0_ffn_Wg': 4.25,
     'L0_ffn_Wu': 4.161,
     'L0_ffn_Wd': 4.143,
     'L0_ffn_Ga': 8.0,
     'L0_ffn_Gb': 8.0,
     'L0_ffn_Ua': 8.0,
     'L0_ffn_Ub': 8.0,
     'L0_ffn_Da': 8.0,
     'L0_ffn_Db': 8.0,
     'L0_ffn_Wr': 5.229,
     'L1_ffn_b1': 64.0,
     'L1_ffn_b2': 36.704,
     'L1_attn_Wa': 6.11,
     'L1_attn_Wb': 3.319,
     'L1_attn_A_log': 7.665,
     'L1_attn_dt_bias': 2.716,
     'L1_ffn_gate_W': 8.0,
     'L1_ffn_W1': 8.0,
     'L1_ffn_W2': 8.0}
    for name, (base, spread) in spreads.items():
        noise = np.random.default_rng([zlib.crc32(name.encode()), seed]).standard_normal(out[name].shape)
        drawn = base * np.exp(spread * noise) if base else spread * noise
        out[name] = jnp.asarray(drawn.astype(out[name].dtype))
    for name, factor in factors.items():
        out[name] = (out[name] * factor).astype(out[name].dtype)
    return out
```

```python
import math
from contextlib import ExitStack

import concourse.bass as bass
from concourse import mybir
from concourse.alu_op_type import AluOpType as ALU

ACT = mybir.ActivationFunctionType
F32 = mybir.dt.float32
BF16 = mybir.dt.bfloat16
I32 = mybir.dt.int32
AX_X = mybir.AxisListType.X

P = 128
BATCH, SEQ, HID = 8, 256, 256
TOKENS = BATCH * SEQ
TILES = TOKENS // P
DC = HID // P
GROUP_TILES = 4
GROUP = GROUP_TILES * P
GROUPS = TOKENS // GROUP
GROUP_BATCHES = GROUP // SEQ
LN_EPS = 1e-5
NEG = -1e30


class Resident:

    def __init__(self, nc, ctx):
        def sb(name, shape, dt=F32):
            return ctx.enter_context(nc.sbuf_tensor(name, shape, dt))

        self.x = sb("x", [P, TILES, HID])
        self.ident = sb("ident", [P, P])
        self.ident_bf = sb("ident_bf", [P, P], BF16)
        self.causal_bf = sb("causal_bf", [P, P], BF16)
        self.ones_row = sb("ones_row", [1, P])
        self.x_loaded = ctx.enter_context(nc.semaphore("x_loaded"))


def end_of_round(nc, sems):
    nums = [s.num for s in sems]
    assert nums == list(range(nums[0], nums[0] + len(nums)))
    nc.gpsimd.sem_clear(range(nums[0], nums[-1] + 1))
    nc.all_engine_barrier()


def setup(nc, hidden, r):
    with ExitStack() as ctx:
        zeroed = ctx.enter_context(nc.semaphore("zeroed"))
        block = ctx.enter_context(nc.Block())

        @block.sync
        def _(sp):
            sp.dma_start(r.x[:], hidden.rearrange("b (h p) d -> p (b h) d", p=P)).then_inc(r.x_loaded, 16)

        @block.gpsimd
        def _(pool):
            nc.gpsimd.memset(r.ident[:], 0.0)
            nc.gpsimd.memset(r.ident_bf[:], 0.0)
            nc.gpsimd.memset(r.ones_row[:], 1.0)
            nc.gpsimd.memset(r.causal_bf[:], 0.0).then_inc(zeroed, 1)
            pool.wait_ge(zeroed, 1)
            for m in (r.ident, r.ident_bf):
                nc.gpsimd.affine_select(out=m[:], in_=m[:], compare_op=ALU.not_equal, fill=1.0, base=0,
                                        pattern=[[-1, P]], channel_multiplier=1)
            nc.gpsimd.affine_select(out=r.causal_bf[:], in_=r.causal_bf[:], compare_op=ALU.is_ge, fill=NEG,
                                    base=0, pattern=[[-1, P]], channel_multiplier=1)


NH, NKV, HD = 16, 4, 128
REP = NH // NKV
QW = 3 * P


class Norm:

    def __init__(self, nc, sb):
        self.stats = sb("ln_stats", [P, GROUP_TILES, 6])
        self.mv = sb("ln_mv", [P, GROUP_TILES, 2])
        self.veps = sb("ln_veps", [P, GROUP_TILES])
        self.lnv = sb("ln_lnv", [P, GROUP_TILES])
        self.r0 = sb("ln_r0", [P, GROUP_TILES])
        self.t = sb("ln_t", [P, GROUP_TILES])
        self.xn = sb("ln_xn", [P, GROUP_TILES, HID])


def norm_vector(nc, dve, link, n, x_of, var_ready, r0_ready, xn_ready):
    for t in range(GROUP_TILES):
        last = nc.vector.bn_stats(n.stats[:, t, :], x_of(t))
    link(last)
    for t in range(GROUP_TILES):
        last = nc.vector.bn_aggr(n.mv[:, t, :], n.stats[:, t, :])
    link(last)
    nc.vector.tensor_scalar(n.veps[:], n.mv[:, :, 1], LN_EPS, None, ALU.add).then_inc(var_ready, 1)
    dve.wait_ge(r0_ready, 2)
    link(nc.vector.tensor_tensor(n.t[:], n.r0[:], n.r0[:], ALU.mult))
    link(nc.vector.tensor_tensor(n.t[:], n.t[:], n.veps[:], ALU.mult))
    link(nc.vector.tensor_scalar(n.t[:], n.t[:], -0.5, 1.5, ALU.mult, ALU.add))
    link(nc.vector.tensor_tensor(n.t[:], n.t[:], n.r0[:], ALU.mult))
    for t in range(GROUP_TILES):
        nc.vector.tensor_scalar(n.xn[:, t, :], x_of(t), n.mv[:, t, 0:1], n.t[:, t:t + 1],
                                ALU.subtract, ALU.mult).then_inc(xn_ready, 1)


def norm_scalar(nc, act, n, var_ready, r0_ready):
    act.wait_ge(var_ready, 1)
    nc.scalar.activation(n.lnv[:], n.veps[:], ACT.Ln).then_inc(r0_ready, 1)
    act.wait_ge(r0_ready, 1)
    nc.scalar.activation(n.r0[:], n.lnv[:], ACT.Exp, scale=-0.5).then_inc(r0_ready, 1)


def norm_tensor(nc, pe, n, ident, banks, xn_ready, xnT_ready):
    for t in range(GROUP_TILES):
        pe.wait_ge(xn_ready, t + 1)
        for c in range(DC):
            mm = nc.tensor.transpose(banks[c][:, t * P:(t + 1) * P], n.xn[:, t, c * P:(c + 1) * P], ident[:])
    mm.then_inc(xnT_ready, 1)


def attention(nc, r, w_q, w_k, w_v, w_o, b_o):
    with ExitStack() as ctx:
        def sb(name, shape, dt=F32):
            return ctx.enter_context(nc.sbuf_tensor("a_" + name, shape, dt))

        def sem(name):
            return ctx.enter_context(nc.semaphore("a_" + name))

        ps = ctx.enter_context(nc.psum_tensor("a_ps", [P, 8, 512], F32))
        PROJ, SC, PTB, OTB = (0, 1), (2, 3), (4, 5), (6, 7)

        n = Norm(nc, sb)
        wq = sb("wq", [P, DC, NH * HD])
        wk = sb("wk", [P, DC, NKV * HD])
        wv = sb("wv", [P, DC, NKV * HD])
        wo = sb("wo", [P, NH, HID])
        bo = sb("bo", [P, 1, HID])
        xnT = sb("xnT", [P, DC, GROUP])
        kT = sb("kT", [P, NKV, GROUP])
        v = sb("v", [P, GROUP_TILES, NKV * HD])
        qT = sb("qT", [P, 2, GROUP])
        negmax = sb("negmax", [P, 2, GROUP_TILES])
        rowsum = sb("rowsum", [P, 2, GROUP_TILES])
        inv = sb("inv", [P, 2, GROUP_TILES])
        probs = sb("probs", [P, 2, GROUP_BATCHES, QW])
        pT = sb("pT", [P, 2, GROUP_BATCHES, QW])
        oT = sb("oT", [P, NH, GROUP])

        w_loaded = [sem(f"w_loaded{i}") for i in range(5)]
        var_ready, r0_ready, xn_ready, xnT_ready, xnT_copied = [
            sem(s) for s in ("var_ready", "r0_ready", "xn_ready", "xnT_ready", "xnT_copied")]
        proj_ready, proj_taken = sem("proj_ready"), sem("proj_taken")
        scores_ready, max_ready, exp_ready, probs_ready = [
            sem(s) for s in ("scores_ready", "max_ready", "exp_ready", "probs_ready")]
        pT_ready, pT_copied, oT_ready, oT_copied = [
            sem(s) for s in ("pT_ready", "pT_copied", "oT_ready", "oT_copied")]
        bias_added, dve_done, out_added = sem("bias_added"), sem("dve_done"), sem("out_added")
        round_sems = [var_ready, r0_ready, xn_ready, xnT_ready, xnT_copied, proj_ready, proj_taken,
                      scores_ready, max_ready, exp_ready, probs_ready, pT_ready, pT_copied, oT_ready,
                      oT_copied, bias_added, dve_done, out_added]

        with nc.Block() as block:
            @block.sync
            def _(sp):
                sp.dma_start(wk[:], w_k.rearrange("(c p) n -> p c n", p=P)).then_inc(w_loaded[0], 16)
                sp.dma_start(wv[:], w_v.rearrange("(c p) n -> p c n", p=P)).then_inc(w_loaded[1], 16)
                sp.dma_start(wq[:], w_q.rearrange("(c p) n -> p c n", p=P)).then_inc(w_loaded[2], 16)
                sp.dma_start(bo[:, 0, :], b_o.rearrange("(a n) -> a n", a=1).to_broadcast([P, HID])
                             ).then_inc(w_loaded[4], 16)
                sp.dma_start(wo[:], w_o.rearrange("(h p) n -> p h n", p=P)).then_inc(w_loaded[3], 16)

        KV_JOBS = NKV + GROUP_TILES

        def chunk(b, half):
            t = 2 * b + half
            return slice(t * P, (t + 1) * P)

        with nc.Fori(0, GROUPS) as i:
            with nc.Block() as block:
                @block.vector
                def _(dve):
                    done = [0]

                    def link(ins):
                        done[0] += 1
                        ins.then_inc(dve_done, 1)
                        dve.wait_ge(dve_done, done[0])

                    x_tile = lambda t: r.x[:, bass.ds(i * GROUP_TILES + t, 1), :].rearrange("p a d -> p (a d)")
                    dve.wait_ge(r.x_loaded, 16)
                    norm_vector(nc, dve, link, n, x_tile, var_ready, r0_ready, xn_ready)

                    def maxima(h):
                        for b in range(GROUP_BATCHES):
                            dve.wait_ge(scores_ready, 2 * h + b + 1)
                            nc.vector.tensor_reduce(negmax[:, h % 2, 2 * b:2 * b + 1], ps[:, SC[b], 0:P],
                                                    AX_X, ALU.max, negate=True)
                            nc.vector.tensor_reduce(negmax[:, h % 2, 2 * b + 1:2 * b + 2], ps[:, SC[b], P:QW],
                                                    AX_X, ALU.max, negate=True).then_inc(max_ready, 1)

                    def copy_pT(h):
                        for b in range(GROUP_BATCHES):
                            dve.wait_ge(pT_ready, 2 * h + b + 1)
                            if h >= 2:
                                dve.wait_ge(oT_ready, h - 1)
                            nc.vector.tensor_copy(pT[:, h % 2, b, :], ps[:, PTB[b], 0:QW]).then_inc(pT_copied, 1)

                    def normalise(h):
                        dve.wait_ge(exp_ready, 2 * h + 2)
                        link(nc.vector.reciprocal(inv[:, h % 2, :], rowsum[:, h % 2, :]))
                        for b in range(GROUP_BATCHES):
                            nc.vector.tensor_scalar(probs[:, h % 2, b, 0:P], probs[:, h % 2, b, 0:P],
                                                    inv[:, h % 2, 2 * b:2 * b + 1], None, ALU.mult)
                            nc.vector.tensor_scalar(probs[:, h % 2, b, P:QW], probs[:, h % 2, b, P:QW],
                                                    inv[:, h % 2, 2 * b + 1:2 * b + 2], None,
                                                    ALU.mult).then_inc(probs_ready, 1)

                    for h in range(NH):
                        maxima(h)
                        if h >= 1:
                            copy_pT(h - 1)
                        normalise(h)
                    copy_pT(NH - 1)
                    dve.wait_ge(bias_added, 1)
                    for t in range(GROUP_TILES):
                        job = KV_JOBS + NH + t
                        dve.wait_ge(proj_ready, job + 1)
                        nc.vector.tensor_tensor(x_tile(t), x_tile(t), ps[:, PROJ[job % 2], 0:HID],
                                                ALU.add).then_inc(proj_taken, 1)

                @block.gpsimd
                def _(pool):
                    pool.wait_ge(xn_ready, GROUP_TILES)
                    pool.wait_ge(w_loaded[4], 16)
                    xg = r.x[:, bass.ds(i * GROUP_TILES, GROUP_TILES), :]
                    nc.gpsimd.tensor_tensor(xg, xg, bo[:].to_broadcast([P, GROUP_TILES, HID]),
                                            ALU.add).then_inc(bias_added, 1)

                @block.scalar
                def _(act):
                    norm_scalar(nc, act, n, var_ready, r0_ready)
                    act.wait_ge(xnT_ready, 1)
                    for c in range(DC):
                        nc.scalar.copy(xnT[:, c, :], ps[:, OTB[c], :]).then_inc(xnT_copied, 1)

                    def take(job, dst):
                        act.wait_ge(proj_ready, job + 1)
                        nc.scalar.copy(dst, ps[:, PROJ[job % 2], :]).then_inc(proj_taken, 1)

                    for g in range(NKV):
                        take(g, kT[:, g, :])
                    for t in range(GROUP_TILES):
                        take(NKV + t, v[:, t, :])
                    take(KV_JOBS, qT[:, 0, :])

                    def exps(h):
                        if h >= 2:
                            act.wait_ge(pT_ready, 2 * (h - 1))
                        for b in range(GROUP_BATCHES):
                            act.wait_ge(max_ready, 2 * h + b + 1)
                            nc.scalar.activation(probs[:, h % 2, b, 0:P], ps[:, SC[b], 0:P], ACT.Exp,
                                                 bias=negmax[:, h % 2, 2 * b:2 * b + 1],
                                                 accum_out=rowsum[:, h % 2, 2 * b:2 * b + 1])
                            nc.scalar.activation(probs[:, h % 2, b, P:QW], ps[:, SC[b], P:QW], ACT.Exp,
                                                 bias=negmax[:, h % 2, 2 * b + 1:2 * b + 2],
                                                 accum_out=rowsum[:, h % 2, 2 * b + 1:2 * b + 2]
                                                 ).then_inc(exp_ready, 1)

                    def copy_oT(h):
                        act.wait_ge(oT_ready, h + 1)
                        nc.scalar.copy(oT[:, h, :], ps[:, OTB[h % 2], :]).then_inc(oT_copied, 1)

                    for h in range(NH):
                        exps(h)
                        if h + 1 < NH:
                            take(KV_JOBS + h + 1, qT[:, (h + 1) % 2, :])
                        if h >= 1:
                            copy_oT(h - 1)
                    copy_oT(NH - 1)

                @block.tensor
                def _(pe):
                    norm_tensor(nc, pe, n, r.ident, [ps[:, OTB[0], :], ps[:, OTB[1], :]], xn_ready, xnT_ready)

                    def bank_free(job):
                        if job >= 2:
                            pe.wait_ge(proj_taken, job - 1)

                    def project(job, w, cols):
                        bank_free(job)
                        for c in range(DC):
                            mm = nc.tensor.matmul(ps[:, PROJ[job % 2], :], w[:, c, cols], xnT[:, c, :],
                                                  start=(c == 0), stop=(c == DC - 1))
                        mm.then_inc(proj_ready, 1)

                    pe.wait_ge(xnT_copied, DC)
                    pe.wait_ge(w_loaded[0], 16)
                    for g in range(NKV):
                        project(g, wk, slice(g * HD, (g + 1) * HD))
                    pe.wait_ge(w_loaded[1], 16)
                    for t in range(GROUP_TILES):
                        bank_free(NKV + t)
                        for c in range(DC):
                            mm = nc.tensor.matmul(ps[:, PROJ[(NKV + t) % 2], :], xnT[:, c, t * P:(t + 1) * P],
                                                  wv[:, c, :], start=(c == 0), stop=(c == DC - 1))
                        mm.then_inc(proj_ready, 1)
                    pe.wait_ge(w_loaded[2], 16)

                    def queries(h):
                        project(KV_JOBS + h, wq, slice(h * HD, (h + 1) * HD))

                    def scores(h):
                        pe.wait_ge(proj_taken, KV_JOBS + h + 1)
                        for b in range(GROUP_BATCHES):
                            if h >= 1:
                                pe.wait_ge(exp_ready, 2 * (h - 1) + b + 1)
                            q, k = qT[:, h % 2, :], kT[:, h // REP, :]
                            nc.tensor.matmul(ps[:, SC[b], 0:P], q[:, chunk(b, 0)], k[:, chunk(b, 0)],
                                             start=True, stop=False)
                            nc.tensor.matmul(ps[:, SC[b], 0:P], r.ident_bf[:], r.causal_bf[:],
                                             start=False, stop=True)
                            nc.tensor.matmul(ps[:, SC[b], P:QW], q[:, chunk(b, 1)],
                                             k[:, 2 * b * P:(2 * b + 2) * P], start=True, stop=False)
                            nc.tensor.matmul(ps[:, SC[b], 2 * P:QW], r.ident_bf[:], r.causal_bf[:],
                                             start=False, stop=True).then_inc(scores_ready, 1)

                    def turn(h):
                        for b in range(GROUP_BATCHES):
                            pe.wait_ge(probs_ready, 2 * h + b + 1)
                            if h >= 1:
                                pe.wait_ge(pT_copied, 2 * (h - 1) + b + 1)
                            for s in range(3):
                                mm = nc.tensor.transpose(ps[:, PTB[b], s * P:(s + 1) * P],
                                                         probs[:, h % 2, b, s * P:(s + 1) * P], r.ident[:])
                            mm.then_inc(pT_ready, 1)

                    def values(h):
                        if h >= 2:
                            pe.wait_ge(oT_copied, h - 1)
                        g = slice((h // REP) * HD, (h // REP + 1) * HD)
                        for b in range(GROUP_BATCHES):
                            pe.wait_ge(pT_copied, 2 * h + b + 1)
                            out = ps[:, OTB[h % 2], 2 * b * P:(2 * b + 2) * P]
                            nc.tensor.matmul(out, v[:, 2 * b, g], pT[:, h % 2, b, 0:2 * P], start=True, stop=False)
                            mm = nc.tensor.matmul(out[:, P:2 * P], v[:, 2 * b + 1, g], pT[:, h % 2, b, 2 * P:QW],
                                                  start=False, stop=True)
                        mm.then_inc(oT_ready, 1)

                    queries(0)
                    scores(0)
                    queries(1)
                    for h in range(1, NH):
                        scores(h)
                        turn(h - 1)
                        if h + 1 < NH:
                            queries(h + 1)
                        values(h - 1)
                    turn(NH - 1)
                    values(NH - 1)
                    pe.wait_ge(oT_copied, NH)
                    pe.wait_ge(w_loaded[3], 16)
                    for t in range(GROUP_TILES):
                        job = KV_JOBS + NH + t
                        bank_free(job)
                        for h in range(NH):
                            mm = nc.tensor.matmul(ps[:, PROJ[job % 2], 0:HID], oT[:, h, t * P:(t + 1) * P],
                                                  wo[:, h, :], start=(h == 0), stop=(h == NH - 1))
                        mm.then_inc(proj_ready, 1)
            end_of_round(nc, round_sems)


NE, FE, RANK, NLORA = 8, 256, 64, 2
FC = FE // P
GOLDEN_CENTER = 1.0 / math.e
GOLDEN_LOWER = 0.5 - math.log(4.0 / 3.0)
ZONE_LOW = math.log(GOLDEN_LOWER / (1.0 - GOLDEN_LOWER))
ZONE_HIGH = 1e-7
F32R = mybir.dt.float32r


def experts(nc, r, Wg, Wu, Wd, Ga, Gb, Ua, Ub, Da, Db, Wr, temperature):
    with ExitStack() as ctx:
        def sb(name, shape, dt=F32):
            return ctx.enter_context(nc.sbuf_tensor("b_" + name, shape, dt))

        def sem(name):
            return ctx.enter_context(nc.semaphore("b_" + name))

        ps = ctx.enter_context(nc.psum_tensor("b_ps", [P, 8, 512], F32))
        GATE, UP, DOWN = (0, 1), (2, 3), (4, 5, 6, 7)

        n = Norm(nc, sb)
        raw = sb("raw", [P, 2, NE, DC, FE])
        high = sb("high", [P, 2, NE, DC, FE], F32R)
        low = sb("low", [P, 2, NE, DC, FE], F32R)
        wd = sb("wd", [P, NE, FC, HID])
        lora_a = sb("lora_a", [RANK, 3, NLORA, FE])
        lora_b = sb("lora_b", [RANK, 3, NLORA, FE])
        wr = sb("wr", [P, DC, NE])
        temp = sb("temp", [P, 1])
        inv_temp = sb("inv_temp", [P, 1])
        rank_of = sb("rank_of", [P, NE])
        xnT = sb("xnT", [P, DC, GROUP])
        xnT_high = sb("xnT_high", [P, DC, GROUP], F32R)
        xnT_low = sb("xnT_low", [P, DC, GROUP], F32R)
        silu = sb("silu", [P, FC, GROUP])
        mid = sb("mid", [P, 2, FC, GROUP])
        TE = [P, GROUP_TILES, NE]
        z, zone, ez, dist, zw, fb = [sb(s, TE) for s in ("z", "zone", "ez", "dist", "zw", "fb")]
        eq, key, first, second, rest, w = [sb(s, TE) for s in ("eq", "key", "first", "second", "rest", "w")]
        top, best, total, none = [sb(s, [P, GROUP_TILES, 1]) for s in ("top", "best", "total", "none")]

        loaded = [sem(f"loaded{i}") for i in range(5)]
        lora_ready, lora_taken, split_done, setup_done = [
            sem(s) for s in ("lora_ready", "lora_taken", "split_done", "setup_done")]
        var_ready, r0_ready, xn_ready, xnT_ready, xnT_copied = [
            sem(s) for s in ("var_ready", "r0_ready", "xn_ready", "xnT_ready", "xnT_copied")]
        low_ready, logits_ready, z_ready, ez_ready, dist_ready, exps_ready = [
            sem(s) for s in ("low_ready", "logits_ready", "z_ready", "ez_ready", "dist_ready", "exps_ready")]
        gate_ready, up_ready, silu_ready, mid_ready, down_ready, added, dve_done = [
            sem(s) for s in ("gate_ready", "up_ready", "silu_ready", "mid_ready", "down_ready", "added", "dve_done")]
        round_sems = [var_ready, r0_ready, xn_ready, xnT_ready, xnT_copied, low_ready, logits_ready, z_ready,
                      ez_ready, dist_ready, exps_ready, gate_ready, up_ready, silu_ready, mid_ready, down_ready,
                      added, dve_done]

        with nc.Block() as block:
            @block.sync
            def _(sp):
                for k, (a, b) in enumerate(((Ga, Gb), (Ua, Ub), (Da, Db))):
                    sp.dma_start(lora_a[:, k], a.rearrange("l r d -> r l d")).then_inc(loaded[0], 16)
                    sp.dma_start(lora_b[:, k], b.rearrange("l r f -> r l f")).then_inc(loaded[0], 16)
                sp.dma_start(temp[:], temperature.rearrange("(a n) -> a n", a=1).to_broadcast([P, 1])
                             ).then_inc(loaded[0], 16)
                sp.dma_start(wr[:], Wr.rearrange("(c p) e -> p c e", p=P)).then_inc(loaded[0], 16)
                for k, src in enumerate((Wg, Wu)):
                    sp.dma_start(raw[:, k], src.rearrange("e (c p) f -> p e c f", p=P)).then_inc(loaded[1 + k], 16)
                sp.dma_start(wd[:], Wd.rearrange("e (c p) f -> p e c f", p=P)).then_inc(loaded[3], 16)

            @block.gpsimd
            def _(pool):
                nc.gpsimd.iota(rank_of[:], pattern=[[-1, NE]], base=NE, channel_multiplier=0,
                               allow_small_or_imprecise_dtypes=True).then_inc(setup_done, 1)

            @block.tensor
            def _(pe):
                pe.wait_ge(loaded[0], 16 * 8)
                for k in range(3):
                    for e in range(NLORA):
                        job = k * NLORA + e
                        for c in range(DC):
                            mm = nc.tensor.matmul(ps[:, job, c * FE:(c + 1) * FE],
                                                  lora_a[:, k, e, c * P:(c + 1) * P], lora_b[:, k, e, :],
                                                  start=True, stop=True)
                        mm.then_inc(lora_ready, 1)

            @block.vector
            def _(dve):
                dve.wait_ge(loaded[0], 16 * 8)
                nc.vector.reciprocal(inv_temp[:], temp[:]).then_inc(setup_done, 1)
                for k in range(3):
                    dve.wait_ge(loaded[1 + k], 16)
                    for e in range(NLORA):
                        job = k * NLORA + e
                        dve.wait_ge(lora_ready, job + 1)
                        dst = (raw[:, k, e] if k < 2 else wd[:, e]).rearrange("p c f -> p (c f)")
                        nc.vector.tensor_tensor(dst, dst, ps[:, job, :], ALU.add).then_inc(lora_taken, 1)
                    if k < 2:
                        for e in range(NE):
                            dve.wait_ge(split_done, k * NE + e + 1)
                            nc.vector.tensor_tensor(low[:, k, e], raw[:, k, e], high[:, k, e].bitcast(F32),
                                                    ALU.subtract)

            @block.scalar
            def _(act):
                for k in range(2):
                    act.wait_ge(loaded[1 + k], 16)
                    act.wait_ge(lora_taken, NLORA * (k + 1))
                    for e in range(NE):
                        nc.scalar.copy(high[:, k, e], raw[:, k, e]).then_inc(split_done, 1)

        with nc.Fori(0, GROUPS) as i:
            with nc.Block() as block:
                @block.vector
                def _(dve):
                    done = [0]

                    def link(ins):
                        done[0] += 1
                        ins.then_inc(dve_done, 1)
                        dve.wait_ge(dve_done, done[0])

                    x_tile = lambda t: r.x[:, bass.ds(i * GROUP_TILES + t, 1), :].rearrange("p a d -> p (a d)")
                    norm_vector(nc, dve, link, n, x_tile, var_ready, r0_ready, xn_ready)
                    for c in range(DC):
                        dve.wait_ge(xnT_copied, 2 * (c + 1))
                        nc.vector.tensor_tensor(xnT_low[:, c, :], ps[:, DOWN[c], :],
                                                xnT_high[:, c, :].bitcast(F32), ALU.subtract).then_inc(low_ready, 1)

                    def mids(e):
                        for m in range(FC):
                            dve.wait_ge(silu_ready, FC * e + m + 1)
                            dve.wait_ge(up_ready, FC * e + m + 1)
                            if e >= 2:
                                dve.wait_ge(down_ready, GROUP_TILES * (e - 1))
                            nc.vector.tensor_tensor(mid[:, e % 2, m, :], silu[:, m, :], ps[:, UP[m], :],
                                                    ALU.mult).then_inc(mid_ready, 1)

                    def add(e):
                        for t in range(GROUP_TILES):
                            dve.wait_ge(down_ready, GROUP_TILES * e + t + 1)
                            if e >= 1:
                                dve.wait_ge(added, GROUP_TILES * (e - 1) + t + 1)
                            nc.vector.scalar_tensor_tensor(x_tile(t), ps[:, DOWN[t], 0:HID], w[:, t, e:e + 1],
                                                           x_tile(t), ALU.mult, ALU.add).then_inc(added, 1)

                    def over_experts(a):
                        return a[:].to_broadcast(TE)

                    def router():
                        dve.wait_ge(logits_ready, 1)
                        link(nc.vector.tensor_scalar(z[:].rearrange("p t e -> p (t e)"),
                                                     ps[:, DOWN[2], 0:GROUP_TILES * NE], inv_temp[:, 0:1], None,
                                                     ALU.mult))
                        nc.vector.tensor_scalar(zone[:], z[:], ZONE_LOW, None, ALU.is_ge).then_inc(z_ready, 1)
                        link(nc.vector.tensor_scalar(eq[:], z[:], ZONE_HIGH, None, ALU.is_le))
                        link(nc.vector.tensor_tensor(zone[:], zone[:], eq[:], ALU.mult))
                        dve.wait_ge(ez_ready, 1)
                        link(nc.vector.tensor_scalar(ez[:], ez[:], 1.0, None, ALU.add))
                        link(nc.vector.reciprocal(ez[:], ez[:]))
                        link(nc.vector.tensor_scalar(ez[:], ez[:], -GOLDEN_CENTER, None, ALU.add))
                        nc.vector.scalar_tensor_tensor(dist[:], ez[:], -1.0, ez[:], ALU.mult, ALU.max).then_inc(dist_ready, 1)
                        dve.wait_ge(exps_ready, 2)
                        link(nc.vector.tensor_tensor(zw[:], zw[:], zone[:], ALU.mult))
                        link(nc.vector.reduce_sum(total[:], zw[:], AX_X))
                        link(nc.vector.tensor_scalar(none[:], total[:], 1e-8, None, ALU.is_lt))

                        def pick(values, chosen):
                            link(nc.vector.reduce_max(top[:], values[:], AX_X))
                            link(nc.vector.tensor_tensor(eq[:], values[:], over_experts(top), ALU.is_equal))
                            link(nc.vector.tensor_tensor(
                                key[:], eq[:], rank_of[:].rearrange("p (a e) -> p a e", a=1).to_broadcast(TE),
                                ALU.mult))
                            link(nc.vector.reduce_max(best[:], key[:], AX_X))
                            link(nc.vector.tensor_tensor(chosen[:], key[:], over_experts(best), ALU.is_equal))

                        pick(fb, first)
                        link(nc.vector.scalar_tensor_tensor(rest[:], first[:], -4.0, fb[:], ALU.mult, ALU.add))
                        pick(rest, second)
                        link(nc.vector.tensor_tensor(first[:], first[:], second[:], ALU.add))
                        link(nc.vector.tensor_tensor(fb[:], fb[:], first[:], ALU.mult))

                        def normalised(a):
                            link(nc.vector.reduce_sum(total[:], a[:], AX_X))
                            link(nc.vector.tensor_scalar(total[:], total[:], 1e-8, None, ALU.max))
                            link(nc.vector.reciprocal(best[:], total[:]))
                            link(nc.vector.tensor_tensor(a[:], a[:], over_experts(best), ALU.mult))

                        normalised(fb)
                        link(nc.vector.tensor_tensor(fb[:], fb[:], zw[:], ALU.subtract))
                        link(nc.vector.tensor_tensor(fb[:], fb[:], over_experts(none), ALU.mult))
                        link(nc.vector.tensor_tensor(w[:], zw[:], fb[:], ALU.add))
                        normalised(w)

                    router()
                    mids(0)
                    for e in range(1, NE):
                        mids(e)
                        add(e - 1)
                    add(NE - 1)

                @block.scalar
                def _(act):
                    norm_scalar(nc, act, n, var_ready, r0_ready)
                    act.wait_ge(xnT_ready, 1)
                    for c in range(DC):
                        nc.scalar.copy(xnT_high[:, c, :], ps[:, DOWN[c], :]).then_inc(xnT_copied, 1)
                        nc.scalar.copy(xnT[:, c, :], ps[:, DOWN[c], :]).then_inc(xnT_copied, 1)
                    act.wait_ge(z_ready, 1)
                    nc.scalar.activation(ez[:], z[:], ACT.Exp, scale=-1.0).then_inc(ez_ready, 1)
                    act.wait_ge(dist_ready, 1)
                    nc.scalar.activation(zw[:], dist[:], ACT.Exp, scale=-1.0 / 0.1).then_inc(exps_ready, 1)
                    nc.scalar.activation(fb[:], dist[:], ACT.Exp, scale=-1.0 / 0.3).then_inc(exps_ready, 1)
                    for e in range(NE):
                        for m in range(FC):
                            act.wait_ge(gate_ready, FC * e + m + 1)
                            if e >= 1:
                                act.wait_ge(mid_ready, FC * (e - 1) + m + 1)
                            nc.scalar.activation(silu[:, m, :], ps[:, GATE[m], :], ACT.Silu).then_inc(silu_ready, 1)

                @block.tensor
                def _(pe):
                    norm_tensor(nc, pe, n, r.ident, [ps[:, DOWN[0], :], ps[:, DOWN[1], :]], xn_ready, xnT_ready)
                    pe.wait_ge(xnT_copied, 2 * DC)
                    for t in range(GROUP_TILES):
                        for c in range(DC):
                            mm = nc.tensor.matmul(ps[:, DOWN[2], t * NE:(t + 1) * NE], xnT[:, c, t * P:(t + 1) * P],
                                                  wr[:, c, :], start=(c == 0), stop=(c == DC - 1))
                    mm.then_inc(logits_ready, 1)

                    def hidden_product(bank, k, e, m, ready):
                        cols = slice(m * P, (m + 1) * P)
                        passes = [(wpart, xpart, c) for c in range(DC)
                                  for wpart, xpart in ((high, xnT_high), (high, xnT_low), (low, xnT_high))]
                        for j, (wpart, xpart, c) in enumerate(passes):
                            mm = nc.tensor.matmul(ps[:, bank, :], wpart[:, k, e, c, cols], xpart[:, c, :],
                                                  start=(j == 0), stop=(j == len(passes) - 1))
                        mm.then_inc(ready, 1)

                    def gate_up(e):
                        for m in range(FC):
                            if e >= 1:
                                pe.wait_ge(silu_ready, FC * (e - 1) + m + 1)
                            hidden_product(GATE[m], 0, e, m, gate_ready)
                            if e >= 1:
                                pe.wait_ge(mid_ready, FC * (e - 1) + m + 1)
                            hidden_product(UP[m], 1, e, m, up_ready)

                    def down(e):
                        pe.wait_ge(mid_ready, FC * (e + 1))
                        for t in range(GROUP_TILES):
                            if e >= 1:
                                pe.wait_ge(added, GROUP_TILES * (e - 1) + t + 1)
                            for m in range(FC):
                                mm = nc.tensor.matmul(ps[:, DOWN[t], 0:HID], mid[:, e % 2, m, t * P:(t + 1) * P],
                                                      wd[:, e, m, :], start=(m == 0), stop=(m == FC - 1))
                            mm.then_inc(down_ready, 1)

                    pe.wait_ge(low_ready, DC)
                    gate_up(0)
                    for e in range(1, NE):
                        gate_up(e)
                        down(e - 1)
                    down(NE - 1)
            end_of_round(nc, round_sems)


DH, DK, DV = 6, 32, 64
KEYS, VALS = DH * DK, DH * DV
TAPS = 4
SUB = 16
BLOCKS = P // SUB
UNITS = DH * GROUP_TILES
SET0 = 4 * DV
GATES = VALS + 2 * DH
RMS_EPS = 1e-5
JOBS = ((0, P), (KEYS, P), (P, KEYS - P), (KEYS + P, KEYS - P),
        (2 * KEYS, P), (2 * KEYS + P, P), (2 * KEYS + 2 * P, P))
QK_JOBS = 4
ATANH_TERMS = 8


def delta(nc, r, w_q, w_k, w_v, w_a, w_b, w_g, w_o, conv_q, conv_k, conv_v, a_log, dt_bias, norm_weight):
    with ExitStack() as ctx:
        def sb(name, shape, dt=F32):
            return ctx.enter_context(nc.sbuf_tensor("c_" + name, shape, dt))

        def sem(name):
            return ctx.enter_context(nc.semaphore("c_" + name))

        ps = ctx.enter_context(nc.psum_tensor("c_ps", [P, 8, 512], F32))
        n = Norm(nc, sb)
        T = GROUP_TILES
        win = sb("win", [P, DC, 2 * KEYS + VALS])
        wgate = sb("wgate", [P, DC, GATES])
        wo = sb("wo", [P, VALS // P, HID])
        taps = sb("taps", [P, len(JOBS), TAPS])
        dtb = sb("dtb", [P, 1, DH])
        neg_rate = sb("neg_rate", [P, 1, DH])
        normw = sb("normw", [P, 1, DV])
        blocks = sb("blocks", [P, BLOCKS])
        even_neg, odd_neg = sb("even_neg", [P, 1]), sb("odd_neg", [P, 1])
        off_blocks = sb("off_blocks", [P, 1, P])
        head_ones = sb("head_ones", [P, P])
        ident4 = sb("ident4", [P, T, P])
        zeros_row = sb("zeros_row", [DH, P])
        xnT = sb("xnT", [P, DC, GROUP])
        chan = sb("chan", [P, len(JOBS), GROUP])
        square = sb("square", [P, 2, GROUP])
        rnorm = sb("rnorm", [P, 2, GROUP])
        kq = sb("kq", [P, 2, 2, GROUP])
        kqg = sb("kqg", [P, 2, 2, 2, P])
        ab = sb("ab", [P, T, 2 * DH])
        u, s, s2, poly, decay, beta = [sb(x, [P, T, DH]) for x in ("u", "s", "s2", "poly", "decay", "beta")]
        eb = sb("eb", [P, T, DH])
        aT = sb("aT", [DH, T, P])
        gT = sb("gT", [DH, 2, P])
        a_all = sb("a_all", [P, DH, GROUP])
        g_all = sb("g_all", [P, 2, 2, P])
        E = sb("E", [P, DH, T, P])
        klast = sb("klast", [P, 2, DH, 1])
        ktok = sb("ktok", [P, 2, DH, DK])
        vtok = sb("vtok", [P, T, VALS])
        gate = sb("gate", [P, T, DH, DV])
        aq = sb("aq", [P, UNITS, 2, P])
        diag = sb("diag", [P, UNITS, SUB])
        urep = sb("urep", [P, SUB, UNITS, SUB])
        prod = sb("prod", [P, UNITS, SUB])
        inv = sb("inv", [P, UNITS, SUB + 1])
        tdT = a_all[:].rearrange("p h (t k) -> p (h t) k", k=P)
        low = sb("low", [P, UNITS, P])
        nT = low
        rhs = sb("rhs", [P, 2, VALS])
        y = sb("y", [P, 2, VALS])
        xk = sb("xk", [P, 2, VALS])
        state = sb("state", [P, 2, VALS])
        own = sb("own", [P, DH, DV])
        o = sb("o", [P, 2, DH, DV])
        osq = sb("osq", [P, 2, DH, DV])
        ms = sb("ms", [P, 2, DH, 1])
        oT = sb("oT", [P, 2, VALS // P, P])
        a_dram = nc.dram_tensor("a_scratch", [1, DH * GROUP], F32).ap()
        g_dram = nc.dram_tensor("g_scratch", [DH, 2 * P], F32).ap()

        names = ("var_ready r0_ready xn_ready xnT_ready xnT_copied gates_ready ab_taken gate_taken chan_ready "
                 "conv_done silu_done square_ready norms_ready rnorm_ready kq_ready a_pre exps_ready a_in a_ready "
                 "beta_ready aT_ready aT_copied g_scanned a_stored a_spread kqg_ready vT_ready vtok_ready kT_ready "
                 "ktok_ready scores_ready aq_ready lT_ready l_ready td_ready nT_ready nT_copied y_ready y_copied "
                 "step_ready step_done s_ready s_copied ks_ready rhs_ready o_ready osq_ready ms_ready r_ready "
                 "gated o_done oT_ready oT_copied out_ready out_added dve_done").split()
        S = {x: sem(x) for x in names}
        round_sems = [S[x] for x in names]
        loaded, built, masks = sem("loaded"), sem("built"), sem("masks")

        def halves(a):
            return a.rearrange("p (b t) -> p b t", b=GROUP_BATCHES)

        with nc.Block() as block:
            @block.sync
            def _(sp):
                def row(a, m):
                    return a.rearrange("(a n) -> a n", a=1).to_broadcast([P, m])

                loads = [(win[:, :, 0:KEYS], w_q.rearrange("(c p) n -> p c n", p=P)),
                         (win[:, :, KEYS:2 * KEYS], w_k.rearrange("(c p) n -> p c n", p=P)),
                         (win[:, :, 2 * KEYS:], w_v.rearrange("(c p) n -> p c n", p=P)),
                         (wgate[:, :, 0:VALS], w_g.rearrange("(c p) n -> p c n", p=P)),
                         (wgate[:, :, VALS:VALS + DH], w_a.rearrange("(c p) n -> p c n", p=P)),
                         (wgate[:, :, VALS + DH:], w_b.rearrange("(c p) n -> p c n", p=P)),
                         (wo[:], w_o.rearrange("(c p) n -> p c n", p=P)),
                         (dtb[:, 0, :], row(dt_bias, DH)), (neg_rate[:, 0, :], row(a_log, DH)),
                         (normw[:, 0, :], row(norm_weight, DV)),
                         (taps[:, 0, :], conv_q[0:P, :]), (taps[:, 1, :], conv_k[0:P, :]),
                         (taps[0:KEYS - P, 2, :], conv_q[P:KEYS, :]), (taps[0:KEYS - P, 3, :], conv_k[P:KEYS, :]),
                         (taps[:, QK_JOBS:, :], conv_v.rearrange("(j p) n -> p j n", p=P))]
                for dst, src in loads:
                    sp.dma_start(dst, src).then_inc(loaded, 16)
                sp.wait_ge(loaded, 16 * len(loads))

            @block.gpsimd
            def _(pool):
                nc.gpsimd.memset(blocks[:], 1.0)
                nc.gpsimd.memset(head_ones[:], 1.0)
                nc.gpsimd.memset(zeros_row[:], 0.0)
                nc.gpsimd.memset(kq[:], 0.0)
                nc.gpsimd.memset(g_all[:], 0.0)
                nc.gpsimd.memset(state[:], 0.0)
                nc.gpsimd.memset(inv[:, :, 0:1], 1.0).then_inc(masks, 1)
                pool.wait_ge(masks, 1)
                nc.gpsimd.affine_select(out=blocks[:], in_=blocks[:], compare_op=ALU.is_ge, fill=0.0, base=0,
                                        pattern=[[-SUB, BLOCKS]], channel_multiplier=1)
                nc.gpsimd.affine_select(out=head_ones[:], in_=head_ones[:], compare_op=ALU.is_ge, fill=0.0, base=0,
                                        pattern=[[-DK, P // DK], [0, DK]], channel_multiplier=1).then_inc(masks, 1)
                pool.wait_ge(masks, 2)
                nc.gpsimd.affine_select(out=blocks[:], in_=blocks[:], compare_op=ALU.is_ge, fill=0.0, base=SUB - 1,
                                        pattern=[[SUB, BLOCKS]], channel_multiplier=-1)
                nc.gpsimd.affine_select(out=head_ones[:], in_=head_ones[:], compare_op=ALU.is_ge, fill=0.0,
                                        base=DK - 1, pattern=[[DK, P // DK], [0, DK]],
                                        channel_multiplier=-1).then_inc(masks, 1)

            @block.vector
            def _(dve):
                for t in range(T):
                    nc.vector.tensor_copy(ident4[:, t, :], r.ident[:])
                dve.wait_ge(masks, 3)
                pairs = blocks[:].rearrange("p (b h) -> p h b", h=2)
                nc.vector.tensor_reduce(even_neg[:], pairs[:, 0:1, :], AX_X, ALU.add, negate=True)
                nc.vector.tensor_reduce(odd_neg[:], pairs[:, 1:2, :], AX_X, ALU.add, negate=True)
                wide = blocks[:].rearrange("p (b o) -> p b o", o=1).to_broadcast([P, BLOCKS, SUB])
                nc.vector.tensor_scalar(off_blocks[:, 0, :].rearrange("p (b t) -> p b t", b=BLOCKS), wide,
                                        -1.0, 1.0, ALU.mult, ALU.add)
                dve.wait_ge(masks, 3)
                for h in range(DH):
                    nc.vector.tensor_copy(own[:, h, :], head_ones[:, (h % 4) * DK:(h % 4) * DK + 1].to_broadcast([P, DV]))
                nc.vector.tensor_reduce(prod[:, 0, :], r.ident[:].rearrange("p (b t) -> p t b", b=BLOCKS),
                                        AX_X, ALU.add).then_inc(masks, 1)
                dve.wait_ge(masks, 4)
                mine = prod[:, 0, :].rearrange("p (o t) -> p o t", o=1)
                nc.vector.tensor_copy(urep[:, 0, :, :], mine.to_broadcast([P, UNITS, SUB]))
                nc.vector.tensor_copy(inv[:, :, 1:2], mine[:, :, 0:1].to_broadcast([P, UNITS, 1]))

            @block.scalar
            def _(act):
                act.wait_ge(loaded, 16 * 15)
                nc.scalar.activation(neg_rate[:], neg_rate[:], ACT.Exp).then_inc(built, 1)
                act.wait_ge(built, 1)
                nc.scalar.mul(neg_rate[:], neg_rate[:], -1.0)

        def head_rows(h):
            return slice((h % 4) * DK, (h % 4) * DK + DK)

        def tile_cols(t):
            return slice(t * P, (t + 1) * P)

        CHAN_BANKS = (6, 7, 0, 1)

        with nc.Fori(0, GROUPS) as i:
            with nc.Block() as block:
                @block.sync
                def _(sp):
                    sp.wait_ge(S["g_scanned"], 4)
                    sp.dma_start(a_dram.rearrange("a (h t) -> (a h) t", h=DH),
                                 aT[:].rearrange("h t p -> h (t p)")).then_inc(S["a_stored"], 16)
                    sp.dma_start(g_dram, gT[:].rearrange("h b p -> h (b p)")).then_inc(S["a_stored"], 16)
                    sp.wait_ge(S["a_stored"], 32)
                    sp.dma_start(a_all[:].rearrange("p h t -> p (h t)"),
                                 a_dram.to_broadcast([P, DH * GROUP])).then_inc(S["a_spread"], 16)
                    for h in range(DH):
                        sp.dma_start(g_all[head_rows(h), h // 4, :, :].rearrange("p b t -> p (b t)"),
                                     g_dram[h:h + 1, :].to_broadcast([DK, 2 * P])).then_inc(S["a_spread"], 16)
                    sp.wait_ge(S["a_spread"], 16 * (1 + DH))

                @block.gpsimd
                def _(pool):
                    for j in range(QK_JOBS):
                        m = JOBS[j][1]
                        pool.wait_ge(S["silu_done"], j + 1)
                        if j >= 2:
                            pool.wait_ge(S["norms_ready"], j - 1)
                        nc.gpsimd.tensor_tensor(square[0:m, j % 2, :], chan[0:m, j, :], chan[0:m, j, :],
                                                ALU.mult).then_inc(S["square_ready"], 1)
                    for j in range(QK_JOBS):
                        m = JOBS[j][1]
                        pool.wait_ge(S["rnorm_ready"], j + 1)
                        nc.gpsimd.tensor_tensor(kq[0:m, j // 2, 1 - j % 2, :], chan[0:m, j, :], rnorm[0:m, j % 2, :],
                                                ALU.mult).then_inc(S["kq_ready"], 1)
                    pool.wait_ge(S["kq_ready"], QK_JOBS)
                    pool.wait_ge(S["a_spread"], 16 * (1 + DH))
                    for hs in range(2):
                        for b in range(GROUP_BATCHES):
                            nc.gpsimd.tensor_tensor(
                                kqg[:, hs, :, b, :], kq[:, hs, :, tile_cols(2 * b + 1)],
                                g_all[:, hs, b:b + 1, :].to_broadcast([P, 2, P]), ALU.mult).then_inc(S["kqg_ready"], 1)
                    pool.wait_ge(S["gate_taken"], T)
                    for t in range(T):
                        nc.gpsimd.tensor_tensor(gate[:, t], gate[:, t], normw[:].to_broadcast([P, DH, DV]),
                                                ALU.mult).then_inc(S["gated"], 1)

                @block.vector
                def _(dve):
                    done = [0]

                    def link(ins):
                        done[0] += 1
                        ins.then_inc(S["dve_done"], 1)
                        dve.wait_ge(S["dve_done"], done[0])

                    x_tile = lambda t: r.x[:, bass.ds(i * T + t, 1), :].rearrange("p a d -> p (a d)")
                    norm_vector(nc, dve, link, n, x_tile, S["var_ready"], S["r0_ready"], S["xn_ready"])

                    for t in range(T):
                        dve.wait_ge(S["gates_ready"], t + 1)
                        nc.vector.tensor_copy(ab[:, t, :], ps[:, 2 + t, VALS:GATES]).then_inc(S["ab_taken"], 1)
                    dve.wait_ge(S["ab_taken"], T)
                    link(nc.vector.tensor_tensor(ab[:, :, 0:DH], ab[:, :, 0:DH], dtb[:].to_broadcast([P, T, DH]),
                                                 ALU.add))
                    nc.vector.scalar_tensor_tensor(u[:], ab[:, :, 0:DH], -1.0, ab[:, :, 0:DH], ALU.mult,
                                                   ALU.max).then_inc(S["a_pre"], 1)
                    dve.wait_ge(S["exps_ready"], 2)
                    link(nc.vector.tensor_scalar(beta[:], beta[:], 1.0, None, ALU.add))
                    nc.vector.reciprocal(beta[:], beta[:])
                    link(nc.vector.tensor_scalar(s[:], u[:], 2.0, None, ALU.add))
                    link(nc.vector.reciprocal(s[:], s[:]))
                    link(nc.vector.tensor_tensor(s[:], s[:], u[:], ALU.mult))
                    link(nc.vector.tensor_tensor(s2[:], s[:], s[:], ALU.mult))
                    link(nc.vector.tensor_scalar(poly[:], s2[:], 1.0 / (2 * ATANH_TERMS + 1), None, ALU.mult))
                    for k in range(ATANH_TERMS - 1, 0, -1):
                        link(nc.vector.scalar_tensor_tensor(poly[:], poly[:], 1.0 / (2 * k + 1), s2[:], ALU.add,
                                                            ALU.mult))
                    link(nc.vector.scalar_tensor_tensor(poly[:], poly[:], 1.0, s[:], ALU.add, ALU.mult))
                    link(nc.vector.tensor_scalar(ab[:, :, 0:DH], ab[:, :, 0:DH], 0.0, None, ALU.max))
                    link(nc.vector.scalar_tensor_tensor(poly[:], poly[:], 2.0, ab[:, :, 0:DH], ALU.mult, ALU.add))
                    nc.vector.tensor_tensor(poly[:], poly[:], neg_rate[:].to_broadcast([P, T, DH]),
                                            ALU.mult).then_inc(S["a_in"], 1)

                    def conv(j):
                        m = JOBS[j][1]
                        dve.wait_ge(S["chan_ready"], j + 1)
                        src = halves(ps[0:m, CHAN_BANKS[j % 4], :])
                        dst = halves(chan[0:m, j, :])
                        link(nc.vector.tensor_scalar(dst, src, taps[0:m, j, TAPS - 1:TAPS], None, ALU.mult))
                        for k in range(1, TAPS):
                            ins = nc.vector.scalar_tensor_tensor(dst[:, :, k:], src[:, :, 0:SEQ - k],
                                                                 taps[0:m, j, TAPS - 1 - k:TAPS - k], dst[:, :, k:],
                                                                 ALU.mult, ALU.add)
                            if k < TAPS - 1:
                                link(ins)
                        ins.then_inc(S["conv_done"], 1)

                    for j in range(len(JOBS)):
                        conv(j)
                        if j == 1:
                            dve.wait_ge(S["aT_ready"], 1)
                            nc.vector.tensor_copy(aT[:].rearrange("h t p -> h (t p)"), ps[0:DH, 2, :]
                                                  ).then_inc(S["aT_copied"], 1)
                            dve.wait_ge(S["aT_copied"], 1)
                            for b in range(GROUP_BATCHES):
                                nc.vector.tensor_tensor_scan(gT[:, b, :], aT[:, 2 * b + 1, :], zeros_row[:], 1.0,
                                                             ALU.mult, ALU.add).then_inc(S["g_scanned"], 1)
                            dve.wait_ge(S["g_scanned"], 2)
                            nc.vector.memset(aT[:, :, 0:1], 0.0).then_inc(S["g_scanned"], 2)
                    for t in range(T):
                        dve.wait_ge(S["vT_ready"], t + 1)
                        nc.vector.tensor_copy(vtok[:, t, :], ps[:, CHAN_BANKS[t], 0:VALS]).then_inc(S["vtok_ready"], 1)

                    dve.wait_ge(S["a_spread"], 16 * (1 + DH))
                    for h in range(DH):
                        ins = nc.vector.tensor_tensor_scan(E[:, h].rearrange("p t k -> p (t k)"), a_all[:, h, :],
                                                           ident4[:].rearrange("p t k -> p (t k)"), 0.0,
                                                           ALU.mult, ALU.add)
                    link(ins)
                    for b in range(GROUP_BATCHES):
                        link(nc.vector.tensor_tensor(klast[:, b], E[:, :, 2 * b, P - 1:P],
                                                     beta[:, 2 * b, :].rearrange("p (h o) -> p h o", o=1), ALU.mult))
                        dve.wait_ge(S["kT_ready"], b + 1)
                        nc.vector.tensor_tensor(ktok[:, b], ps[:, 4 + b, 0:KEYS].rearrange("p (h k) -> p h k", h=DH),
                                                klast[:, b].to_broadcast([P, DH, DK]), ALU.mult
                                                ).then_inc(S["ktok_ready"], 1)
                    for h in range(DH):
                        for t in range(T):
                            q = h * 2 + t // 2
                            dve.wait_ge(S["scores_ready"], q + 1)
                            src = ps[:, q % 4, (t % 2) * 2 * P:(t % 2 + 1) * 2 * P].rearrange("p (c t) -> p c t", c=2)
                            nc.vector.scalar_tensor_tensor(aq[:, h * T + t], src, beta[:, t, h:h + 1],
                                                           E[:, h, t:t + 1, :].to_broadcast([P, 2, P]),
                                                           ALU.mult, ALU.mult).then_inc(S["aq_ready"], 1)
                    dve.wait_ge(S["aq_ready"], UNITS)
                    for h in range(DH):
                        dve.wait_ge(S["lT_ready"], h + 1)
                        nc.vector.tensor_tensor(low[:, h * T:(h + 1) * T, :],
                                                ps[:, 4 + h % 2, :].rearrange("p (t k) -> p t k", t=T),
                                                off_blocks[:].to_broadcast([P, T, P]), ALU.mult
                                                ).then_inc(S["l_ready"], 1)
                    for q in range(P // 32):
                        rows = slice(32 * q, 32 * q + 32)
                        ins = nc.vector.tensor_scalar(diag[rows], aq[rows, :, 0, 32 * q:32 * q + SUB],
                                                      even_neg[rows], None, ALU.mult)
                    link(ins)
                    for q in range(P // 32):
                        rows = slice(32 * q, 32 * q + 32)
                        ins = nc.vector.scalar_tensor_tensor(diag[rows], aq[rows, :, 0, 32 * q + SUB:32 * q + 32],
                                                             odd_neg[rows], diag[rows], ALU.mult, ALU.add)
                    link(ins)
                    for k in range(SUB - 1):
                        ins = nc.vector.stream_shuffle(urep[:, 1 + k].rearrange("p u t -> p (u t)"),
                                                       diag[:].rearrange("p u t -> p (u t)"),
                                                       [k] * SUB + [SUB + k] * SUB)
                    link(ins)
                    for t in range(1, SUB):
                        link(nc.vector.tensor_tensor(prod[:, :, 0:t + 1], inv[:, :, 0:t + 1],
                                                     urep[:, 0:t + 1, :, t].rearrange("p k u -> p u k"), ALU.mult))
                        link(nc.vector.reduce_sum(inv[:, :, 1 + t:2 + t], prod[:, :, 0:t + 1], AX_X))
                    for h in range(DH):
                        us = slice(h * T, (h + 1) * T)
                        nc.vector.tensor_tensor(
                            tdT[:, us, :].rearrange("p u (b t) -> p u b t", b=BLOCKS),
                            inv[:, us, 1:SUB + 1].rearrange("p u (o t) -> p u o t", o=1).to_broadcast(
                                [P, T, BLOCKS, SUB]),
                            blocks[:].rearrange("p (o b k) -> p o b k", o=1, k=1).to_broadcast([P, T, BLOCKS, SUB]),
                            ALU.mult).then_inc(S["td_ready"], 1)

                    STEPS = BLOCKS - 1
                    for half in range(2):
                        if half:
                            for b in range(GROUP_BATCHES):
                                dve.wait_ge(S["s_ready"], b + 1)
                                nc.vector.tensor_tensor(state[:, b, 0:SET0], ps[:, 4 + b, 0:SET0],
                                                        own[:, 0:4, :].rearrange("p h v -> p (h v)"), ALU.mult)
                                low_rows = slice(0, KEYS - P)
                                nc.vector.tensor_tensor(state[low_rows, b, SET0:VALS], ps[low_rows, 4 + b, SET0:VALS],
                                                        own[low_rows, 4:DH, :].rearrange("p h v -> p (h v)"),
                                                        ALU.mult).then_inc(S["s_copied"], 1)
                            for b in range(GROUP_BATCHES):
                                dve.wait_ge(S["ks_ready"], b + 1)
                                nc.vector.tensor_tensor(rhs[:, b, :], vtok[:, 2 * b + 1, :], ps[:, 4 + b, 0:VALS],
                                                        ALU.subtract).then_inc(S["rhs_ready"], 1)
                        for k in range(STEPS):
                            for b in range(GROUP_BATCHES):
                                nstep = (half * STEPS + k) * 2 + b
                                dve.wait_ge(S["step_ready"], nstep + 1)
                                if k == 0:
                                    dve.wait_ge(S["y_copied"], half * 2 + b + 1)
                                nc.vector.tensor_tensor(xk[:, b, :], y[:, b, :], ps[:, b, 0:VALS],
                                                        ALU.add).then_inc(S["step_done"], 1)
                        for b in range(GROUP_BATCHES):
                            job = half * 2 + b
                            t = 2 * b + half
                            dve.wait_ge(S["osq_ready"], job + 1)
                            link(nc.vector.reduce_sum(ms[:, b], osq[:, b], AX_X))
                            nc.vector.tensor_scalar(ms[:, b], ms[:, b], 1.0 / DV, RMS_EPS, ALU.mult, ALU.add
                                                    ).then_inc(S["ms_ready"], 1)
                            dve.wait_ge(S["gated"], t + 1)
                            link(nc.vector.tensor_tensor(o[:, b], ps[:, 6 + b, 0:VALS].rearrange(
                                "p (h v) -> p h v", h=DH), gate[:, t], ALU.mult))
                            dve.wait_ge(S["r_ready"], 2 * (job + 1))
                            nc.vector.tensor_tensor(o[:, b], o[:, b], ms[:, b].to_broadcast([P, DH, DV]),
                                                    ALU.mult).then_inc(S["o_done"], 1)
                        for b in range(GROUP_BATCHES):
                            job = half * 2 + b
                            dve.wait_ge(S["out_ready"], job + 1)
                            nc.vector.tensor_tensor(x_tile(2 * b + half), x_tile(2 * b + half), ps[:, 4 + b, 0:HID],
                                                    ALU.add).then_inc(S["out_added"], 1)

                @block.scalar
                def _(act):
                    norm_scalar(nc, act, n, S["var_ready"], S["r0_ready"])
                    act.wait_ge(S["xnT_ready"], 1)
                    for c in range(DC):
                        nc.scalar.copy(xnT[:, c, :], ps[:, c, :]).then_inc(S["xnT_copied"], 1)
                    act.wait_ge(S["a_pre"], 1)
                    nc.scalar.activation(u[:], u[:], ACT.Exp, scale=-1.0).then_inc(S["exps_ready"], 1)
                    nc.scalar.activation(beta[:], ab[:, :, DH:], ACT.Exp, scale=-1.0).then_inc(S["exps_ready"], 1)
                    act.wait_ge(S["a_in"], 1)
                    nc.scalar.activation(decay[:], poly[:], ACT.Exp).then_inc(S["a_ready"], 1)
                    for t in range(T):
                        act.wait_ge(S["ab_taken"], T)
                        nc.scalar.activation(gate[:, t].rearrange("p h v -> p (h v)"), ps[:, 2 + t, 0:VALS],
                                             ACT.Silu).then_inc(S["gate_taken"], 1)
                    for j in range(len(JOBS)):
                        m = JOBS[j][1]
                        act.wait_ge(S["conv_done"], j + 1)
                        nc.scalar.activation(chan[0:m, j, :], chan[0:m, j, :], ACT.Silu).then_inc(S["silu_done"], 1)
                    for j in range(QK_JOBS):
                        m = JOBS[j][1]
                        act.wait_ge(S["norms_ready"], j + 1)
                        if j >= 2:
                            act.wait_ge(S["kq_ready"], j - 1)
                        nc.scalar.activation(rnorm[0:m, j % 2, :], ps[0:m, 3 + j % 2, :], ACT.Ln,
                                             scale=float(DK) if j % 2 == 0 else 1.0).then_inc(S["exps_ready"], 1)
                        act.wait_ge(S["exps_ready"], 3 + j)
                        nc.scalar.activation(rnorm[0:m, j % 2, :], rnorm[0:m, j % 2, :], ACT.Exp,
                                             scale=-0.5).then_inc(S["rnorm_ready"], 1)
                    for h in range(DH):
                        act.wait_ge(S["nT_ready"], h + 1)
                        nc.scalar.mul(nT[:, h * T:(h + 1) * T, :].rearrange("p u t -> p (u t)"), ps[:, 6 + h % 2, :],
                                      -1.0).then_inc(S["nT_copied"], 1)
                    for half in range(2):
                        for b in range(GROUP_BATCHES):
                            act.wait_ge(S["y_ready"], half * 2 + b + 1)
                            nc.scalar.copy(y[:, b, :], ps[:, 2 + b, 0:VALS]).then_inc(S["y_copied"], 1)
                        for b in range(GROUP_BATCHES):
                            job = half * 2 + b
                            act.wait_ge(S["o_ready"], job + 1)
                            if half:
                                act.wait_ge(S["ms_ready"], b + 1)
                            nc.scalar.activation(osq[:, b].rearrange("p h v -> p (h v)"), ps[:, 6 + b, 0:VALS],
                                                 ACT.Square).then_inc(S["osq_ready"], 1)
                            act.wait_ge(S["ms_ready"], job + 1)
                            nc.scalar.activation(ms[:, b], ms[:, b], ACT.Ln).then_inc(S["r_ready"], 1)
                            act.wait_ge(S["r_ready"], 2 * job + 1)
                            nc.scalar.activation(ms[:, b], ms[:, b], ACT.Exp, scale=-0.5).then_inc(S["r_ready"], 1)
                        for b in range(GROUP_BATCHES):
                            job = half * 2 + b
                            act.wait_ge(S["oT_ready"], job + 1)
                            nc.scalar.copy(oT[:, b].rearrange("p c t -> p (c t)"), ps[:, 2 + b, 0:VALS]
                                           ).then_inc(S["oT_copied"], 1)

                @block.tensor
                def _(pe):
                    norm_tensor(nc, pe, n, r.ident, [ps[:, 0, :], ps[:, 1, :]], S["xn_ready"], S["xnT_ready"])
                    pe.wait_ge(S["xnT_copied"], DC)
                    for t in range(T):
                        for c in range(DC):
                            mm = nc.tensor.matmul(ps[:, 2 + t, 0:GATES], xnT[:, c, tile_cols(t)], wgate[:, c, :],
                                                  start=(c == 0), stop=(c == DC - 1))
                        mm.then_inc(S["gates_ready"], 1)
                    for j, (col, m) in enumerate(JOBS):
                        if j >= 4:
                            pe.wait_ge(S["conv_done"], j - 3)
                        for c in range(DC):
                            mm = nc.tensor.matmul(ps[0:m, CHAN_BANKS[j % 4], :], win[:, c, col:col + m], xnT[:, c, :],
                                                  start=(c == 0), stop=(c == DC - 1))
                        mm.then_inc(S["chan_ready"], 1)
                        if j == 3:
                            pe.wait_ge(S["a_ready"], 1)
                            pe.wait_ge(S["gate_taken"], 1)
                            for t in range(T):
                                mm = nc.tensor.transpose(ps[0:DH, 2, tile_cols(t)], decay[:, t, :], r.ident[:])
                            mm.then_inc(S["aT_ready"], 1)
                    for j in range(QK_JOBS):
                        m = JOBS[j][1]
                        pe.wait_ge(S["square_ready"], j + 1)
                        pe.wait_ge(S["gate_taken"], T)
                        if j >= 2:
                            pe.wait_ge(S["rnorm_ready"], j - 1)
                        nc.tensor.matmul(ps[0:m, 3 + j % 2, :], head_ones[0:m, 0:m], square[0:m, j % 2, :],
                                         start=True, stop=True).then_inc(S["norms_ready"], 1)
                    pe.wait_ge(S["silu_done"], len(JOBS))
                    for t in range(T):
                        for c in range(VALS // P):
                            mm = nc.tensor.transpose(ps[:, CHAN_BANKS[t], c * P:(c + 1) * P],
                                                     chan[:, QK_JOBS + c, tile_cols(t)], r.ident[:])
                        mm.then_inc(S["vT_ready"], 1)
                    pe.wait_ge(S["kq_ready"], QK_JOBS)
                    for b in range(GROUP_BATCHES):
                        nc.tensor.transpose(ps[:, 4 + b, 0:P], kq[:, 0, 0, tile_cols(2 * b)], r.ident[:])
                        nc.tensor.transpose(ps[:, 4 + b, P:KEYS], kq[0:KEYS - P, 1, 0, tile_cols(2 * b)],
                                            r.ident[0:KEYS - P, 0:KEYS - P]).then_inc(S["kT_ready"], 1)
                    pe.wait_ge(S["vtok_ready"], T)
                    pe.wait_ge(S["aT_copied"], 1)

                    def turn_l(h):
                        pe.wait_ge(S["aq_ready"], T * (h + 1))
                        pe.wait_ge(S["ktok_ready"], 2)
                        if h >= 2:
                            pe.wait_ge(S["l_ready"], h - 1)
                        for t in range(T):
                            mm = nc.tensor.transpose(ps[:, 4 + h % 2, tile_cols(t)], aq[:, h * T + t, 0, :], r.ident[:])
                        mm.then_inc(S["lT_ready"], 1)

                    for h in range(DH):
                        rows = head_rows(h)
                        for tt in range(2):
                            q = 2 * h + tt
                            if q >= 4:
                                pe.wait_ge(S["aq_ready"], 2 * (q - 3))
                            for t in (2 * tt, 2 * tt + 1):
                                mm = nc.tensor.matmul(ps[:, q % 4, (t % 2) * 2 * P:(t % 2 + 1) * 2 * P],
                                                      kq[rows, h // 4, 0, tile_cols(t)], kq[rows, h // 4, :, tile_cols(t)],
                                                      start=True, stop=True)
                            mm.then_inc(S["scores_ready"], 1)
                    for h in range(DH):
                        turn_l(h)
                    for h in range(DH):
                        pe.wait_ge(S["td_ready"], h + 1)
                        pe.wait_ge(S["l_ready"], h + 1)
                        if h >= 2:
                            pe.wait_ge(S["nT_copied"], h - 1)
                        for t in range(T):
                            mm = nc.tensor.matmul(ps[:, 6 + h % 2, tile_cols(t)], low[:, h * T + t, :],
                                                  tdT[:, h * T + t, :], start=True, stop=True)
                        mm.then_inc(S["nT_ready"], 1)
                    pe.wait_ge(S["nT_copied"], DH)

                    def head_cols(h):
                        return slice(h * DV, (h + 1) * DV)

                    STEPS = BLOCKS - 1
                    for half in range(2):
                        if half:
                            for b in range(GROUP_BATCHES):
                                pe.wait_ge(S["out_added"], b + 1)
                                nc.tensor.matmul(ps[:, 4 + b, 0:SET0], ktok[:, b, 0:4, :].rearrange("p h k -> p (h k)"), xk[:, b, 0:SET0],
                                                 start=True, stop=True)
                                nc.tensor.matmul(ps[0:KEYS - P, 4 + b, SET0:VALS], ktok[:, b, 4:DH, :].rearrange("p h k -> p (h k)"),
                                                 xk[:, b, SET0:VALS], start=True, stop=True
                                                 ).then_inc(S["s_ready"], 1)
                            pe.wait_ge(S["kqg_ready"], 4)
                            for b in range(GROUP_BATCHES):
                                pe.wait_ge(S["s_copied"], b + 1)
                                for hs, cols in enumerate((slice(0, SET0), slice(SET0, VALS))):
                                    mm = nc.tensor.matmul(ps[:, 4 + b, cols], kqg[:, hs, 0, b, :], state[:, b, cols],
                                                          start=True, stop=True)
                                mm.then_inc(S["ks_ready"], 1)
                        for b in range(GROUP_BATCHES):
                            t = 2 * b + half
                            if half:
                                pe.wait_ge(S["rhs_ready"], b + 1)
                            r_in = rhs[:, b, :] if half else vtok[:, t, :]
                            for h in range(DH):
                                mm = nc.tensor.matmul(ps[:, 2 + b, head_cols(h)], tdT[:, h * T + t, :],
                                                      r_in[:, head_cols(h)], start=True, stop=True)
                            mm.then_inc(S["y_ready"], 1)
                        for k in range(STEPS):
                            for b in range(GROUP_BATCHES):
                                t = 2 * b + half
                                if k == 0:
                                    pe.wait_ge(S["y_copied"], half * 2 + b + 1)
                                else:
                                    pe.wait_ge(S["step_done"], (half * STEPS + k - 1) * 2 + b + 1)
                                src = y if k == 0 else xk
                                for h in range(DH):
                                    mm = nc.tensor.matmul(ps[:, b, head_cols(h)], nT[:, h * T + t, :],
                                                          src[:, b, head_cols(h)], start=True, stop=True)
                                mm.then_inc(S["step_ready"], 1)
                        for b in range(GROUP_BATCHES):
                            t = 2 * b + half
                            pe.wait_ge(S["step_done"], ((half + 1) * STEPS - 1) * 2 + b + 1)
                            if half:
                                pe.wait_ge(S["o_done"], b + 1)
                            if half:
                                for hs, cols in enumerate((slice(0, SET0), slice(SET0, VALS))):
                                    nc.tensor.matmul(ps[:, 6 + b, cols], kqg[:, hs, 1, b, :], state[:, b, cols],
                                                     start=(hs == 0), stop=False, skip_group_check=True)
                            for h in range(DH):
                                mm = nc.tensor.matmul(ps[:, 6 + b, head_cols(h)], aq[:, h * T + t, 1, :],
                                                      xk[:, b, head_cols(h)], start=not half, stop=True,
                                                      skip_group_check=bool(half))
                            mm.then_inc(S["o_ready"], 1)
                        for b in range(GROUP_BATCHES):
                            job = half * 2 + b
                            pe.wait_ge(S["o_done"], job + 1)
                            of = o[:, b].rearrange("p h v -> p (h v)")
                            for c in range(VALS // P):
                                mm = nc.tensor.transpose(ps[:, 2 + b, c * P:(c + 1) * P], of[:, c * P:(c + 1) * P],
                                                         r.ident[:])
                            mm.then_inc(S["oT_ready"], 1)
                        for b in range(GROUP_BATCHES):
                            job = half * 2 + b
                            pe.wait_ge(S["oT_copied"], job + 1)
                            for c in range(VALS // P):
                                mm = nc.tensor.matmul(ps[:, 4 + b, 0:HID], oT[:, b, c, :], wo[:, c, :],
                                                      start=(c == 0), stop=(c == VALS // P - 1))
                            mm.then_inc(S["out_ready"], 1)
            end_of_round(nc, round_sems)


EXPERTS, FF, TOP = 6, 176, 2
FF1 = FF - P
BIAS_ROW = 64
W1_AT, W2_AT, B1_AT = 0, DC * FF, DC * FF + 2 * HID
PACKED = B1_AT + 2
ROUND_BATCHES = 4


def routed(nc, r, packed, w_gate, out):
    with ExitStack() as ctx:
        def sb(name, shape, dt=F32):
            return ctx.enter_context(nc.sbuf_tensor("d_" + name, shape, dt))

        def sem(name):
            return ctx.enter_context(nc.semaphore("d_" + name))

        ps = ctx.enter_context(nc.psum_tensor("d_ps", [P, 8, 512], F32))
        HIDDEN, OUT = (0, 1, 2, 3), (4, 5)
        n = Norm(nc, sb)
        gate_w = sb("gate_w", [P, DC, EXPERTS])
        xnT = sb("xnT", [P, DC, TOKENS])
        sums = sb("sums", [P, DC, BATCH])
        BE = [1, BATCH, EXPERTS]
        rank_of, index_of = sb("rank_of", [1, 1, EXPERTS]), sb("index_of", [1, 1, EXPERTS])
        prob, eq, key, picked, rest, part = [sb(x, BE) for x in ("prob", "eq", "key", "picked", "rest", "part")]
        top, best, total = [sb(x, [1, BATCH, 1]) for x in ("top", "best", "total")]
        chosen, chosen_f = sb("chosen", [1, BATCH * TOP], I32), sb("chosen_f", [1, BATCH, TOP])
        weight = sb("weight", [1, BATCH, TOP])
        weights = sb("weights", [P, BATCH * TOP])
        slots = sb("slots", [P, ROUND_BATCHES * TOP, PACKED])
        gelu = sb("gelu", [P, 2, 2, SEQ])
        hid = sb("hid", [P, 2 * TOP, 2, SEQ])

        gate_loaded, zeroed = sem("gate_loaded"), sem("zeroed")
        names = ("var_ready r0_ready xn_ready xnT_ready xnT_copied dve_done").split()
        N = {x: sem(x) for x in names}
        logits_ready, exp_ready, shifted, weight_ready, spread_ready, route_done = [
            sem(x) for x in ("logits_ready", "exp_ready", "shifted", "weight_ready", "spread_ready", "route_done")]
        names = ("hidden_ready gelu_done hid_ready out_ready added stored").split()
        S = {x: sem(x) for x in names}
        slot_loaded = [sem(f"slot_loaded{j}") for j in range(ROUND_BATCHES * TOP)]

        with nc.Block() as block:
            @block.sync
            def _(sp):
                sp.dma_start(gate_w[:], w_gate.rearrange("(c p) e -> p c e", p=P)).then_inc(gate_loaded, 16)

        with nc.Fori(0, GROUPS) as i:
            with nc.Block() as block:
                @block.vector
                def _(dve):
                    done = [0]

                    def link(ins):
                        done[0] += 1
                        ins.then_inc(N["dve_done"], 1)
                        dve.wait_ge(N["dve_done"], done[0])

                    x_tile = lambda t: r.x[:, bass.ds(i * GROUP_TILES + t, 1), :].rearrange("p a d -> p (a d)")
                    norm_vector(nc, dve, link, n, x_tile, N["var_ready"], N["r0_ready"], N["xn_ready"])
                    for c in range(DC):
                        dve.wait_ge(N["xnT_copied"], c + 1)
                        nc.vector.reduce_sum(sums[:, c, bass.ds(i * GROUP_BATCHES, GROUP_BATCHES)],
                                             ps[:, c, :].rearrange("p (b t) -> p b t", b=GROUP_BATCHES), AX_X)

                @block.scalar
                def _(act):
                    norm_scalar(nc, act, n, N["var_ready"], N["r0_ready"])
                    act.wait_ge(N["xnT_ready"], 1)
                    for c in range(DC):
                        nc.scalar.copy(xnT[:, c, bass.ds(i * GROUP, GROUP)], ps[:, c, :]
                                       ).then_inc(N["xnT_copied"], 1)

                @block.tensor
                def _(pe):
                    norm_tensor(nc, pe, n, r.ident, [ps[:, 0, :], ps[:, 1, :]], N["xn_ready"], N["xnT_ready"])
            end_of_round(nc, list(N.values()))

        with nc.Block() as block:
            @block.tensor
            def _(pe):
                pe.wait_ge(gate_loaded, 16)
                for b in range(BATCH):
                    for c in range(DC):
                        mm = nc.tensor.matmul(ps[0:1, 0, b * EXPERTS:(b + 1) * EXPERTS], sums[:, c, b:b + 1],
                                              gate_w[:, c, :], start=(c == 0), stop=(c == DC - 1))
                mm.then_inc(logits_ready, 1)
                pe.wait_ge(weight_ready, 1)
                nc.tensor.matmul(ps[:, 1, 0:BATCH * TOP], r.ones_row[:], weight[:].rearrange("o b k -> o (b k)"),
                                 start=True, stop=True).then_inc(spread_ready, 1)

            @block.scalar
            def _(act):
                act.wait_ge(shifted, 1)
                nc.scalar.activation(prob[:], prob[:], ACT.Exp, scale=1.0 / SEQ).then_inc(exp_ready, 1)

            @block.gpsimd
            def _(pool):
                nc.gpsimd.memset(hid[:], 0.0)
                nc.gpsimd.iota(index_of[:], pattern=[[1, EXPERTS]], base=0, channel_multiplier=0,
                               allow_small_or_imprecise_dtypes=True)
                nc.gpsimd.iota(rank_of[:], pattern=[[-1, EXPERTS]], base=EXPERTS, channel_multiplier=0,
                               allow_small_or_imprecise_dtypes=True).then_inc(zeroed, 1)

            @block.vector
            def _(dve):
                done = [0]

                def link(ins):
                    done[0] += 1
                    ins.then_inc(route_done, 1)
                    dve.wait_ge(route_done, done[0])

                dve.wait_ge(logits_ready, 1)
                dve.wait_ge(zeroed, 1)
                logits = ps[0:1, 0, 0:BATCH * EXPERTS].rearrange("o (b e) -> o b e", b=BATCH)
                link(nc.vector.reduce_max(top[:], logits, AX_X))
                nc.vector.tensor_tensor(prob[:], logits, top[:].to_broadcast(BE), ALU.subtract).then_inc(shifted, 1)
                dve.wait_ge(exp_ready, 1)
                link(nc.vector.reduce_sum(total[:], prob[:], AX_X))
                link(nc.vector.reciprocal(total[:], total[:]))
                link(nc.vector.tensor_tensor(prob[:], prob[:], total[:].to_broadcast(BE), ALU.mult))

                def pick(values, k):
                    link(nc.vector.reduce_max(top[:], values[:], AX_X))
                    link(nc.vector.tensor_tensor(eq[:], values[:], top[:].to_broadcast(BE), ALU.is_equal))
                    link(nc.vector.tensor_tensor(key[:], eq[:], rank_of[:].to_broadcast(BE), ALU.mult))
                    link(nc.vector.reduce_max(best[:], key[:], AX_X))
                    link(nc.vector.tensor_tensor(picked[:], key[:], best[:].to_broadcast(BE), ALU.is_equal))
                    link(nc.vector.tensor_tensor(part[:], picked[:], index_of[:].to_broadcast(BE), ALU.mult))
                    link(nc.vector.reduce_sum(chosen_f[:, :, k:k + 1], part[:], AX_X))
                    link(nc.vector.tensor_copy(weight[:, :, k:k + 1], top[:]))

                pick(prob, 0)
                link(nc.vector.scalar_tensor_tensor(rest[:], picked[:], -4.0, prob[:], ALU.mult, ALU.add))
                pick(rest, 1)
                link(nc.vector.reduce_sum(total[:], weight[:], AX_X))
                link(nc.vector.reciprocal(total[:], total[:]))
                nc.vector.tensor_tensor(weight[:], weight[:], total[:].to_broadcast([1, BATCH, TOP]),
                                        ALU.mult).then_inc(weight_ready, 1)
                nc.vector.tensor_copy(chosen[:], chosen_f[:].rearrange("o b k -> o (b k)"))
                dve.wait_ge(spread_ready, 1)
                nc.vector.tensor_copy(weights[:], ps[:, 1, 0:BATCH * TOP])

        with nc.Fori(0, BATCH // ROUND_BATCHES) as i:
            with nc.Block() as block:
                @block.sync
                def _(sp):
                    for j in range(ROUND_BATCHES * TOP):
                        e = sp.value_load(chosen[0:1, bass.ds(i * ROUND_BATCHES * TOP + j, 1)],
                                          min_val=0, max_val=EXPERTS - 1)
                        sp.dma_start(slots[:, j, :], packed[bass.ds(e, 1)].rearrange("e p n -> p (e n)")
                                     ).then_inc(slot_loaded[j], 16)
                    for b in range(ROUND_BATCHES):
                        sp.wait_ge(S["added"], 2 * (b + 1))
                        sp.dma_start(out[bass.ds(i * ROUND_BATCHES + b, 1)].rearrange("b (h p) d -> p (b h) d", p=P),
                                     r.x[:, bass.ds(i * ROUND_BATCHES * 2 + 2 * b, 2), :]).then_inc(S["stored"], 16)
                    sp.wait_ge(S["stored"], 16 * ROUND_BATCHES)

                @block.tensor
                def _(pe):
                    def hidden(j):
                        pe.wait_ge(slot_loaded[j], 16)
                        if j >= 4:
                            pe.wait_ge(S["gelu_done"], 2 * (j - 3))
                        for m, rows in enumerate((P, FF1)):
                            for c in range(DC):
                                mm = nc.tensor.matmul(
                                    ps[0:rows, HIDDEN[j % 4], m * SEQ:(m + 1) * SEQ],
                                    slots[:, j, c * FF + m * P:c * FF + m * P + rows],
                                    xnT[:, c, bass.ds((i * ROUND_BATCHES + j // TOP) * SEQ, SEQ)],
                                    start=(c == 0), stop=(c == DC - 1))
                        mm.then_inc(S["hidden_ready"], 1)

                    def down(b):
                        pe.wait_ge(S["hid_ready"], TOP * (b + 1))
                        for t in range(2):
                            job = 2 * b + t
                            if job >= 2:
                                pe.wait_ge(S["added"], job - 1)
                            for k in range(TOP):
                                j = b * TOP + k
                                cols = slice(t * P, (t + 1) * P)
                                nc.tensor.matmul(ps[:, OUT[job % 2], 0:HID], hid[:, j % 4, 0, cols],
                                                 slots[:, j, W2_AT:W2_AT + HID], start=(k == 0), stop=False)
                                mm = nc.tensor.matmul(ps[:, OUT[job % 2], 0:HID], hid[:, j % 4, 1, cols],
                                                      slots[:, j, W2_AT + HID:W2_AT + 2 * HID],
                                                      start=False, stop=(k == TOP - 1))
                            mm.then_inc(S["out_ready"], 1)

                    for b in range(ROUND_BATCHES + 1):
                        if b < ROUND_BATCHES:
                            for k in range(TOP):
                                hidden(b * TOP + k)
                        if b >= 1:
                            down(b - 1)

                @block.scalar
                def _(act):
                    for j in range(ROUND_BATCHES * TOP):
                        act.wait_ge(S["hidden_ready"], j + 1)
                        if j >= 2:
                            act.wait_ge(S["hid_ready"], j - 1)
                        for m, rows in enumerate((P, FF1)):
                            nc.scalar.activation(gelu[0:rows, j % 2, m, :], ps[0:rows, HIDDEN[j % 4], m * SEQ:(m + 1) * SEQ],
                                                 ACT.Gelu, bias=slots[0:rows, j, B1_AT + m:B1_AT + m + 1]
                                                 ).then_inc(S["gelu_done"], 1)

                @block.vector
                def _(dve):
                    def weighted(j):
                        dve.wait_ge(S["gelu_done"], 2 * (j + 1))
                        if j >= 4:
                            dve.wait_ge(S["out_ready"], 2 * ((j - 4) // TOP + 1))
                        w_at = i * ROUND_BATCHES * TOP + j
                        nc.vector.tensor_scalar(hid[:, j % 4, 0, :], gelu[:, j % 2, 0, :],
                                                weights[:, bass.ds(w_at, 1)], None, ALU.mult)
                        nc.vector.tensor_copy(hid[BIAS_ROW:BIAS_ROW + 1, j % 4, 1, :],
                                              weights[BIAS_ROW:BIAS_ROW + 1, bass.ds(w_at, 1)].to_broadcast([1, SEQ]))
                        nc.vector.tensor_scalar(hid[0:FF1, j % 4, 1, :], gelu[0:FF1, j % 2, 1, :],
                                                weights[0:FF1, bass.ds(w_at, 1)], None, ALU.mult
                                                ).then_inc(S["hid_ready"], 1)

                    def add(b):
                        for t in range(2):
                            job = 2 * b + t
                            dve.wait_ge(S["out_ready"], job + 1)
                            xt = r.x[:, bass.ds(i * ROUND_BATCHES * 2 + job, 1), :].rearrange("p a d -> p (a d)")
                            nc.vector.tensor_tensor(xt, xt, ps[:, OUT[job % 2], 0:HID], ALU.add
                                                    ).then_inc(S["added"], 1)

                    for b in range(ROUND_BATCHES + 1):
                        if b < ROUND_BATCHES:
                            for k in range(TOP):
                                weighted(b * TOP + k)
                        if b >= 1:
                            add(b - 1)
            end_of_round(nc, list(S.values()) + slot_loaded)


def build(nc, a, out):
    with ExitStack() as ctx:
        r = Resident(nc, ctx)
        setup(nc, a["hidden"], r)
        attention(nc, r, a["A_q"], a["A_k"], a["A_v"], a["A_o"], a["A_bo"])
        experts(nc, r, a["B_g"], a["B_u"], a["B_d"], a["B_ga"], a["B_gb"], a["B_ua"], a["B_ub"], a["B_da"],
                a["B_db"], a["B_r"], a["B_temp"])
        delta(nc, r, a["C_q"], a["C_k"], a["C_v"], a["C_a"], a["C_b"], a["C_g"], a["C_o"], a["C_cq"], a["C_ck"],
              a["C_cv"], a["C_alog"], a["C_dt"], a["C_nw"])
        routed(nc, r, a["D_packed"], a["D_gate"], out)


def kernel(**inputs):
    import numpy as np
    import concourse.bacc as bacc
    from concourse.bass_utils import run_bass_kernel_spmd

    def layer(prefix):
        return {k[len(prefix):]: np.asarray(v) for k, v in inputs.items() if k.startswith(prefix)}

    A, B, C, D = layer("L0_attn_"), layer("L0_ffn_"), layer("L1_attn_"), layer("L1_ffn_")
    packed = np.zeros((EXPERTS, P, PACKED), D["W1"].dtype)
    for c in range(DC):
        packed[:, :, c * FF:(c + 1) * FF] = D["W1"][:, c * P:(c + 1) * P, :]
    packed[:, :, W2_AT:W2_AT + HID] = D["W2"][:, 0:P, :]
    packed[:, 0:FF1, W2_AT + HID:W2_AT + 2 * HID] = D["W2"][:, P:FF, :]
    packed[:, BIAS_ROW, W2_AT + HID:W2_AT + 2 * HID] = D["b2"]
    packed[:, :, B1_AT] = D["b1"][:, 0:P]
    packed[:, 0:FF1, B1_AT + 1] = D["b1"][:, P:FF]
    arrays = {
        "hidden": A["hidden_states"],
        "A_q": A["Wq"].T, "A_k": A["Wk"].T, "A_v": A["Wv"].T, "A_o": A["Wo"].T, "A_bo": A["bo"],
        "B_g": B["Wg"], "B_u": B["Wu"], "B_d": B["Wd"],
        "B_ga": B["Ga"].transpose(0, 2, 1), "B_gb": B["Gb"], "B_ua": B["Ua"].transpose(0, 2, 1), "B_ub": B["Ub"],
        "B_da": B["Da"].transpose(0, 2, 1), "B_db": B["Db"], "B_r": B["Wr"], "B_temp": B["temperature"],
        "C_q": C["Wq"], "C_k": C["Wk"], "C_v": C["Wv"], "C_a": C["Wa"], "C_b": C["Wb"], "C_g": C["Wg"],
        "C_o": C["Wo"], "C_cq": C["conv_wq"], "C_ck": C["conv_wk"], "C_cv": C["conv_wv"], "C_alog": C["A_log"],
        "C_dt": C["dt_bias"], "C_nw": C["norm_weight"],
        "D_packed": packed, "D_gate": D["gate_W"].T,
    }
    nc = bacc.Bacc("TRN2", target_bir_lowering=False, num_devices=1)
    arrays = {"in_" + k: np.ascontiguousarray(v) for k, v in arrays.items()}
    dram = {k[3:]: nc.dram_tensor(k, v.shape, mybir.dt.from_np(v.dtype), kind="ExternalInput").ap()
            for k, v in arrays.items()}
    out = nc.dram_tensor("out", (BATCH, SEQ, HID), F32, kind="ExternalOutput").ap()
    build(nc, dram, out)
    return run_bass_kernel_spmd(nc, [arrays], core_ids=[0]).results[0]["out"]
```

```python
import math
from contextlib import ExitStack

import concourse.bass as bass
from concourse import mybir
from concourse.alu_op_type import AluOpType as ALU

ACT = mybir.ActivationFunctionType
F32 = mybir.dt.float32
BF16 = mybir.dt.bfloat16
I32 = mybir.dt.int32
AX_X = mybir.AxisListType.X

P = 128
BATCH, SEQ, HID = 8, 256, 256
TOKENS = BATCH * SEQ
TILES = TOKENS // P
DC = HID // P
GROUP_TILES = 4
GROUP = GROUP_TILES * P
GROUPS = TOKENS // GROUP
GROUP_BATCHES = GROUP // SEQ
LN_EPS = 1e-5
NEG = -1e30


class Resident:

    def __init__(self, nc, ctx):
        def sb(name, shape, dt=F32):
            return ctx.enter_context(nc.sbuf_tensor(name, shape, dt))

        self.x = sb("x", [P, TILES, HID])
        self.ident = sb("ident", [P, P])
        self.ident_bf = sb("ident_bf", [P, P], BF16)
        self.causal_bf = sb("causal_bf", [P, P], BF16)
        self.ones_row = sb("ones_row", [1, P])
        self.x_loaded = ctx.enter_context(nc.semaphore("x_loaded"))


def end_of_round(nc, sems):
    nums = sorted(s.num for s in sems)
    while nums:
        n = 1
        while n < len(nums) and nums[n] == nums[0] + n:
            n += 1
        nc.gpsimd.sem_clear(range(nums[0], nums[0] + n))
        nums = nums[n:]
    nc.all_engine_barrier()


def setup(nc, hidden, r):
    with ExitStack() as ctx:
        zeroed = ctx.enter_context(nc.semaphore("zeroed"))
        with nc.Block() as block:
            @block.sync
            def _(sp):
                sp.dma_start(r.x[:], hidden.rearrange("b (h p) d -> p (b h) d", p=P)).then_inc(r.x_loaded, 16)

            @block.gpsimd
            def _(pool):
                nc.gpsimd.memset(r.ident[:], 0.0)
                nc.gpsimd.memset(r.ident_bf[:], 0.0)
                nc.gpsimd.memset(r.ones_row[:], 1.0)
                nc.gpsimd.memset(r.causal_bf[:], 0.0).then_inc(zeroed, 1)
                pool.wait_ge(zeroed, 1)
                for m in (r.ident, r.ident_bf):
                    nc.gpsimd.affine_select(out=m[:], in_=m[:], compare_op=ALU.not_equal, fill=1.0, base=0,
                                            pattern=[[-1, P]], channel_multiplier=1)
                nc.gpsimd.affine_select(out=r.causal_bf[:], in_=r.causal_bf[:], compare_op=ALU.is_ge, fill=NEG,
                                        base=0, pattern=[[-1, P]], channel_multiplier=1)
        end_of_round(nc, [zeroed])


NH, NKV, HD = 16, 4, 128
REP = NH // NKV
QW = 3 * P


class Norm:

    def __init__(self, nc, sb):
        self.stats = sb("ln_stats", [P, GROUP_TILES, 6])
        self.mv = sb("ln_mv", [P, GROUP_TILES, 2])
        self.veps = sb("ln_veps", [P, GROUP_TILES])
        self.lnv = sb("ln_lnv", [P, GROUP_TILES])
        self.r0 = sb("ln_r0", [P, GROUP_TILES])
        self.t = sb("ln_t", [P, GROUP_TILES])
        self.xn = sb("ln_xn", [P, GROUP_TILES, HID])


def norm_vector(nc, dve, link, n, x_of, var_ready, r0_ready, xn_ready):
    for t in range(GROUP_TILES):
        last = nc.vector.bn_stats(n.stats[:, t, :], x_of(t))
    link(last)
    for t in range(GROUP_TILES):
        last = nc.vector.bn_aggr(n.mv[:, t, :], n.stats[:, t, :])
    link(last)
    nc.vector.tensor_scalar(n.veps[:], n.mv[:, :, 1], LN_EPS, None, ALU.add).then_inc(var_ready, 1)
    dve.wait_ge(r0_ready, 2)
    link(nc.vector.tensor_tensor(n.t[:], n.r0[:], n.r0[:], ALU.mult))
    link(nc.vector.tensor_tensor(n.t[:], n.t[:], n.veps[:], ALU.mult))
    link(nc.vector.tensor_scalar(n.t[:], n.t[:], -0.5, 1.5, ALU.mult, ALU.add))
    link(nc.vector.tensor_tensor(n.t[:], n.t[:], n.r0[:], ALU.mult))
    for t in range(GROUP_TILES):
        nc.vector.tensor_scalar(n.xn[:, t, :], x_of(t), n.mv[:, t, 0:1], n.t[:, t:t + 1],
                                ALU.subtract, ALU.mult).then_inc(xn_ready, 1)


def norm_scalar(nc, act, n, var_ready, r0_ready):
    act.wait_ge(var_ready, 1)
    nc.scalar.activation(n.lnv[:], n.veps[:], ACT.Ln).then_inc(r0_ready, 1)
    act.wait_ge(r0_ready, 1)
    nc.scalar.activation(n.r0[:], n.lnv[:], ACT.Exp, scale=-0.5).then_inc(r0_ready, 1)


def norm_tensor(nc, pe, n, ident, banks, xn_ready, xnT_ready):
    for t in range(GROUP_TILES):
        pe.wait_ge(xn_ready, t + 1)
        for c in range(DC):
            mm = nc.tensor.transpose(banks[c][:, t * P:(t + 1) * P], n.xn[:, t, c * P:(c + 1) * P], ident[:])
    mm.then_inc(xnT_ready, 1)


def attention(nc, r, w_q, w_k, w_v, w_o, b_o):
    with ExitStack() as ctx:
        def sb(name, shape, dt=F32):
            return ctx.enter_context(nc.sbuf_tensor("a_" + name, shape, dt))

        def sem(name):
            return ctx.enter_context(nc.semaphore("a_" + name))

        ps = ctx.enter_context(nc.psum_tensor("a_ps", [P, 8, 512], F32))
        PROJ, SC, PTB, OTB = (0, 1), (2, 3), (4, 5), (6, 7)

        n = Norm(nc, sb)
        wq = sb("wq", [P, DC, NH * HD])
        wk = sb("wk", [P, DC, NKV * HD])
        wv = sb("wv", [P, DC, NKV * HD])
        wo = sb("wo", [P, NH, HID])
        bo = sb("bo", [P, 1, HID])
        xnT = sb("xnT", [P, DC, GROUP])
        kT = sb("kT", [P, NKV, GROUP])
        v = sb("v", [P, GROUP_TILES, NKV * HD])
        qT = sb("qT", [P, 2, GROUP])
        negmax = sb("negmax", [P, 2, GROUP_TILES])
        rowsum = sb("rowsum", [P, 2, GROUP_TILES])
        inv = sb("inv", [P, 2, GROUP_TILES])
        probs = sb("probs", [P, 2, GROUP_BATCHES, QW])
        pT = sb("pT", [P, 2, GROUP_BATCHES, QW])
        oT = sb("oT", [P, NH, GROUP])

        w_loaded = [sem(f"w_loaded{i}") for i in range(5)]
        var_ready, r0_ready, xn_ready, xnT_ready, xnT_copied = [
            sem(s) for s in ("var_ready", "r0_ready", "xn_ready", "xnT_ready", "xnT_copied")]
        proj_ready, proj_taken = sem("proj_ready"), sem("proj_taken")
        scores_ready, max_ready, exp_ready, probs_ready = [
            sem(s) for s in ("scores_ready", "max_ready", "exp_ready", "probs_ready")]
        pT_ready, pT_copied, oT_ready, oT_copied = [
            sem(s) for s in ("pT_ready", "pT_copied", "oT_ready", "oT_copied")]
        bias_added, dve_done, out_added = sem("bias_added"), sem("dve_done"), sem("out_added")
        round_sems = [var_ready, r0_ready, xn_ready, xnT_ready, xnT_copied, proj_ready, proj_taken,
                      scores_ready, max_ready, exp_ready, probs_ready, pT_ready, pT_copied, oT_ready,
                      oT_copied, bias_added, dve_done, out_added]

        with nc.Block() as block:
            @block.sync
            def _(sp):
                sp.dma_start(wk[:], w_k.rearrange("(c p) n -> p c n", p=P)).then_inc(w_loaded[0], 16)
                sp.dma_start(wv[:], w_v.rearrange("(c p) n -> p c n", p=P)).then_inc(w_loaded[1], 16)
                sp.dma_start(wq[:], w_q.rearrange("(c p) n -> p c n", p=P)).then_inc(w_loaded[2], 16)
                sp.dma_start(bo[:, 0, :], b_o.rearrange("(a n) -> a n", a=1).to_broadcast([P, HID])
                             ).then_inc(w_loaded[4], 16)
                sp.dma_start(wo[:], w_o.rearrange("(h p) n -> p h n", p=P)).then_inc(w_loaded[3], 16)

        KV_JOBS = NKV + GROUP_TILES

        def chunk(b, half):
            t = 2 * b + half
            return slice(t * P, (t + 1) * P)

        with nc.Fori(0, GROUPS) as i:
            with nc.Block() as block:
                @block.vector
                def _(dve):
                    done = [0]

                    def link(ins):
                        done[0] += 1
                        ins.then_inc(dve_done, 1)
                        dve.wait_ge(dve_done, done[0])

                    x_tile = lambda t: r.x[:, bass.ds(i * GROUP_TILES + t, 1), :].rearrange("p a d -> p (a d)")
                    dve.wait_ge(r.x_loaded, 16)
                    norm_vector(nc, dve, link, n, x_tile, var_ready, r0_ready, xn_ready)

                    def maxima(h):
                        for b in range(GROUP_BATCHES):
                            dve.wait_ge(scores_ready, 2 * h + b + 1)
                            nc.vector.tensor_reduce(negmax[:, h % 2, 2 * b:2 * b + 1], ps[:, SC[b], 0:P],
                                                    AX_X, ALU.max, negate=True)
                            nc.vector.tensor_reduce(negmax[:, h % 2, 2 * b + 1:2 * b + 2], ps[:, SC[b], P:QW],
                                                    AX_X, ALU.max, negate=True).then_inc(max_ready, 1)

                    def copy_pT(h):
                        for b in range(GROUP_BATCHES):
                            dve.wait_ge(pT_ready, 2 * h + b + 1)
                            if h >= 2:
                                dve.wait_ge(oT_ready, h - 1)
                            nc.vector.tensor_copy(pT[:, h % 2, b, :], ps[:, PTB[b], 0:QW]).then_inc(pT_copied, 1)

                    def normalise(h):
                        dve.wait_ge(exp_ready, 2 * h + 2)
                        link(nc.vector.reciprocal(inv[:, h % 2, :], rowsum[:, h % 2, :]))
                        for b in range(GROUP_BATCHES):
                            nc.vector.tensor_scalar(probs[:, h % 2, b, 0:P], probs[:, h % 2, b, 0:P],
                                                    inv[:, h % 2, 2 * b:2 * b + 1], None, ALU.mult)
                            nc.vector.tensor_scalar(probs[:, h % 2, b, P:QW], probs[:, h % 2, b, P:QW],
                                                    inv[:, h % 2, 2 * b + 1:2 * b + 2], None,
                                                    ALU.mult).then_inc(probs_ready, 1)

                    for h in range(NH):
                        maxima(h)
                        if h >= 1:
                            copy_pT(h - 1)
                        normalise(h)
                    copy_pT(NH - 1)
                    dve.wait_ge(bias_added, 1)
                    for t in range(GROUP_TILES):
                        job = KV_JOBS + NH + t
                        dve.wait_ge(proj_ready, job + 1)
                        nc.vector.tensor_tensor(x_tile(t), x_tile(t), ps[:, PROJ[job % 2], 0:HID],
                                                ALU.add).then_inc(proj_taken, 1)

                @block.gpsimd
                def _(pool):
                    pool.wait_ge(xn_ready, GROUP_TILES)
                    pool.wait_ge(w_loaded[4], 16)
                    xg = r.x[:, bass.ds(i * GROUP_TILES, GROUP_TILES), :]
                    nc.gpsimd.tensor_tensor(xg, xg, bo[:].to_broadcast([P, GROUP_TILES, HID]),
                                            ALU.add).then_inc(bias_added, 1)

                @block.scalar
                def _(act):
                    norm_scalar(nc, act, n, var_ready, r0_ready)
                    act.wait_ge(xnT_ready, 1)
                    for c in range(DC):
                        nc.scalar.copy(xnT[:, c, :], ps[:, OTB[c], :]).then_inc(xnT_copied, 1)

                    def take(job, dst):
                        act.wait_ge(proj_ready, job + 1)
                        nc.scalar.copy(dst, ps[:, PROJ[job % 2], :]).then_inc(proj_taken, 1)

                    for g in range(NKV):
                        take(g, kT[:, g, :])
                    for t in range(GROUP_TILES):
                        take(NKV + t, v[:, t, :])
                    take(KV_JOBS, qT[:, 0, :])

                    def exps(h):
                        if h >= 2:
                            act.wait_ge(pT_ready, 2 * (h - 1))
                        for b in range(GROUP_BATCHES):
                            act.wait_ge(max_ready, 2 * h + b + 1)
                            nc.scalar.activation(probs[:, h % 2, b, 0:P], ps[:, SC[b], 0:P], ACT.Exp,
                                                 bias=negmax[:, h % 2, 2 * b:2 * b + 1],
                                                 accum_out=rowsum[:, h % 2, 2 * b:2 * b + 1])
                            nc.scalar.activation(probs[:, h % 2, b, P:QW], ps[:, SC[b], P:QW], ACT.Exp,
                                                 bias=negmax[:, h % 2, 2 * b + 1:2 * b + 2],
                                                 accum_out=rowsum[:, h % 2, 2 * b + 1:2 * b + 2]
                                                 ).then_inc(exp_ready, 1)

                    def copy_oT(h):
                        act.wait_ge(oT_ready, h + 1)
                        nc.scalar.copy(oT[:, h, :], ps[:, OTB[h % 2], :]).then_inc(oT_copied, 1)

                    for h in range(NH):
                        exps(h)
                        if h + 1 < NH:
                            take(KV_JOBS + h + 1, qT[:, (h + 1) % 2, :])
                        if h >= 1:
                            copy_oT(h - 1)
                    copy_oT(NH - 1)

                @block.tensor
                def _(pe):
                    norm_tensor(nc, pe, n, r.ident, [ps[:, OTB[0], :], ps[:, OTB[1], :]], xn_ready, xnT_ready)

                    def bank_free(job):
                        if job >= 2:
                            pe.wait_ge(proj_taken, job - 1)

                    def project(job, w, cols):
                        bank_free(job)
                        for c in range(DC):
                            mm = nc.tensor.matmul(ps[:, PROJ[job % 2], :], w[:, c, cols], xnT[:, c, :],
                                                  start=(c == 0), stop=(c == DC - 1))
                        mm.then_inc(proj_ready, 1)

                    pe.wait_ge(xnT_copied, DC)
                    pe.wait_ge(w_loaded[0], 16)
                    for g in range(NKV):
                        project(g, wk, slice(g * HD, (g + 1) * HD))
                    pe.wait_ge(w_loaded[1], 16)
                    for t in range(GROUP_TILES):
                        bank_free(NKV + t)
                        for c in range(DC):
                            mm = nc.tensor.matmul(ps[:, PROJ[(NKV + t) % 2], :], xnT[:, c, t * P:(t + 1) * P],
                                                  wv[:, c, :], start=(c == 0), stop=(c == DC - 1))
                        mm.then_inc(proj_ready, 1)
                    pe.wait_ge(w_loaded[2], 16)

                    def queries(h):
                        project(KV_JOBS + h, wq, slice(h * HD, (h + 1) * HD))

                    def scores(h):
                        pe.wait_ge(proj_taken, KV_JOBS + h + 1)
                        for b in range(GROUP_BATCHES):
                            if h >= 1:
                                pe.wait_ge(exp_ready, 2 * (h - 1) + b + 1)
                            q, k = qT[:, h % 2, :], kT[:, h // REP, :]
                            nc.tensor.matmul(ps[:, SC[b], 0:P], q[:, chunk(b, 0)], k[:, chunk(b, 0)],
                                             start=True, stop=False)
                            nc.tensor.matmul(ps[:, SC[b], 0:P], r.ident_bf[:], r.causal_bf[:],
                                             start=False, stop=True)
                            nc.tensor.matmul(ps[:, SC[b], P:QW], q[:, chunk(b, 1)],
                                             k[:, 2 * b * P:(2 * b + 2) * P], start=True, stop=False)
                            nc.tensor.matmul(ps[:, SC[b], 2 * P:QW], r.ident_bf[:], r.causal_bf[:],
                                             start=False, stop=True).then_inc(scores_ready, 1)

                    def turn(h):
                        for b in range(GROUP_BATCHES):
                            pe.wait_ge(probs_ready, 2 * h + b + 1)
                            if h >= 1:
                                pe.wait_ge(pT_copied, 2 * (h - 1) + b + 1)
                            for s in range(3):
                                mm = nc.tensor.transpose(ps[:, PTB[b], s * P:(s + 1) * P],
                                                         probs[:, h % 2, b, s * P:(s + 1) * P], r.ident[:])
                            mm.then_inc(pT_ready, 1)

                    def values(h):
                        if h >= 2:
                            pe.wait_ge(oT_copied, h - 1)
                        g = slice((h // REP) * HD, (h // REP + 1) * HD)
                        for b in range(GROUP_BATCHES):
                            pe.wait_ge(pT_copied, 2 * h + b + 1)
                            out = ps[:, OTB[h % 2], 2 * b * P:(2 * b + 2) * P]
                            nc.tensor.matmul(out, v[:, 2 * b, g], pT[:, h % 2, b, 0:2 * P], start=True, stop=False)
                            mm = nc.tensor.matmul(out[:, P:2 * P], v[:, 2 * b + 1, g], pT[:, h % 2, b, 2 * P:QW],
                                                  start=False, stop=True)
                        mm.then_inc(oT_ready, 1)

                    queries(0)
                    scores(0)
                    queries(1)
                    for h in range(1, NH):
                        scores(h)
                        turn(h - 1)
                        if h + 1 < NH:
                            queries(h + 1)
                        values(h - 1)
                    turn(NH - 1)
                    values(NH - 1)
                    pe.wait_ge(oT_copied, NH)
                    pe.wait_ge(w_loaded[3], 16)
                    for t in range(GROUP_TILES):
                        job = KV_JOBS + NH + t
                        bank_free(job)
                        for h in range(NH):
                            mm = nc.tensor.matmul(ps[:, PROJ[job % 2], 0:HID], oT[:, h, t * P:(t + 1) * P],
                                                  wo[:, h, :], start=(h == 0), stop=(h == NH - 1))
                        mm.then_inc(proj_ready, 1)
            end_of_round(nc, round_sems)
        end_of_round(nc, w_loaded)


NE, FE, RANK, NLORA = 8, 256, 64, 2
FC = FE // P
GOLDEN_CENTER = 1.0 / math.e
GOLDEN_LOWER = 0.5 - math.log(4.0 / 3.0)
ZONE_LOW = math.log(GOLDEN_LOWER / (1.0 - GOLDEN_LOWER))
ZONE_HIGH = 1e-7
F32R = mybir.dt.float32r


def experts(nc, r, Wg, Wu, Wd, Ga, Gb, Ua, Ub, Da, Db, Wr, temperature):
    with ExitStack() as ctx:
        def sb(name, shape, dt=F32):
            return ctx.enter_context(nc.sbuf_tensor("b_" + name, shape, dt))

        def sem(name):
            return ctx.enter_context(nc.semaphore("b_" + name))

        ps = ctx.enter_context(nc.psum_tensor("b_ps", [P, 8, 512], F32))
        GATE, UP, DOWN = (0, 1), (2, 3), (4, 5, 6, 7)

        n = Norm(nc, sb)
        raw = sb("raw", [P, 2, NE, DC, FE])
        high = sb("high", [P, 2, NE, DC, FE], F32R)
        low = sb("low", [P, 2, NE, DC, FE], F32R)
        wd = sb("wd", [P, NE, FC, HID])
        lora_a = sb("lora_a", [RANK, 3, NLORA, FE])
        lora_b = sb("lora_b", [RANK, 3, NLORA, FE])
        wr = sb("wr", [P, DC, NE])
        temp = sb("temp", [P, 1])
        inv_temp = sb("inv_temp", [P, 1])
        rank_of = sb("rank_of", [P, NE])
        xnT = sb("xnT", [P, DC, GROUP])
        xnT_high = sb("xnT_high", [P, DC, GROUP], F32R)
        xnT_low = sb("xnT_low", [P, DC, GROUP], F32R)
        silu = sb("silu", [P, FC, GROUP])
        mid = sb("mid", [P, 2, FC, GROUP])
        TE = [P, GROUP_TILES, NE]
        z, zone, ez, dist, zw, fb = [sb(s, TE) for s in ("z", "zone", "ez", "dist", "zw", "fb")]
        eq, key, first, second, rest, w = [sb(s, TE) for s in ("eq", "key", "first", "second", "rest", "w")]
        top, best, total, none = [sb(s, [P, GROUP_TILES, 1]) for s in ("top", "best", "total", "none")]

        loaded = [sem(f"loaded{i}") for i in range(5)]
        lora_ready, lora_taken, split_done, setup_done = [
            sem(s) for s in ("lora_ready", "lora_taken", "split_done", "setup_done")]
        var_ready, r0_ready, xn_ready, xnT_ready, xnT_copied = [
            sem(s) for s in ("var_ready", "r0_ready", "xn_ready", "xnT_ready", "xnT_copied")]
        low_ready, logits_ready, z_ready, ez_ready, dist_ready, exps_ready = [
            sem(s) for s in ("low_ready", "logits_ready", "z_ready", "ez_ready", "dist_ready", "exps_ready")]
        gate_ready, up_ready, silu_ready, mid_ready, down_ready, added, dve_done = [
            sem(s) for s in ("gate_ready", "up_ready", "silu_ready", "mid_ready", "down_ready", "added", "dve_done")]
        round_sems = [var_ready, r0_ready, xn_ready, xnT_ready, xnT_copied, low_ready, logits_ready, z_ready,
                      ez_ready, dist_ready, exps_ready, gate_ready, up_ready, silu_ready, mid_ready, down_ready,
                      added, dve_done]

        with nc.Block() as block:
            @block.sync
            def _(sp):
                for k, (a, b) in enumerate(((Ga, Gb), (Ua, Ub), (Da, Db))):
                    sp.dma_start(lora_a[:, k], a.rearrange("l r d -> r l d")).then_inc(loaded[0], 16)
                    sp.dma_start(lora_b[:, k], b.rearrange("l r f -> r l f")).then_inc(loaded[0], 16)
                sp.dma_start(temp[:], temperature.rearrange("(a n) -> a n", a=1).to_broadcast([P, 1])
                             ).then_inc(loaded[0], 16)
                sp.dma_start(wr[:], Wr.rearrange("(c p) e -> p c e", p=P)).then_inc(loaded[0], 16)
                for k, src in enumerate((Wg, Wu)):
                    sp.dma_start(raw[:, k], src.rearrange("e (c p) f -> p e c f", p=P)).then_inc(loaded[1 + k], 16)
                sp.dma_start(wd[:], Wd.rearrange("e (c p) f -> p e c f", p=P)).then_inc(loaded[3], 16)

            @block.gpsimd
            def _(pool):
                nc.gpsimd.iota(rank_of[:], pattern=[[-1, NE]], base=NE, channel_multiplier=0,
                               allow_small_or_imprecise_dtypes=True).then_inc(setup_done, 1)

            @block.tensor
            def _(pe):
                pe.wait_ge(loaded[0], 16 * 8)
                for k in range(3):
                    for e in range(NLORA):
                        job = k * NLORA + e
                        for c in range(DC):
                            mm = nc.tensor.matmul(ps[:, job, c * FE:(c + 1) * FE],
                                                  lora_a[:, k, e, c * P:(c + 1) * P], lora_b[:, k, e, :],
                                                  start=True, stop=True)
                        mm.then_inc(lora_ready, 1)

            @block.vector
            def _(dve):
                dve.wait_ge(loaded[0], 16 * 8)
                nc.vector.reciprocal(inv_temp[:], temp[:]).then_inc(setup_done, 1)
                for k in range(3):
                    dve.wait_ge(loaded[1 + k], 16)
                    for e in range(NLORA):
                        job = k * NLORA + e
                        dve.wait_ge(lora_ready, job + 1)
                        dst = (raw[:, k, e] if k < 2 else wd[:, e]).rearrange("p c f -> p (c f)")
                        nc.vector.tensor_tensor(dst, dst, ps[:, job, :], ALU.add).then_inc(lora_taken, 1)
                    if k < 2:
                        for e in range(NE):
                            dve.wait_ge(split_done, k * NE + e + 1)
                            nc.vector.tensor_tensor(low[:, k, e], raw[:, k, e], high[:, k, e].bitcast(F32),
                                                    ALU.subtract)

            @block.scalar
            def _(act):
                for k in range(2):
                    act.wait_ge(loaded[1 + k], 16)
                    act.wait_ge(lora_taken, NLORA * (k + 1))
                    for e in range(NE):
                        nc.scalar.copy(high[:, k, e], raw[:, k, e]).then_inc(split_done, 1)

        with nc.Fori(0, GROUPS) as i:
            with nc.Block() as block:
                @block.vector
                def _(dve):
                    done = [0]

                    def link(ins):
                        done[0] += 1
                        ins.then_inc(dve_done, 1)
                        dve.wait_ge(dve_done, done[0])

                    x_tile = lambda t: r.x[:, bass.ds(i * GROUP_TILES + t, 1), :].rearrange("p a d -> p (a d)")
                    norm_vector(nc, dve, link, n, x_tile, var_ready, r0_ready, xn_ready)
                    for c in range(DC):
                        dve.wait_ge(xnT_copied, 2 * (c + 1))
                        nc.vector.tensor_tensor(xnT_low[:, c, :], ps[:, DOWN[c], :],
                                                xnT_high[:, c, :].bitcast(F32), ALU.subtract).then_inc(low_ready, 1)

                    def mids(e):
                        for m in range(FC):
                            dve.wait_ge(silu_ready, FC * e + m + 1)
                            dve.wait_ge(up_ready, FC * e + m + 1)
                            if e >= 2:
                                dve.wait_ge(down_ready, GROUP_TILES * (e - 1))
                            nc.vector.tensor_tensor(mid[:, e % 2, m, :], silu[:, m, :], ps[:, UP[m], :],
                                                    ALU.mult).then_inc(mid_ready, 1)

                    def add(e):
                        for t in range(GROUP_TILES):
                            dve.wait_ge(down_ready, GROUP_TILES * e + t + 1)
                            if e >= 1:
                                dve.wait_ge(added, GROUP_TILES * (e - 1) + t + 1)
                            nc.vector.scalar_tensor_tensor(x_tile(t), ps[:, DOWN[t], 0:HID], w[:, t, e:e + 1],
                                                           x_tile(t), ALU.mult, ALU.add).then_inc(added, 1)

                    def over_experts(a):
                        return a[:].to_broadcast(TE)

                    def router():
                        dve.wait_ge(logits_ready, 1)
                        link(nc.vector.tensor_scalar(z[:].rearrange("p t e -> p (t e)"),
                                                     ps[:, DOWN[2], 0:GROUP_TILES * NE], inv_temp[:, 0:1], None,
                                                     ALU.mult))
                        nc.vector.tensor_scalar(zone[:], z[:], ZONE_LOW, None, ALU.is_ge).then_inc(z_ready, 1)
                        link(nc.vector.tensor_scalar(eq[:], z[:], ZONE_HIGH, None, ALU.is_le))
                        link(nc.vector.tensor_tensor(zone[:], zone[:], eq[:], ALU.mult))
                        dve.wait_ge(ez_ready, 1)
                        link(nc.vector.tensor_scalar(ez[:], ez[:], 1.0, None, ALU.add))
                        link(nc.vector.reciprocal(ez[:], ez[:]))
                        link(nc.vector.tensor_scalar(ez[:], ez[:], -GOLDEN_CENTER, None, ALU.add))
                        nc.vector.scalar_tensor_tensor(dist[:], ez[:], -1.0, ez[:], ALU.mult, ALU.max).then_inc(dist_ready, 1)
                        dve.wait_ge(exps_ready, 2)
                        link(nc.vector.tensor_tensor(zw[:], zw[:], zone[:], ALU.mult))
                        link(nc.vector.reduce_sum(total[:], zw[:], AX_X))
                        link(nc.vector.tensor_scalar(none[:], total[:], 1e-8, None, ALU.is_lt))

                        def pick(values, chosen):
                            link(nc.vector.reduce_max(top[:], values[:], AX_X))
                            link(nc.vector.tensor_tensor(eq[:], values[:], over_experts(top), ALU.is_equal))
                            link(nc.vector.tensor_tensor(
                                key[:], eq[:], rank_of[:].rearrange("p (a e) -> p a e", a=1).to_broadcast(TE),
                                ALU.mult))
                            link(nc.vector.reduce_max(best[:], key[:], AX_X))
                            link(nc.vector.tensor_tensor(chosen[:], key[:], over_experts(best), ALU.is_equal))

                        pick(fb, first)
                        link(nc.vector.scalar_tensor_tensor(rest[:], first[:], -4.0, fb[:], ALU.mult, ALU.add))
                        pick(rest, second)
                        link(nc.vector.tensor_tensor(first[:], first[:], second[:], ALU.add))
                        link(nc.vector.tensor_tensor(fb[:], fb[:], first[:], ALU.mult))

                        def normalised(a):
                            link(nc.vector.reduce_sum(total[:], a[:], AX_X))
                            link(nc.vector.tensor_scalar(total[:], total[:], 1e-8, None, ALU.max))
                            link(nc.vector.reciprocal(best[:], total[:]))
                            link(nc.vector.tensor_tensor(a[:], a[:], over_experts(best), ALU.mult))

                        normalised(fb)
                        link(nc.vector.tensor_tensor(fb[:], fb[:], zw[:], ALU.subtract))
                        link(nc.vector.tensor_tensor(fb[:], fb[:], over_experts(none), ALU.mult))
                        link(nc.vector.tensor_tensor(w[:], zw[:], fb[:], ALU.add))
                        normalised(w)

                    router()
                    mids(0)
                    for e in range(1, NE):
                        mids(e)
                        add(e - 1)
                    add(NE - 1)

                @block.scalar
                def _(act):
                    norm_scalar(nc, act, n, var_ready, r0_ready)
                    act.wait_ge(xnT_ready, 1)
                    for c in range(DC):
                        nc.scalar.copy(xnT_high[:, c, :], ps[:, DOWN[c], :]).then_inc(xnT_copied, 1)
                        nc.scalar.copy(xnT[:, c, :], ps[:, DOWN[c], :]).then_inc(xnT_copied, 1)
                    act.wait_ge(z_ready, 1)
                    nc.scalar.activation(ez[:], z[:], ACT.Exp, scale=-1.0).then_inc(ez_ready, 1)
                    act.wait_ge(dist_ready, 1)
                    nc.scalar.activation(zw[:], dist[:], ACT.Exp, scale=-1.0 / 0.1).then_inc(exps_ready, 1)
                    nc.scalar.activation(fb[:], dist[:], ACT.Exp, scale=-1.0 / 0.3).then_inc(exps_ready, 1)
                    for e in range(NE):
                        for m in range(FC):
                            act.wait_ge(gate_ready, FC * e + m + 1)
                            if e >= 1:
                                act.wait_ge(mid_ready, FC * (e - 1) + m + 1)
                            nc.scalar.activation(silu[:, m, :], ps[:, GATE[m], :], ACT.Silu).then_inc(silu_ready, 1)

                @block.tensor
                def _(pe):
                    norm_tensor(nc, pe, n, r.ident, [ps[:, DOWN[0], :], ps[:, DOWN[1], :]], xn_ready, xnT_ready)
                    pe.wait_ge(xnT_copied, 2 * DC)
                    for t in range(GROUP_TILES):
                        for c in range(DC):
                            mm = nc.tensor.matmul(ps[:, DOWN[2], t * NE:(t + 1) * NE], xnT[:, c, t * P:(t + 1) * P],
                                                  wr[:, c, :], start=(c == 0), stop=(c == DC - 1))
                    mm.then_inc(logits_ready, 1)

                    def hidden_product(bank, k, e, m, ready):
                        cols = slice(m * P, (m + 1) * P)
                        passes = [(wpart, xpart, c) for c in range(DC)
                                  for wpart, xpart in ((high, xnT_high), (high, xnT_low), (low, xnT_high))]
                        for j, (wpart, xpart, c) in enumerate(passes):
                            mm = nc.tensor.matmul(ps[:, bank, :], wpart[:, k, e, c, cols], xpart[:, c, :],
                                                  start=(j == 0), stop=(j == len(passes) - 1))
                        mm.then_inc(ready, 1)

                    def gate_up(e):
                        for m in range(FC):
                            if e >= 1:
                                pe.wait_ge(silu_ready, FC * (e - 1) + m + 1)
                            hidden_product(GATE[m], 0, e, m, gate_ready)
                            if e >= 1:
                                pe.wait_ge(mid_ready, FC * (e - 1) + m + 1)
                            hidden_product(UP[m], 1, e, m, up_ready)

                    def down(e):
                        pe.wait_ge(mid_ready, FC * (e + 1))
                        for t in range(GROUP_TILES):
                            if e >= 1:
                                pe.wait_ge(added, GROUP_TILES * (e - 1) + t + 1)
                            for m in range(FC):
                                mm = nc.tensor.matmul(ps[:, DOWN[t], 0:HID], mid[:, e % 2, m, t * P:(t + 1) * P],
                                                      wd[:, e, m, :], start=(m == 0), stop=(m == FC - 1))
                            mm.then_inc(down_ready, 1)

                    pe.wait_ge(low_ready, DC)
                    gate_up(0)
                    for e in range(1, NE):
                        gate_up(e)
                        down(e - 1)
                    down(NE - 1)
            end_of_round(nc, round_sems)
        end_of_round(nc, loaded + [lora_ready, lora_taken, split_done, setup_done])


DH, DK, DV = 6, 32, 64
KEYS, VALS = DH * DK, DH * DV
TAPS = 4
SUB = 16
BLOCKS = P // SUB
HALVES = SEQ // P
UNITS = DH * HALVES
SET0 = 4 * DV
GATES = VALS + 2 * DH
RMS_EPS = 1e-5
JOBS = ((0, P), (KEYS, P), (P, KEYS - P), (KEYS + P, KEYS - P),
        (2 * KEYS, P), (2 * KEYS + P, P), (2 * KEYS + 2 * P, P))
QK_JOBS = 4
ATANH_TERMS = 8


class NormAll:

    RING = 4

    def __init__(self, nc, ctx, prefix, ps):
        def sb(name, shape):
            return ctx.enter_context(nc.sbuf_tensor(prefix + name, shape, F32))

        self.nc, self.ps = nc, ps
        self.stats = sb("ln_stats", [P, TILES, 6])
        self.mv = sb("ln_mv", [P, TILES, 2])
        self.veps = sb("ln_veps", [P, TILES])
        self.lnv = sb("ln_lnv", [P, TILES])
        self.r0 = sb("ln_r0", [P, TILES])
        self.t = sb("ln_t", [P, TILES])
        self.xn = sb("ln_xn", [P, self.RING, HID])
        self.sems = [
            ctx.enter_context(nc.semaphore(prefix + s)) for s in
            ("ln_chained", "ln_var_ready", "ln_r0_ready", "ln_xn_ready", "ln_turned", "ln_copied")]
        self.chained, self.var_ready, self.r0_ready, self.xn_ready, self.turned, self.copied = self.sems

    def vector(self, dve, x):
        nc = self.nc
        for t in range(TILES):
            last = nc.vector.bn_stats(self.stats[:, t, :], x[:, t, :])
        last.then_inc(self.chained, 1)
        dve.wait_ge(self.chained, 1)
        for t in range(TILES):
            last = nc.vector.bn_aggr(self.mv[:, t, :], self.stats[:, t, :])
        last.then_inc(self.chained, 1)
        dve.wait_ge(self.chained, 2)
        nc.vector.tensor_scalar(self.veps[:], self.mv[:, :, 1], LN_EPS, None, ALU.add).then_inc(self.var_ready, 1)
        dve.wait_ge(self.r0_ready, 2)
        nc.vector.tensor_tensor(self.t[:], self.r0[:], self.r0[:], ALU.mult).then_inc(self.chained, 1)
        dve.wait_ge(self.chained, 3)
        nc.vector.tensor_tensor(self.t[:], self.t[:], self.veps[:], ALU.mult).then_inc(self.chained, 1)
        dve.wait_ge(self.chained, 4)
        nc.vector.tensor_scalar(self.t[:], self.t[:], -0.5, 1.5, ALU.mult, ALU.add).then_inc(self.chained, 1)
        dve.wait_ge(self.chained, 5)
        nc.vector.tensor_tensor(self.t[:], self.t[:], self.r0[:], ALU.mult).then_inc(self.chained, 1)
        dve.wait_ge(self.chained, 6)
        for t in range(TILES):
            if t >= self.RING:
                dve.wait_ge(self.turned, t - self.RING + 1)
            nc.vector.tensor_scalar(self.xn[:, t % self.RING, :], x[:, t, :], self.mv[:, t, 0:1], self.t[:, t:t + 1],
                                    ALU.subtract, ALU.mult).then_inc(self.xn_ready, 1)

    def scalar_root(self, act):
        nc = self.nc
        nc.scalar.preload_act_table_set("natural_log_exp_and_others")
        act.wait_ge(self.var_ready, 1)
        nc.scalar.activation(self.lnv[:], self.veps[:], ACT.Ln).then_inc(self.r0_ready, 1)
        act.wait_ge(self.r0_ready, 1)
        nc.scalar.activation(self.r0[:], self.lnv[:], ACT.Exp, scale=-0.5).then_inc(self.r0_ready, 1)

    def bank(self, g, c):
        return (g % 2) * DC + c

    def tensor(self, pe, ident, g):
        nc = self.nc
        if g >= 2:
            pe.wait_ge(self.copied, DC * (g - 1))
        for t in range(g * GROUP_TILES, (g + 1) * GROUP_TILES):
            pe.wait_ge(self.xn_ready, t + 1)
            for c in range(DC):
                at = (t % GROUP_TILES) * P
                mm = nc.tensor.transpose(self.ps[:, self.bank(g, c), at:at + P],
                                         self.xn[:, t % self.RING, c * P:(c + 1) * P], ident[:])
            mm.then_inc(self.turned, 1)


def delta(nc, r, w_q, w_k, w_v, w_a, w_b, w_g, w_o, conv_q, conv_k, conv_v, a_log, dt_bias, norm_weight):
    with ExitStack() as ctx:
        def sb(name, shape, dt=F32):
            return ctx.enter_context(nc.sbuf_tensor("c_" + name, shape, dt))

        def sem(name):
            return ctx.enter_context(nc.semaphore("c_" + name))

        ps = ctx.enter_context(nc.psum_tensor("c_ps", [P, 8, 512], F32))
        win = sb("win", [P, DC, 2 * KEYS + VALS])
        wgate = sb("wgate", [P, DC, VALS])
        wab = sb("wab", [P, DC, 2 * DH])
        wo = sb("wo", [P, VALS // P, HID])
        taps = sb("taps", [P, len(JOBS), TAPS])
        dtb = sb("dtb", [P, 1, DH])
        neg_rate = sb("neg_rate", [P, 1, DH])
        normw = sb("normw", [P, 1, DV])
        blocks = sb("blocks", [P, BLOCKS])
        even_neg, odd_neg = sb("even_neg", [P, 1]), sb("odd_neg", [P, 1])
        off_blocks = sb("off_blocks", [P, 1, P])
        head_ones = sb("head_ones", [P, P])
        own = sb("own", [P, DH, DV])
        ident2 = sb("ident2", [P, HALVES, P])
        urep = sb("urep", [P, SUB, UNITS, SUB])
        inv = sb("inv", [P, UNITS, SUB + 1])
        xnT = sb("xnT", [P, DC, TOKENS])
        beta = sb("beta", [P, TILES, DH])
        a_dram = nc.dram_tensor("a_scratch", [BATCH, DH * SEQ], F32).ap()
        g_dram = nc.dram_tensor("g_scratch", [BATCH, DH * P], F32).ap()
        state = sb("state", [P, VALS])
        chan = sb("chan", [P, len(JOBS), SEQ])
        square = sb("square", [P, QK_JOBS, SEQ])
        a_all = sb("a_all", [P, DH, SEQ])
        kq = sb("kq", [P, 2, 2, SEQ])
        g_all = sb("g_all", [P, 2, P])

        loaded, masks = sem("loaded"), sem("masks")

        with nc.Block() as block:
            @block.sync
            def _(sp):
                def row(a, m):
                    return a.rearrange("(a n) -> a n", a=1).to_broadcast([P, m])

                loads = [(wab[:, :, 0:DH], w_a.rearrange("(c p) n -> p c n", p=P)),
                         (wab[:, :, DH:], w_b.rearrange("(c p) n -> p c n", p=P)),
                         (dtb[:, 0, :], row(dt_bias, DH)), (neg_rate[:, 0, :], row(a_log, DH)),
                         (normw[:, 0, :], row(norm_weight, DV)),
                         (win[:, :, 0:KEYS], w_q.rearrange("(c p) n -> p c n", p=P)),
                         (win[:, :, KEYS:2 * KEYS], w_k.rearrange("(c p) n -> p c n", p=P)),
                         (win[:, :, 2 * KEYS:], w_v.rearrange("(c p) n -> p c n", p=P)),
                         (wgate[:], w_g.rearrange("(c p) n -> p c n", p=P)),
                         (wo[:], w_o.rearrange("(c p) n -> p c n", p=P)),
                         (taps[:, 0, :], conv_q[0:P, :]), (taps[:, 1, :], conv_k[0:P, :]),
                         (taps[0:KEYS - P, 2, :], conv_q[P:KEYS, :]), (taps[0:KEYS - P, 3, :], conv_k[P:KEYS, :]),
                         (taps[:, QK_JOBS:, :], conv_v.rearrange("(j p) n -> p j n", p=P))]
                for dst, src in loads:
                    sp.dma_start(dst, src).then_inc(loaded, 16)
                assert len(loads) == LOADS

            @block.gpsimd
            def _(pool):
                nc.gpsimd.memset(blocks[:], 1.0)
                nc.gpsimd.memset(head_ones[:], 1.0)
                nc.gpsimd.memset(kq[:], 0.0)
                nc.gpsimd.memset(g_all[:], 0.0)
                nc.gpsimd.memset(state[:], 0.0)
                nc.gpsimd.memset(inv[:, :, 0:1], 1.0).then_inc(masks, 1)
                pool.wait_ge(masks, 1)
                nc.gpsimd.affine_select(out=blocks[:], in_=blocks[:], compare_op=ALU.is_ge, fill=0.0, base=0,
                                        pattern=[[-SUB, BLOCKS]], channel_multiplier=1)
                nc.gpsimd.affine_select(out=head_ones[:], in_=head_ones[:], compare_op=ALU.is_ge, fill=0.0, base=0,
                                        pattern=[[-DK, P // DK], [0, DK]], channel_multiplier=1).then_inc(masks, 1)
                pool.wait_ge(masks, 2)
                nc.gpsimd.affine_select(out=blocks[:], in_=blocks[:], compare_op=ALU.is_ge, fill=0.0, base=SUB - 1,
                                        pattern=[[SUB, BLOCKS]], channel_multiplier=-1)
                nc.gpsimd.affine_select(out=head_ones[:], in_=head_ones[:], compare_op=ALU.is_ge, fill=0.0,
                                        base=DK - 1, pattern=[[DK, P // DK], [0, DK]],
                                        channel_multiplier=-1).then_inc(masks, 1)

        decays(nc, r, ps, win, taps, chan, square, a_all, g_all, xnT, wab, dtb, neg_rate, beta, a_dram, g_dram, loaded, masks,
               (blocks, even_neg, odd_neg, off_blocks, head_ones, own, ident2, urep, inv))
        batches(nc, r, ps, win, wgate, wo, taps, normw, blocks, even_neg, odd_neg, off_blocks, head_ones, own,
                ident2, urep, inv, xnT, beta, a_dram, g_dram, state, chan, square, kq, a_all, g_all)


def spread_decays(nc, sp, a_dram, g_dram, a_all, g_all, batch, signal):
    sp.dma_start(a_all[:].rearrange("p h t -> p (h t)"), a_dram[batch].to_broadcast([P, DH * SEQ])
                 ).then_inc(signal, 16)
    for h in range(DH):
        rows = slice((h % 4) * DK, (h % 4 + 1) * DK)
        cols = slice(h * P, (h + 1) * P)
        sp.dma_start(g_all[rows, h // 4, :], g_dram[batch, cols].to_broadcast([DK, P])).then_inc(signal, 16)


SPREADS = 16 * (1 + DH)


class Channels:

    def __init__(self, nc, sems, ps, banks, win, taps, chan, square, xnT):
        self.nc, self.S, self.ps, self.banks = nc, sems, ps, banks
        self.win, self.taps, self.chan, self.square, self.xnT = win, taps, chan, square, xnT

    NAMES = "tap_ready job_ready conv_step silu_done square_ready"

    def place(self, j):
        at = (j % 2) * SEQ
        return self.ps[0:JOBS[j][1], self.banks[j // 2], at:at + SEQ]

    def through(self, j):
        return min(j // 2 * 2 + 2, len(JOBS))

    def job(self, pe, j, tokens):
        nc, S = self.nc, self.S
        col, m = JOBS[j]
        if self.banks[j // 2] in self.banks[0:j // 2]:
            pe.wait_ge(S["conv_step"], (TAPS - 1) * 2 * (self.banks.index(self.banks[j // 2]) + 1))
        for c in range(DC):
            mm = nc.tensor.matmul(self.place(j), self.win[:, c, col:col + m], self.xnT[:, c, tokens],
                                  start=(c == 0), stop=(c == DC - 1))
        mm.then_inc(S["job_ready"], 1)

    def tap(self, act, j):
        m = JOBS[j][1]
        act.wait_ge(self.S["job_ready"], self.through(j))
        self.nc.scalar.activation(self.chan[0:m, j, :], self.place(j), ACT.Copy,
                                  scale=self.taps[0:m, j, TAPS - 1:TAPS]).then_inc(self.S["tap_ready"], 1)

    def conv(self, dve, q):
        j, k = q // (TAPS - 1), 1 + q % (TAPS - 1)
        m = JOBS[j][1]
        if k == 1:
            dve.wait_ge(self.S["tap_ready"], self.through(j))
        else:
            dve.wait_ge(self.S["conv_step"], q)
        self.nc.vector.scalar_tensor_tensor(self.chan[0:m, j, k:], self.place(j)[:, 0:SEQ - k],
                                            self.taps[0:m, j, TAPS - 1 - k:TAPS - k], self.chan[0:m, j, k:],
                                            ALU.mult, ALU.add).then_inc(self.S["conv_step"], 1)

    def silu(self, act, j):
        m = JOBS[j][1]
        act.wait_ge(self.S["conv_step"], (TAPS - 1) * (j + 1))
        self.nc.scalar.activation(self.chan[0:m, j, :], self.chan[0:m, j, :], ACT.Silu
                                  ).then_inc(self.S["silu_done"], 1)

    def squares(self, pool, j):
        m = JOBS[j][1]
        pool.wait_ge(self.S["silu_done"], j + 1)
        self.nc.gpsimd.tensor_tensor(self.square[0:m, j, :], self.chan[0:m, j, :], self.chan[0:m, j, :], ALU.mult
                                     ).then_inc(self.S["square_ready"], 1)


LOADS = 15


def decays(nc, r, ps, win, taps, chan, square, a_all, g_all, xnT, wab, dtb, neg_rate, beta_all, a_dram, g_dram, loaded, masks, consts):
    blocks, even_neg, odd_neg, off_blocks, head_ones, own, ident2, urep, inv = consts
    with ExitStack() as ctx:
        def sb(name, shape, dt=F32):
            return ctx.enter_context(nc.sbuf_tensor("cd_" + name, shape, dt))

        def sem(name):
            return ctx.enter_context(nc.semaphore("cd_" + name))

        n = NormAll(nc, ctx, "cd_", ps)
        TH = [P, TILES, DH]
        ab = sb("ab", [P, TILES, 2 * DH])
        u, s, s2, poly, decay = [sb(x, TH) for x in ("u", "s", "s2", "poly", "decay")]
        aT = sb("aT", [DH, TILES, P])
        gT = sb("gT", [DH, BATCH, P])
        zeros_row = sb("zeros_row", [DH, P])
        mine = sb("mine", [P, 1, SUB])
        ab_ready, a_pre, exps_ready, a_in, a_ready, aT_ready, chained, scanned, stored, rate, spread = [
            sem(x) for x in ("ab_ready", "a_pre", "exps_ready", "a_in", "a_ready", "aT_ready", "chained", "scanned",
                             "stored", "rate", "spread")]
        AB, ROWS = 4, (0, 1, 2, 3)
        first = Channels(nc, {x: sem(x) for x in Channels.NAMES.split()}, ps, (5, 6, 7, 5), win, taps, chan, square, xnT)

        with nc.Block() as block:
            @block.sync
            def _(sp):
                sp.wait_ge(scanned, BATCH + 1)
                sp.dma_start(a_dram.rearrange("b (h t) -> h b t", h=DH),
                             aT[:].rearrange("h (b k) p -> h b (k p)", b=BATCH)).then_inc(stored, 16)
                sp.dma_start(g_dram.rearrange("b (h t) -> h b t", h=DH), gT[:]).then_inc(stored, 16)
                sp.wait_ge(stored, 32)
                spread_decays(nc, sp, a_dram, g_dram, a_all, g_all, slice(0, 1), spread)
                sp.wait_ge(spread, SPREADS)
                sp.wait_ge(loaded, 16 * LOADS)

            @block.scalar
            def _(act):
                n.scalar_root(act)
                act.wait_ge(loaded, 16 * LOADS)
                nc.scalar.activation(neg_rate[:], neg_rate[:], ACT.Exp).then_inc(rate, 1)
                act.wait_ge(rate, 1)
                nc.scalar.mul(neg_rate[:], neg_rate[:], -1.0).then_inc(rate, 1)
                for g in range(GROUPS):
                    act.wait_ge(n.turned, GROUP_TILES * (g + 1))
                    for c in range(DC):
                        nc.scalar.copy(xnT[:, c, g * GROUP:(g + 1) * GROUP], ps[:, n.bank(g, c), :]
                                       ).then_inc(n.copied, 1)
                for j in range(len(JOBS) - 1):
                    first.tap(act, j)
                act.wait_ge(a_pre, 1)
                nc.scalar.activation(u[:], u[:], ACT.Exp, scale=-1.0).then_inc(exps_ready, 1)
                nc.scalar.activation(beta_all[:], ab[:, :, DH:], ACT.Exp, scale=-1.0).then_inc(exps_ready, 1)
                first.tap(act, len(JOBS) - 1)
                act.wait_ge(a_in, 1)
                nc.scalar.activation(decay[:], poly[:], ACT.Exp).then_inc(a_ready, 1)
                for j in range(len(JOBS)):
                    first.silu(act, j)

            @block.gpsimd
            def _(pool):
                for j in range(QK_JOBS):
                    first.squares(pool, j)

            @block.tensor
            def _(pe):
                for g in range(GROUPS):
                    n.tensor(pe, r.ident, g)
                pe.wait_ge(loaded, 16 * LOADS)
                for g in range(GROUPS):
                    pe.wait_ge(n.copied, DC * (g + 1))
                    for t in range(g * GROUP_TILES, (g + 1) * GROUP_TILES):
                        for c in range(DC):
                            mm = nc.tensor.matmul(ps[:, AB, t * 2 * DH:(t + 1) * 2 * DH],
                                                  xnT[:, c, t * P:(t + 1) * P], wab[:, c, :],
                                                  start=(c == 0), stop=(c == DC - 1))
                mm.then_inc(ab_ready, 1)
                for j in range(len(JOBS)):
                    first.job(pe, j, slice(0, SEQ))
                pe.wait_ge(a_ready, 1)
                for t in range(TILES):
                    at = (t % GROUP_TILES) * P
                    mm = nc.tensor.transpose(ps[0:DH, ROWS[t // GROUP_TILES], at:at + P], decay[:, t, :], r.ident[:])
                mm.then_inc(aT_ready, 1)

            @block.vector
            def _(dve):
                done, convs = [0], [0]

                def link(ins):
                    done[0] += 1
                    ins.then_inc(chained, 1)
                    if done[0] >= 3 and convs[0] < len(JOBS) * (TAPS - 1):
                        first.conv(dve, convs[0])
                        convs[0] += 1
                    dve.wait_ge(chained, done[0])

                n.vector(dve, r.x)
                nc.vector.memset(zeros_row[:], 0.0)
                for k in range(HALVES):
                    nc.vector.tensor_copy(ident2[:, k, :], r.ident[:])
                dve.wait_ge(masks, 3)
                pairs = blocks[:].rearrange("p (b h) -> p h b", h=2)
                nc.vector.tensor_reduce(even_neg[:], pairs[:, 0:1, :], AX_X, ALU.add, negate=True)
                nc.vector.tensor_reduce(odd_neg[:], pairs[:, 1:2, :], AX_X, ALU.add, negate=True)
                wide = blocks[:].rearrange("p (b o) -> p b o", o=1).to_broadcast([P, BLOCKS, SUB])
                nc.vector.tensor_scalar(off_blocks[:, 0, :].rearrange("p (b t) -> p b t", b=BLOCKS), wide,
                                        -1.0, 1.0, ALU.mult, ALU.add)
                for h in range(DH):
                    nc.vector.tensor_copy(own[:, h, :],
                                          head_ones[:, (h % 4) * DK:(h % 4) * DK + 1].to_broadcast([P, DV]))
                link(nc.vector.tensor_reduce(mine[:, 0, :], r.ident[:].rearrange("p (b t) -> p t b", b=BLOCKS),
                                             AX_X, ALU.add))
                nc.vector.tensor_copy(urep[:, 0, :, :], mine[:].to_broadcast([P, UNITS, SUB]))
                nc.vector.tensor_copy(inv[:, :, 1:2], mine[:, :, 0:1].to_broadcast([P, UNITS, 1]))

                dve.wait_ge(ab_ready, 1)
                link(nc.vector.tensor_copy(ab[:].rearrange("p t h -> p (t h)"), ps[:, AB, 0:TILES * 2 * DH]))
                link(nc.vector.tensor_tensor(ab[:, :, 0:DH], ab[:, :, 0:DH], dtb[:].to_broadcast(TH), ALU.add))
                nc.vector.scalar_tensor_tensor(u[:], ab[:, :, 0:DH], -1.0, ab[:, :, 0:DH], ALU.mult,
                                               ALU.max).then_inc(a_pre, 1)
                dve.wait_ge(exps_ready, 2)
                link(nc.vector.tensor_scalar(beta_all[:], beta_all[:], 1.0, None, ALU.add))
                nc.vector.reciprocal(beta_all[:], beta_all[:])
                link(nc.vector.tensor_scalar(s[:], u[:], 2.0, None, ALU.add))
                link(nc.vector.reciprocal(s[:], s[:]))
                link(nc.vector.tensor_tensor(s[:], s[:], u[:], ALU.mult))
                link(nc.vector.tensor_tensor(s2[:], s[:], s[:], ALU.mult))
                link(nc.vector.tensor_scalar(poly[:], s2[:], 1.0 / (2 * ATANH_TERMS + 1), None, ALU.mult))
                for k in range(ATANH_TERMS - 1, 0, -1):
                    link(nc.vector.scalar_tensor_tensor(poly[:], poly[:], 1.0 / (2 * k + 1), s2[:], ALU.add, ALU.mult))
                link(nc.vector.scalar_tensor_tensor(poly[:], poly[:], 1.0, s[:], ALU.add, ALU.mult))
                link(nc.vector.tensor_scalar(ab[:, :, 0:DH], ab[:, :, 0:DH], 0.0, None, ALU.max))
                link(nc.vector.scalar_tensor_tensor(poly[:], poly[:], 2.0, ab[:, :, 0:DH], ALU.mult, ALU.add))
                dve.wait_ge(rate, 2)
                nc.vector.tensor_tensor(poly[:], poly[:], neg_rate[:].to_broadcast(TH), ALU.mult).then_inc(a_in, 1)
                while convs[0] < len(JOBS) * (TAPS - 1):
                    first.conv(dve, convs[0])
                    convs[0] += 1
                dve.wait_ge(aT_ready, 1)
                for g in range(GROUPS):
                    ins = nc.vector.tensor_copy(
                        aT[:, g * GROUP_TILES:(g + 1) * GROUP_TILES, :].rearrange("h t p -> h (t p)"),
                        ps[0:DH, ROWS[g], :])
                link(ins)
                for b in range(BATCH):
                    nc.vector.tensor_tensor_scan(gT[:, b, :], aT[:, HALVES * b + 1, :], zeros_row[:], 1.0,
                                                 ALU.mult, ALU.add).then_inc(scanned, 1)
                dve.wait_ge(scanned, BATCH)
                nc.vector.memset(aT[:, :, 0:1], 0.0).then_inc(scanned, 1)
        end_of_round(nc, [loaded, masks, ab_ready, a_pre, exps_ready, a_in, a_ready, aT_ready, chained, scanned,
                          stored, rate, spread] + list(n.sems) + list(first.S.values()))


def batches(nc, r, ps, win, wgate, wo, taps, normw, blocks, even_neg, odd_neg, off_blocks, head_ones, own,
            ident2, urep, inv, xnT, beta, a_dram, g_dram, state, chan, square, kq, a_all, g_all):
    with ExitStack() as ctx:
        def sb(name, shape, dt=F32):
            return ctx.enter_context(nc.sbuf_tensor("cb_" + name, shape, dt))

        def sem(name):
            return ctx.enter_context(nc.semaphore("cb_" + name))

        WIDE = DV + DK
        SET = VALS + WIDE
        WIDES = (DH - 1) * WIDE
        xb = sb("xb", [P, DC, SEQ])
        bb = sb("bb", [P, HALVES, DH])
        rnorm = sb("rnorm", [P, QK_JOBS, SEQ])
        E = sb("E", [P, DH, HALVES, P])
        klast = sb("klast", [P, DH, 1])
        diag = sb("diag", [P, UNITS, SUB])
        prod = sb("prod", [P, UNITS, SUB])
        kqg = sb("kqg", [P, 2, 2, 2, P])
        ktok = sb("ktok", [P, 2, DH, DK])
        right = sb("right", [P, 2, HALVES, SET])
        gate = sb("gate", [P, 2, HALVES, DH, DV])
        aq = sb("aq", [P, 2, UNITS, 2, P])
        low = sb("low", [P, 2, UNITS, P])
        tdT = sb("tdT", [P, UNITS, P])
        nN, nT, n2T = [sb(x, [P, UNITS, P]) for x in ("nN", "nT", "n2T")]
        y, z = [sb(x, [P, HALVES, SET]) for x in ("y", "z")]
        wk = sb("wk", [P, KEYS])
        wkT = sb("wkT", [P, 2, P])
        x1 = sb("x1", [P, VALS])
        o, osq = [sb(x, [P, DH, DV]) for x in ("o", "osq")]
        ms = sb("ms", [P, DH, 1])
        oT = sb("oT", [P, VALS // P, P])

        names = (Channels.NAMES + " xb_ready a_spread norms_ready ln_ready rnorm_ready kq_pool kq_vector kqg_ready "
                 "gates_ready gate_taken gated vT_ready v_ready kT_ready ktok_ready kg_ready "
                 "e_ready klast_ready scores_ready aq_ready lT_ready l_ready folded inv_step td_pool td_vector "
                 "n_ready n_copied y_ready y_copied step_ready step_done state_ready state_copied wk_ready wkT_ready "
                 "wkT_copied ks_ready x1_ready o_ready osq_ready "
                 "epi_chain ms_ready root_ready o_done oT_ready oT_copied out_ready out_added").split()
        S = {x: sem(x) for x in names}
        round_sems = [S[x] for x in names]

        NORM_BANKS, N_BANKS, SCORE_BANKS, K_BANK, V_BANKS = (0, 1), (2, 3, 4), (0, 1), 2, (3, 4)
        L_BANKS, SET_BANKS, O_BANKS, JOB_BANKS, GATE_BANKS = (0, 1, 2), (5, 6), (3, 5), (7, 7, 4, 0), (1, 2)
        PAIRS = DH // 2
        STEPS = 4
        CONVS = len(JOBS) * (TAPS - 1)

        channels = Channels(nc, S, ps, JOB_BANKS, win, taps, chan, square, xnT)

        def head_cols(h):
            return slice(h * DV, (h + 1) * DV)

        def half_cols(k):
            return slice(k * P, (k + 1) * P)

        def wide(h):
            return (1, h * WIDE) if h < DH - 1 else (0, VALS)

        def rights(s):
            if s:
                return [(h, 1, slice(h * WIDE, (h + 1) * WIDE)) for h in range(DH - 1)]
            return [(h, 0, head_cols(h)) for h in range(DH)] + [(DH - 1, 1, slice(VALS, SET))]

        WIDTHS = (SET, WIDES)
        HEAD_SETS = ((0, slice(0, SET0)), (1, slice(SET0, VALS)))

        def wides(t):
            return t[:, 0:WIDES].rearrange("p (h w) -> p h w", w=WIDE)

        def stage(first, middle, ms_, last, ls):
            C_, M_, S_ = first is not None, middle is not None, last is not None
            with nc.Block() as block:
                @block.sync
                def _(sp):
                    if C_:
                        sp.wait_ge(S["e_ready"], DH)
                        sp.wait_ge(S["kqg_ready"], 2)
                        spread_decays(nc, sp, a_dram, g_dram, a_all, g_all, bass.ds(first, 1), S["a_spread"])
                        sp.wait_ge(S["a_spread"], SPREADS)

                def normalise_channels(engine, eng, j, sem_name):
                    m = JOBS[j][1]
                    engine.wait_ge(S["rnorm_ready"], j + 1)
                    eng.tensor_tensor(kq[0:m, j // 2, 1 - j % 2, :], chan[0:m, j, :], rnorm[0:m, j, :],
                                      ALU.mult).then_inc(S[sem_name], 1)

                def spread_inverse(eng, p, sem_name):
                    us = slice(p * 2 * HALVES, (p + 1) * 2 * HALVES)
                    eng.tensor_tensor(
                        tdT[:, us, :].rearrange("p u (b t) -> p u b t", b=BLOCKS),
                        inv[:, us, 1:SUB + 1].rearrange("p u (o t) -> p u o t", o=1).to_broadcast(
                            [P, 2 * HALVES, BLOCKS, SUB]),
                        blocks[:].rearrange("p (o b k) -> p o b k", o=1, k=1).to_broadcast(
                            [P, 2 * HALVES, BLOCKS, SUB]), ALU.mult).then_inc(S[sem_name], 1)

                @block.gpsimd
                def _(pool):
                    if M_:
                        nc.gpsimd.tensor_copy(bb[:], beta[:, bass.ds(middle * HALVES, HALVES), :]
                                              ).then_inc(S["xb_ready"], 1)
                        for j in (0, 2):
                            normalise_channels(pool, nc.gpsimd, j, "kq_pool")
                        pool.wait_ge(S["kq_pool"], 2)
                        pool.wait_ge(S["kq_vector"], 2)
                        for hs in range(2):
                            nc.gpsimd.tensor_tensor(kqg[:, ms_, hs], kq[:, hs, :, P:SEQ],
                                                    g_all[:, hs:hs + 1, :].to_broadcast([P, 2, P]), ALU.mult
                                                    ).then_inc(S["kqg_ready"], 1)
                        nc.gpsimd.tensor_copy(xb[:], xnT[:, :, bass.ds(middle * SEQ, SEQ)]).then_inc(S["xb_ready"], 1)
                    if S_:
                        for k in range(HALVES):
                            nc.gpsimd.tensor_tensor(gate[:, ls, k], gate[:, ls, k],
                                                    normw[:].to_broadcast([P, DH, DV]), ALU.mult
                                                    ).then_inc(S["gated"], 1)
                    if C_:
                        pool.wait_ge(S["norms_ready"], QK_JOBS)
                        for j in range(QK_JOBS):
                            channels.squares(pool, j)
                    if M_:
                        pool.wait_ge(S["inv_step"], 2 * (SUB - 1))
                        if S_:
                            pool.wait_ge(S["y_ready"], 2)
                        spread_inverse(nc.gpsimd, 2, "td_pool")

                @block.vector
                def _(dve):
                    def scan(h):
                        nc.vector.tensor_tensor_scan(E[:, h].rearrange("p t k -> p (t k)"), a_all[:, h, :],
                                                     ident2[:].rearrange("p t k -> p (t k)"), 0.0,
                                                     ALU.mult, ALU.add).then_inc(S["e_ready"], 1)

                    def last_decays():
                        dve.wait_ge(S["e_ready"], DH)
                        dve.wait_ge(S["xb_ready"], 1)
                        nc.vector.tensor_tensor(klast[:], E[:, :, 0, P - 1:P],
                                                bb[:, 0, :].rearrange("p (h o) -> p h o", o=1), ALU.mult
                                                ).then_inc(S["klast_ready"], 1)

                    def keys_by_token():
                        dve.wait_ge(S["klast_ready"], 1)
                        dve.wait_ge(S["kg_ready"], 2)
                        nc.vector.tensor_tensor(ktok[:, ms_], ps[:, K_BANK, 0:KEYS].rearrange("p (h k) -> p h k", h=DH),
                                                klast[:].to_broadcast([P, DH, DK]), ALU.mult
                                                ).then_inc(S["ktok_ready"], 1)

                    def products(h):
                        dve.wait_ge(S["scores_ready"], h + 1)
                        for k in range(HALVES):
                            src = ps[:, SCORE_BANKS[h % 2], k * 2 * P:(k + 1) * 2 * P].rearrange("p (c t) -> p c t", c=2)
                            nc.vector.scalar_tensor_tensor(aq[:, ms_, h * HALVES + k], src, bb[:, k, h:h + 1],
                                                           E[:, h, k:k + 1, :].to_broadcast([P, 2, P]),
                                                           ALU.mult, ALU.mult).then_inc(S["aq_ready"], 1)

                    def off_diagonal(p):
                        dve.wait_ge(S["lT_ready"], p + 1)
                        nc.vector.tensor_tensor(low[:, ms_, p * 2 * HALVES:(p + 1) * 2 * HALVES, :],
                                                ps[:, L_BANKS[p], :].rearrange("p (t k) -> p t k", k=P),
                                                off_blocks[:].to_broadcast([P, 2 * HALVES, P]), ALU.mult
                                                ).then_inc(S["l_ready"], 1)

                    def fold_even():
                        dve.wait_ge(S["aq_ready"], UNITS)
                        for q in range(P // 32):
                            rows = slice(32 * q, 32 * q + 32)
                            ins = nc.vector.tensor_scalar(diag[rows], aq[rows, ms_, :, 0, 32 * q:32 * q + SUB],
                                                          even_neg[rows], None, ALU.mult)
                        ins.then_inc(S["folded"], 1)

                    def fold_odd():
                        dve.wait_ge(S["folded"], 1)
                        for q in range(P // 32):
                            rows = slice(32 * q, 32 * q + 32)
                            ins = nc.vector.scalar_tensor_tensor(diag[rows],
                                                                 aq[rows, ms_, :, 0, 32 * q + SUB:32 * q + 32],
                                                                 odd_neg[rows], diag[rows], ALU.mult, ALU.add)
                        ins.then_inc(S["folded"], 1)

                    def shuffle(k):
                        if k == 0:
                            dve.wait_ge(S["folded"], 2)
                        ins = nc.vector.stream_shuffle(urep[:, 1 + k, :, k + 1:SUB], diag[:, :, k + 1:SUB],
                                                       [k] * SUB + [SUB + k] * SUB)
                        if k == SUB - 2:
                            ins.then_inc(S["folded"], 1)

                    def column_product(t):
                        if t == 1:
                            dve.wait_ge(S["folded"], 3)
                        else:
                            dve.wait_ge(S["inv_step"], 2 * (t - 1))
                        nc.vector.tensor_tensor(prod[:, :, 0:t + 1], inv[:, :, 0:t + 1],
                                                urep[:, 0:t + 1, :, t].rearrange("p k u -> p u k"), ALU.mult
                                                ).then_inc(S["inv_step"], 1)

                    def column_sum(t):
                        dve.wait_ge(S["inv_step"], 2 * t - 1)
                        nc.vector.reduce_sum(inv[:, :, 1 + t:2 + t], prod[:, :, 0:t + 1], AX_X
                                             ).then_inc(S["inv_step"], 1)

                    def step(k, s):
                        dve.wait_ge(S["step_ready"], 2 * k + s + 1)
                        w = WIDTHS[s]
                        if k == 0:
                            dve.wait_ge(S["y_copied"], s + 1)
                        dst, base = (z, y) if k == 0 else (y, z)
                        nc.vector.tensor_tensor(dst[:, s, 0:w], base[:, s, 0:w], ps[:, SET_BANKS[s], 0:w], ALU.add
                                                ).then_inc(S["step_done"], 1)

                    def keep_state():
                        dve.wait_ge(S["state_ready"], 1)
                        nc.vector.tensor_tensor(state[:, 0:SET0], ps[:, SET_BANKS[0], 0:SET0],
                                                own[:, 0:4, :].rearrange("p h v -> p (h v)"), ALU.mult)
                        rows = slice(0, KEYS - P)
                        nc.vector.tensor_tensor(state[rows, SET0:VALS], ps[rows, SET_BANKS[0], SET0:VALS],
                                                own[rows, 4:DH, :].rearrange("p h v -> p (h v)"), ALU.mult
                                                ).then_inc(S["state_copied"], 1)

                    def second_values():
                        dve.wait_ge(S["ks_ready"], 1)
                        dve.wait_ge(S["step_done"], 2 * STEPS)
                        nc.vector.tensor_tensor(x1[:, 0:(DH - 1) * DV].rearrange("p (h v) -> p h v", v=DV),
                                                wides(y[:, 1])[:, :, 0:DV],
                                                ps[:, SET_BANKS[1], 0:(DH - 1) * DV].rearrange("p (h v) -> p h v", v=DV),
                                                ALU.subtract)
                        nc.vector.tensor_tensor(x1[:, (DH - 1) * DV:], y[:, 0, VALS:VALS + DV],
                                                ps[:, SET_BANKS[1], (DH - 1) * DV:VALS], ALU.subtract
                                                ).then_inc(S["x1_ready"], 1)

                    def mean_square(half):
                        dve.wait_ge(S["osq_ready"], half + 1)
                        if half:
                            dve.wait_ge(S["o_done"], 1)
                        nc.vector.reduce_sum(ms[:], osq[:], AX_X).then_inc(S["epi_chain"], 1)

                    def gated_output(half):
                        dve.wait_ge(S["epi_chain"], 2 * half + 1)
                        nc.vector.tensor_scalar(ms[:], ms[:], 1.0 / DV, RMS_EPS, ALU.mult, ALU.add
                                                ).then_inc(S["ms_ready"], 1)
                        dve.wait_ge(S["gated"], half + 1)
                        if half:
                            dve.wait_ge(S["oT_ready"], 1)
                        nc.vector.tensor_tensor(o[:], ps[:, O_BANKS[half], 0:VALS].rearrange("p (h v) -> p h v", h=DH),
                                                gate[:, ls, half], ALU.mult).then_inc(S["epi_chain"], 1)

                    def normalise(half):
                        dve.wait_ge(S["epi_chain"], 2 * half + 2)
                        dve.wait_ge(S["root_ready"], 2 * (half + 1))
                        nc.vector.tensor_tensor(o[:], o[:], ms[:].to_broadcast([P, DH, DV]), ALU.mult
                                                ).then_inc(S["o_done"], 1)

                    def add_out(half):
                        dve.wait_ge(S["out_ready"], half + 1)
                        xt = r.x[:, bass.ds(last * HALVES + half, 1), :].rearrange("p a d -> p (a d)")
                        nc.vector.tensor_tensor(xt, xt, ps[:, O_BANKS[half], 0:HID], ALU.add
                                                ).then_inc(S["out_added"], 1)

                    def run(on, f, *args):
                        if on:
                            f(*args)

                    def convolve(q, to):
                        for q in range(q, to):
                            run(C_, channels.conv, dve, q)

                    for h in range(DH):
                        run(M_, scan, h)
                    run(M_, last_decays)
                    for j in (1, 3):
                        run(M_, normalise_channels, dve, nc.vector, j, "kq_vector")
                    for h in range(DH):
                        run(M_, products, h)
                        if h >= 2:
                            convolve(h - 2, h - 1)
                    convolve(4, 6)
                    run(M_, fold_even)
                    run(M_, fold_odd)
                    for k in range(SUB - 1):
                        run(M_, shuffle, k)
                    conv = [(channels.conv, dve, q) for q in range(6, CONVS)] if C_ else []
                    keys = [(keys_by_token,)] if M_ else []
                    off = [(off_diagonal, p) for p in range(PAIRS)] if M_ else []
                    solving = [(step, 0, 0), (step, 0, 1), (step, 1, 0), (step, 1, 1),
                               (step, 2, 0), (step, 2, 1), (step, 3, 0), (step, 3, 1), (keep_state,), (second_values,),
                               (mean_square, 0), (gated_output, 0), (normalise, 0), (mean_square, 1),
                               (gated_output, 1), (add_out, 0), (normalise, 1), (add_out, 1)] if S_ else []
                    fill = (keys + conv[0:1] + solving[0:1] + conv[1:2] + solving[1:2] + conv[2:3] + solving[2:3]
                            + conv[3:4] + solving[3:4] + off[0:1] + solving[4:5] + off[1:2] + solving[5:6] + off[2:3]
                            + solving[6:7] + conv[4:5] + solving[7:8] + conv[5:6] + solving[8:9] + conv[6:7]
                            + solving[9:10] + conv[7:8] + solving[10:12] + conv[8:9] + solving[12:13] + conv[9:11] + solving[13:15] + conv[11:12] + solving[15:17]
                            + conv[12:14] + solving[17:] + conv[14:])
                    if M_:
                        for t in range(1, SUB):
                            column_product(t)
                            if fill:
                                f, *args = fill.pop(0)
                                f(*args)
                            column_sum(t)
                            if fill:
                                f, *args = fill.pop(0)
                                f(*args)
                        dve.wait_ge(S["inv_step"], 2 * (SUB - 1))
                        if S_:
                            dve.wait_ge(S["y_ready"], 2)
                        for p in range(2):
                            spread_inverse(nc.vector, p, "td_vector")
                    for f, *args in fill:
                        f(*args)

                @block.scalar
                def _(act):
                    def gate_silu(k):
                        act.wait_ge(S["gates_ready"], k + 1)
                        nc.scalar.activation(gate[:, ms_, k].rearrange("p h v -> p (h v)"),
                                             ps[:, GATE_BANKS[k], 0:VALS], ACT.Silu).then_inc(S["gate_taken"], 1)

                    def norm_ln(j):
                        m = JOBS[j][1]
                        act.wait_ge(S["norms_ready"], 2 * (j // 2) + 2)
                        nc.scalar.activation(rnorm[0:m, j, :], ps[0:m, NORM_BANKS[j // 2], (j % 2) * SEQ:(j % 2 + 1) * SEQ],
                                             ACT.Ln, scale=float(DK) if j % 2 == 0 else 1.0).then_inc(S["ln_ready"], 1)

                    def norm_exp(j):
                        m = JOBS[j][1]
                        act.wait_ge(S["ln_ready"], j + 1)
                        nc.scalar.activation(rnorm[0:m, j, :], rnorm[0:m, j, :], ACT.Exp, scale=-0.5
                                             ).then_inc(S["rnorm_ready"], 1)

                    def values_by_token(k):
                        act.wait_ge(S["vT_ready"], k + 1)
                        if k == 0:
                            nc.scalar.copy(right[:, ms_, 0, 0:VALS], ps[:, V_BANKS[0], 0:VALS]
                                           ).then_inc(S["v_ready"], 1)
                        else:
                            w = (DH - 1) * DV
                            nc.scalar.copy(wides(right[:, ms_, 1])[:, :, 0:DV],
                                           ps[:, V_BANKS[1], 0:w].rearrange("p (h v) -> p h v", v=DV)
                                           ).then_inc(S["v_ready"], 1)
                            nc.scalar.copy(right[:, ms_, 0, VALS:VALS + DV], ps[:, V_BANKS[1], w:VALS]
                                           ).then_inc(S["v_ready"], 1)

                    def second_keys():
                        act.wait_ge(S["kT_ready"], 1)
                        w = (DH - 1) * DK
                        nc.scalar.copy(wides(right[:, ms_, 1])[:, :, DV:WIDE],
                                       ps[:, K_BANK, KEYS:KEYS + w].rearrange("p (h k) -> p h k", k=DK)
                                       ).then_inc(S["kg_ready"], 1)
                        nc.scalar.copy(right[:, ms_, 0, VALS + DV:SET], ps[:, K_BANK, KEYS + w:2 * KEYS]
                                       ).then_inc(S["kg_ready"], 1)

                    def copy_n(q):
                        dst, scale = ((nT, -1.0), (nN, 1.0), (n2T, -1.0))[q // PAIRS]
                        p = q % PAIRS
                        act.wait_ge(S["n_ready"], q + 1)
                        nc.scalar.mul(dst[:, p * 2 * HALVES:(p + 1) * 2 * HALVES, :].rearrange("p u t -> p (u t)"),
                                      ps[:, N_BANKS[q % 3], :], scale).then_inc(S["n_copied"], 1)

                    def copy_y(s):
                        act.wait_ge(S["y_ready"], s + 1)
                        nc.scalar.copy(y[:, s, 0:WIDTHS[s]], ps[:, SET_BANKS[s], 0:WIDTHS[s]]
                                       ).then_inc(S["y_copied"], 1)

                    def solved_keys():
                        act.wait_ge(S["step_done"], 2 * STEPS)
                        w = (DH - 1) * DK
                        nc.scalar.copy(wk[:, 0:w].rearrange("p (h k) -> p h k", k=DK), wides(y[:, 1])[:, :, DV:WIDE]
                                       ).then_inc(S["wk_ready"], 1)
                        nc.scalar.copy(wk[:, w:KEYS], y[:, 0, VALS + DV:SET]).then_inc(S["wk_ready"], 1)

                    def copy_wkT():
                        act.wait_ge(S["wkT_ready"], 1)
                        nc.scalar.copy(wkT[:, 0, :], ps[:, SET_BANKS[1], 0:P]).then_inc(S["wkT_copied"], 1)
                        nc.scalar.copy(wkT[0:KEYS - P, 1, :], ps[0:KEYS - P, SET_BANKS[1], P:2 * P]
                                       ).then_inc(S["wkT_copied"], 1)

                    def squares(half):
                        act.wait_ge(S["o_ready"], half + 1)
                        if half:
                            act.wait_ge(S["epi_chain"], 1)
                        nc.scalar.activation(osq[:].rearrange("p h v -> p (h v)"), ps[:, O_BANKS[half], 0:VALS],
                                             ACT.Square).then_inc(S["osq_ready"], 1)

                    def root(half):
                        act.wait_ge(S["ms_ready"], half + 1)
                        nc.scalar.activation(ms[:], ms[:], ACT.Ln).then_inc(S["root_ready"], 1)
                        act.wait_ge(S["root_ready"], 2 * half + 1)
                        nc.scalar.activation(ms[:], ms[:], ACT.Exp, scale=-0.5).then_inc(S["root_ready"], 1)

                    def copy_oT(half):
                        act.wait_ge(S["oT_ready"], half + 1)
                        if half:
                            act.wait_ge(S["out_ready"], 1)
                        nc.scalar.copy(oT[:].rearrange("p c t -> p (c t)"), ps[:, O_BANKS[half], 0:VALS]
                                       ).then_inc(S["oT_copied"], 1)

                    nc.scalar.preload_act_table_set("natural_log_exp_and_others")

                    def run(on, f, *args):
                        if on:
                            f(*args)

                    for j in range(QK_JOBS):
                        run(M_, norm_ln, j)
                    for j in range(QK_JOBS):
                        run(M_, norm_exp, j)
                    for q in range(PAIRS + 1):
                        run(S_, copy_n, q)
                    if M_ and C_:
                        act.wait_ge(S["kq_pool"], 2)
                        act.wait_ge(S["kq_vector"], 2)
                    run(C_, channels.tap, act, 0)
                    run(C_, channels.tap, act, 1)
                    for q in range(PAIRS + 1, 3 * PAIRS):
                        run(S_, copy_n, q)
                    run(S_, copy_y, 0)
                    run(S_, copy_y, 1)
                    run(M_, second_keys)
                    run(C_, channels.tap, act, 2)
                    run(C_, channels.tap, act, 3)
                    run(M_, values_by_token, 0)
                    run(M_, values_by_token, 1)
                    run(C_, channels.tap, act, 4)
                    run(C_, channels.tap, act, 5)
                    run(S_, solved_keys)
                    run(S_, copy_wkT)
                    run(S_, squares, 0)
                    run(S_, root, 0)
                    run(S_, squares, 1)
                    run(S_, copy_oT, 0)
                    run(C_, channels.tap, act, 6)
                    run(S_, root, 1)
                    for j in range(QK_JOBS):
                        run(C_, channels.silu, act, j)
                    for k in range(HALVES):
                        run(M_, gate_silu, k)
                    run(S_, copy_oT, 1)
                    for j in range(QK_JOBS, len(JOBS)):
                        run(C_, channels.silu, act, j)

                @block.tensor
                def _(pe):
                    def norms(j):
                        m = JOBS[j][1]
                        nc.tensor.matmul(ps[0:m, NORM_BANKS[j // 2], (j % 2) * SEQ:(j % 2 + 1) * SEQ],
                                         head_ones[0:m, 0:m], square[0:m, j, :], start=True, stop=True
                                         ).then_inc(S["norms_ready"], 1)

                    def scores(h):
                        rows = slice((h % 4) * DK, (h % 4 + 1) * DK)
                        if h == 0:
                            pe.wait_ge(S["kq_pool"], 2)
                            pe.wait_ge(S["kq_vector"], 2)
                        if h >= 2:
                            pe.wait_ge(S["aq_ready"], HALVES * (h - 1))
                        for k in range(HALVES):
                            mm = nc.tensor.matmul(ps[:, SCORE_BANKS[h % 2], k * 2 * P:(k + 1) * 2 * P],
                                                  kq[rows, h // 4, 0, half_cols(k)], kq[rows, h // 4, :, half_cols(k)],
                                                  start=True, stop=True)
                        mm.then_inc(S["scores_ready"], 1)

                    def turn_keys():
                        pe.wait_ge(S["kqg_ready"], 2)
                        if S_:
                            pe.wait_ge(S["n_copied"], 7)
                        m = KEYS - P
                        nc.tensor.transpose(ps[:, K_BANK, 0:P], kq[:, 0, 0, 0:P], r.ident[:])
                        nc.tensor.transpose(ps[:, K_BANK, P:KEYS], kq[0:m, 1, 0, 0:P], r.ident[0:m, 0:m])
                        nc.tensor.transpose(ps[:, K_BANK, KEYS:KEYS + P], kqg[:, ms_, 0, 0, :], r.ident[:])
                        nc.tensor.transpose(ps[:, K_BANK, KEYS + P:2 * KEYS], kqg[0:m, ms_, 1, 0, :],
                                            r.ident[0:m, 0:m]).then_inc(S["kT_ready"], 1)

                    def turn_values(k):
                        if S_:
                            pe.wait_ge(S["n_copied"], 8 + k)
                        for c in range(VALS // P):
                            mm = nc.tensor.transpose(ps[:, V_BANKS[k], c * P:(c + 1) * P],
                                                     chan[:, QK_JOBS + c, half_cols(k)], r.ident[:])
                        mm.then_inc(S["vT_ready"], 1)

                    def turn_low(p):
                        pe.wait_ge(S["aq_ready"], (10, 12, 12)[p])
                        if p == 2:
                            pe.wait_ge(S["ktok_ready"], 1)
                        for u in range(2 * HALVES):
                            mm = nc.tensor.transpose(ps[:, L_BANKS[p], u * P:(u + 1) * P],
                                                     aq[:, ms_, p * 2 * HALVES + u, 0, :], r.ident[:])
                        mm.then_inc(S["lT_ready"], 1)

                    def gates(k):
                        pe.wait_ge(S["xb_ready"], 2)
                        pe.wait_ge(S["l_ready"], k + 2)
                        for c in range(DC):
                            mm = nc.tensor.matmul(ps[:, GATE_BANKS[k], 0:VALS], xb[:, c, half_cols(k)], wgate[:, c, :],
                                                  start=(c == 0), stop=(c == DC - 1))
                        mm.then_inc(S["gates_ready"], 1)

                    def job(j):
                        if M_ and j == 4:
                            pe.wait_ge(S["v_ready"], 3)
                        if M_ and j == 6:
                            pe.wait_ge(S["l_ready"], 1)
                        channels.job(pe, j, bass.ds(first * SEQ, SEQ))

                    def n_product(q):
                        kind, p = divmod(q, PAIRS)
                        if kind:
                            pe.wait_ge(S["n_copied"], q - 2)
                        if kind == 2:
                            pe.wait_ge(S["n_copied"], PAIRS + p + 1)
                        for k in range(2 * HALVES):
                            u = p * 2 * HALVES + k
                            lhsT, rhs_ = ((low[:, ls, u, :], tdT[:, u, :]), (tdT[:, u, :], low[:, ls, u, :]),
                                          (nN[:, u, :], nT[:, u, :]))[kind]
                            mm = nc.tensor.matmul(ps[:, N_BANKS[q % 3], k * P:(k + 1) * P], lhsT, rhs_,
                                                  start=True, stop=True)
                        mm.then_inc(S["n_ready"], 1)

                    def multiply(s, mat, src, signal):
                        for h, half, cols in rights(s):
                            mm = nc.tensor.matmul(ps[:, SET_BANKS[s], cols], mat[:, h * HALVES + half, :],
                                                  src[:, cols], start=True, stop=True)
                        mm.then_inc(S[signal], 1)

                    def solve_blocks(s):
                        multiply(s, tdT, right[:, ls, s], "y_ready")

                    def step(k, s):
                        if k == 0:
                            pe.wait_ge(S["y_copied"], s + 1)
                            pe.wait_ge(S["n_copied"], PAIRS)
                        else:
                            pe.wait_ge(S["step_done"], 2 * (k - 1) + s + 1)
                            pe.wait_ge(S["n_copied"], 3 * PAIRS)
                        multiply(s, nT if k == 0 else n2T, (z if k == 1 else y)[:, s], "step_ready")

                    def new_state():
                        pe.wait_ge(S["step_done"], 2 * (STEPS - 1) + 1)
                        nc.tensor.matmul(ps[:, SET_BANKS[0], 0:SET0], ktok[:, ls, 0:4, :].rearrange("p h k -> p (h k)"),
                                         y[:, 0, 0:SET0], start=True, stop=True)
                        nc.tensor.matmul(ps[0:KEYS - P, SET_BANKS[0], SET0:VALS],
                                         ktok[:, ls, 4:DH, :].rearrange("p h k -> p (h k)"),
                                         y[:, 0, SET0:VALS], start=True, stop=True).then_inc(S["state_ready"], 1)

                    def turn_solved_keys():
                        pe.wait_ge(S["wk_ready"], 2)
                        nc.tensor.transpose(ps[:, SET_BANKS[1], 0:P], wk[:, 0:P], r.ident[:])
                        nc.tensor.transpose(ps[0:KEYS - P, SET_BANKS[1], P:2 * P], wk[:, P:KEYS], r.ident[:]
                                            ).then_inc(S["wkT_ready"], 1)

                    def known():
                        pe.wait_ge(S["state_copied"], 1)
                        pe.wait_ge(S["wkT_copied"], 2)
                        m = KEYS - P
                        nc.tensor.matmul(ps[:, SET_BANKS[1], 0:SET0], wkT[:, 0, :], state[:, 0:SET0],
                                         start=True, stop=True)
                        nc.tensor.matmul(ps[:, SET_BANKS[1], SET0:VALS], wkT[0:m, 1, :], state[0:m, SET0:VALS],
                                         start=True, stop=True).then_inc(S["ks_ready"], 1)

                    def outputs(half):
                        if M_ and not half:
                            pe.wait_ge(S["v_ready"], 1)
                        if half:
                            for hs, cols in HEAD_SETS:
                                nc.tensor.matmul(ps[:, O_BANKS[1], cols], kqg[:, ls, hs, 1, :], state[:, cols],
                                                 start=(hs == 0), stop=False, skip_group_check=True)
                            pe.wait_ge(S["x1_ready"], 1)
                        for h in range(DH):
                            src = x1[:, head_cols(h)] if half else y[:, 0, head_cols(h)]
                            mm = nc.tensor.matmul(ps[:, O_BANKS[half], head_cols(h)],
                                                  aq[:, ls, h * HALVES + half, 1, :], src, start=not half, stop=True,
                                                  skip_group_check=bool(half))
                        mm.then_inc(S["o_ready"], 1)

                    def turn_out(half):
                        pe.wait_ge(S["o_done"], half + 1)
                        of = o[:].rearrange("p h v -> p (h v)")
                        for c in range(VALS // P):
                            mm = nc.tensor.transpose(ps[:, O_BANKS[half], c * P:(c + 1) * P],
                                                     of[:, c * P:(c + 1) * P], r.ident[:])
                        mm.then_inc(S["oT_ready"], 1)

                    def project_out(half):
                        pe.wait_ge(S["oT_copied"], half + 1)
                        for c in range(VALS // P):
                            mm = nc.tensor.matmul(ps[:, O_BANKS[half], 0:HID], oT[:, c, :], wo[:, c, :],
                                                  start=(c == 0), stop=(c == VALS // P - 1))
                        mm.then_inc(S["out_ready"], 1)

                    def run(on, f, *args):
                        if on:
                            f(*args)

                    for j in range(QK_JOBS):
                        run(M_, norms, j)
                    for q in range(PAIRS):
                        run(S_, n_product, q)
                    for h in range(DH):
                        run(M_, scores, h)
                        run(S_, n_product, PAIRS + h)
                        run(C_ and h < 2, job, h)
                    run(S_, solve_blocks, 0)
                    run(S_, solve_blocks, 1)
                    run(M_, turn_keys)
                    run(C_, job, 2)
                    run(C_, job, 3)
                    run(S_, step, 0, 0)
                    run(M_, turn_values, 0)
                    run(S_, step, 0, 1)
                    run(M_, turn_values, 1)
                    run(S_, step, 1, 0)
                    run(M_, turn_low, 0)
                    run(S_, step, 1, 1)
                    run(M_, turn_low, 1)
                    run(S_, step, 2, 0)
                    run(M_, turn_low, 2)
                    run(S_, step, 2, 1)
                    run(C_, job, 4)
                    run(S_, step, 3, 0)
                    run(C_, job, 5)
                    run(S_, step, 3, 1)
                    run(S_, new_state)
                    run(S_, turn_solved_keys)
                    run(S_, outputs, 0)
                    run(M_, gates, 0)
                    run(S_, known)
                    run(C_, job, 6)
                    run(S_, outputs, 1)
                    run(S_, turn_out, 0)
                    run(S_, project_out, 0)
                    run(M_, gates, 1)
                    run(S_, turn_out, 1)
                    run(S_, project_out, 1)
            end_of_round(nc, round_sems)

        stage(1, 0, 0, None, None)
        with nc.Fori(0, BATCH // 2 - 1) as i:
            stage(i * 2 + 2, i * 2 + 1, 1, i * 2, 0)
            stage(i * 2 + 3, i * 2 + 2, 0, i * 2 + 1, 1)
        stage(None, BATCH - 1, 1, BATCH - 2, 0)
        stage(None, None, None, BATCH - 1, 1)


EXPERTS, FF, TOP = 6, 176, 2
FF1 = FF - P
BIAS_ROW = 64
W1_AT, W2_AT, B1_AT = 0, DC * FF, DC * FF + 2 * HID
PACKED = B1_AT + 2
ROUND_BATCHES = 4


def routed(nc, r, packed, w_gate, out):
    with ExitStack() as ctx:
        def sb(name, shape, dt=F32):
            return ctx.enter_context(nc.sbuf_tensor("d_" + name, shape, dt))

        def sem(name):
            return ctx.enter_context(nc.semaphore("d_" + name))

        ps = ctx.enter_context(nc.psum_tensor("d_ps", [P, 8, 512], F32))
        HIDDEN, OUT = (0, 1, 2, 3), (4, 5)
        n = Norm(nc, sb)
        gate_w = sb("gate_w", [P, DC, EXPERTS])
        xnT = sb("xnT", [P, DC, TOKENS])
        sums = sb("sums", [P, DC, BATCH])
        BE = [1, BATCH, EXPERTS]
        rank_of, index_of = sb("rank_of", [1, 1, EXPERTS]), sb("index_of", [1, 1, EXPERTS])
        prob, eq, key, picked, rest, part = [sb(x, BE) for x in ("prob", "eq", "key", "picked", "rest", "part")]
        top, best, total = [sb(x, [1, BATCH, 1]) for x in ("top", "best", "total")]
        chosen, chosen_f = sb("chosen", [1, BATCH * TOP], I32), sb("chosen_f", [1, BATCH, TOP])
        weight = sb("weight", [1, BATCH, TOP])
        weights = sb("weights", [P, BATCH * TOP])
        slots = sb("slots", [P, ROUND_BATCHES * TOP, PACKED])
        gelu = sb("gelu", [P, 2, 2, SEQ])
        hid = sb("hid", [P, 2 * TOP, 2, SEQ])

        gate_loaded, zeroed = sem("gate_loaded"), sem("zeroed")
        names = ("var_ready r0_ready xn_ready xnT_ready xnT_copied dve_done").split()
        N = {x: sem(x) for x in names}
        logits_ready, exp_ready, shifted, weight_ready, spread_ready, route_done = [
            sem(x) for x in ("logits_ready", "exp_ready", "shifted", "weight_ready", "spread_ready", "route_done")]
        names = ("hidden_ready gelu_done hid_ready out_ready added stored").split()
        S = {x: sem(x) for x in names}
        slot_loaded = [sem(f"slot_loaded{j}") for j in range(ROUND_BATCHES * TOP)]

        with nc.Block() as block:
            @block.sync
            def _(sp):
                sp.dma_start(gate_w[:], w_gate.rearrange("(c p) e -> p c e", p=P)).then_inc(gate_loaded, 16)

        with nc.Fori(0, GROUPS) as i:
            with nc.Block() as block:
                @block.vector
                def _(dve):
                    done = [0]

                    def link(ins):
                        done[0] += 1
                        ins.then_inc(N["dve_done"], 1)
                        dve.wait_ge(N["dve_done"], done[0])

                    x_tile = lambda t: r.x[:, bass.ds(i * GROUP_TILES + t, 1), :].rearrange("p a d -> p (a d)")
                    norm_vector(nc, dve, link, n, x_tile, N["var_ready"], N["r0_ready"], N["xn_ready"])
                    for c in range(DC):
                        dve.wait_ge(N["xnT_copied"], c + 1)
                        nc.vector.reduce_sum(sums[:, c, bass.ds(i * GROUP_BATCHES, GROUP_BATCHES)],
                                             ps[:, c, :].rearrange("p (b t) -> p b t", b=GROUP_BATCHES), AX_X)

                @block.scalar
                def _(act):
                    norm_scalar(nc, act, n, N["var_ready"], N["r0_ready"])
                    act.wait_ge(N["xnT_ready"], 1)
                    for c in range(DC):
                        nc.scalar.copy(xnT[:, c, bass.ds(i * GROUP, GROUP)], ps[:, c, :]
                                       ).then_inc(N["xnT_copied"], 1)

                @block.tensor
                def _(pe):
                    norm_tensor(nc, pe, n, r.ident, [ps[:, 0, :], ps[:, 1, :]], N["xn_ready"], N["xnT_ready"])
            end_of_round(nc, list(N.values()))

        with nc.Block() as block:
            @block.tensor
            def _(pe):
                pe.wait_ge(gate_loaded, 16)
                for b in range(BATCH):
                    for c in range(DC):
                        mm = nc.tensor.matmul(ps[0:1, 0, b * EXPERTS:(b + 1) * EXPERTS], sums[:, c, b:b + 1],
                                              gate_w[:, c, :], start=(c == 0), stop=(c == DC - 1))
                mm.then_inc(logits_ready, 1)
                pe.wait_ge(weight_ready, 1)
                nc.tensor.matmul(ps[:, 1, 0:BATCH * TOP], r.ones_row[:], weight[:].rearrange("o b k -> o (b k)"),
                                 start=True, stop=True).then_inc(spread_ready, 1)

            @block.scalar
            def _(act):
                act.wait_ge(shifted, 1)
                nc.scalar.activation(prob[:], prob[:], ACT.Exp, scale=1.0 / SEQ).then_inc(exp_ready, 1)

            @block.gpsimd
            def _(pool):
                nc.gpsimd.memset(hid[:], 0.0)
                nc.gpsimd.iota(index_of[:], pattern=[[1, EXPERTS]], base=0, channel_multiplier=0,
                               allow_small_or_imprecise_dtypes=True)
                nc.gpsimd.iota(rank_of[:], pattern=[[-1, EXPERTS]], base=EXPERTS, channel_multiplier=0,
                               allow_small_or_imprecise_dtypes=True).then_inc(zeroed, 1)

            @block.vector
            def _(dve):
                done = [0]

                def link(ins):
                    done[0] += 1
                    ins.then_inc(route_done, 1)
                    dve.wait_ge(route_done, done[0])

                dve.wait_ge(logits_ready, 1)
                dve.wait_ge(zeroed, 1)
                logits = ps[0:1, 0, 0:BATCH * EXPERTS].rearrange("o (b e) -> o b e", b=BATCH)
                link(nc.vector.reduce_max(top[:], logits, AX_X))
                nc.vector.tensor_tensor(prob[:], logits, top[:].to_broadcast(BE), ALU.subtract).then_inc(shifted, 1)
                dve.wait_ge(exp_ready, 1)
                link(nc.vector.reduce_sum(total[:], prob[:], AX_X))
                link(nc.vector.reciprocal(total[:], total[:]))
                link(nc.vector.tensor_tensor(prob[:], prob[:], total[:].to_broadcast(BE), ALU.mult))

                def pick(values, k):
                    link(nc.vector.reduce_max(top[:], values[:], AX_X))
                    link(nc.vector.tensor_tensor(eq[:], values[:], top[:].to_broadcast(BE), ALU.is_equal))
                    link(nc.vector.tensor_tensor(key[:], eq[:], rank_of[:].to_broadcast(BE), ALU.mult))
                    link(nc.vector.reduce_max(best[:], key[:], AX_X))
                    link(nc.vector.tensor_tensor(picked[:], key[:], best[:].to_broadcast(BE), ALU.is_equal))
                    link(nc.vector.tensor_tensor(part[:], picked[:], index_of[:].to_broadcast(BE), ALU.mult))
                    link(nc.vector.reduce_sum(chosen_f[:, :, k:k + 1], part[:], AX_X))
                    link(nc.vector.tensor_copy(weight[:, :, k:k + 1], top[:]))

                pick(prob, 0)
                link(nc.vector.scalar_tensor_tensor(rest[:], picked[:], -4.0, prob[:], ALU.mult, ALU.add))
                pick(rest, 1)
                link(nc.vector.reduce_sum(total[:], weight[:], AX_X))
                link(nc.vector.reciprocal(total[:], total[:]))
                nc.vector.tensor_tensor(weight[:], weight[:], total[:].to_broadcast([1, BATCH, TOP]),
                                        ALU.mult).then_inc(weight_ready, 1)
                nc.vector.tensor_copy(chosen[:], chosen_f[:].rearrange("o b k -> o (b k)"))
                dve.wait_ge(spread_ready, 1)
                nc.vector.tensor_copy(weights[:], ps[:, 1, 0:BATCH * TOP])

        with nc.Fori(0, BATCH // ROUND_BATCHES) as i:
            with nc.Block() as block:
                @block.sync
                def _(sp):
                    for j in range(ROUND_BATCHES * TOP):
                        e = sp.value_load(chosen[0:1, bass.ds(i * ROUND_BATCHES * TOP + j, 1)],
                                          min_val=0, max_val=EXPERTS - 1)
                        sp.dma_start(slots[:, j, :], packed[bass.ds(e, 1)].rearrange("e p n -> p (e n)")
                                     ).then_inc(slot_loaded[j], 16)
                    for b in range(ROUND_BATCHES):
                        sp.wait_ge(S["added"], 2 * (b + 1))
                        sp.dma_start(out[bass.ds(i * ROUND_BATCHES + b, 1)].rearrange("b (h p) d -> p (b h) d", p=P),
                                     r.x[:, bass.ds(i * ROUND_BATCHES * 2 + 2 * b, 2), :]).then_inc(S["stored"], 16)
                    sp.wait_ge(S["stored"], 16 * ROUND_BATCHES)

                @block.tensor
                def _(pe):
                    def hidden(j):
                        pe.wait_ge(slot_loaded[j], 16)
                        if j >= 4:
                            pe.wait_ge(S["gelu_done"], 2 * (j - 3))
                        for m, rows in enumerate((P, FF1)):
                            for c in range(DC):
                                mm = nc.tensor.matmul(
                                    ps[0:rows, HIDDEN[j % 4], m * SEQ:(m + 1) * SEQ],
                                    slots[:, j, c * FF + m * P:c * FF + m * P + rows],
                                    xnT[:, c, bass.ds((i * ROUND_BATCHES + j // TOP) * SEQ, SEQ)],
                                    start=(c == 0), stop=(c == DC - 1))
                        mm.then_inc(S["hidden_ready"], 1)

                    def down(b):
                        pe.wait_ge(S["hid_ready"], TOP * (b + 1))
                        for t in range(2):
                            job = 2 * b + t
                            if job >= 2:
                                pe.wait_ge(S["added"], job - 1)
                            for k in range(TOP):
                                j = b * TOP + k
                                cols = slice(t * P, (t + 1) * P)
                                nc.tensor.matmul(ps[:, OUT[job % 2], 0:HID], hid[:, j % 4, 0, cols],
                                                 slots[:, j, W2_AT:W2_AT + HID], start=(k == 0), stop=False)
                                mm = nc.tensor.matmul(ps[:, OUT[job % 2], 0:HID], hid[:, j % 4, 1, cols],
                                                      slots[:, j, W2_AT + HID:W2_AT + 2 * HID],
                                                      start=False, stop=(k == TOP - 1))
                            mm.then_inc(S["out_ready"], 1)

                    for b in range(ROUND_BATCHES + 1):
                        if b < ROUND_BATCHES:
                            for k in range(TOP):
                                hidden(b * TOP + k)
                        if b >= 1:
                            down(b - 1)

                @block.scalar
                def _(act):
                    for j in range(ROUND_BATCHES * TOP):
                        act.wait_ge(S["hidden_ready"], j + 1)
                        if j >= 2:
                            act.wait_ge(S["hid_ready"], j - 1)
                        for m, rows in enumerate((P, FF1)):
                            nc.scalar.activation(gelu[0:rows, j % 2, m, :], ps[0:rows, HIDDEN[j % 4], m * SEQ:(m + 1) * SEQ],
                                                 ACT.Gelu, bias=slots[0:rows, j, B1_AT + m:B1_AT + m + 1]
                                                 ).then_inc(S["gelu_done"], 1)

                @block.vector
                def _(dve):
                    def weighted(j):
                        dve.wait_ge(S["gelu_done"], 2 * (j + 1))
                        if j >= 4:
                            dve.wait_ge(S["out_ready"], 2 * ((j - 4) // TOP + 1))
                        w_at = i * ROUND_BATCHES * TOP + j
                        nc.vector.tensor_scalar(hid[:, j % 4, 0, :], gelu[:, j % 2, 0, :],
                                                weights[:, bass.ds(w_at, 1)], None, ALU.mult)
                        nc.vector.tensor_copy(hid[BIAS_ROW:BIAS_ROW + 1, j % 4, 1, :],
                                              weights[BIAS_ROW:BIAS_ROW + 1, bass.ds(w_at, 1)].to_broadcast([1, SEQ]))
                        nc.vector.tensor_scalar(hid[0:FF1, j % 4, 1, :], gelu[0:FF1, j % 2, 1, :],
                                                weights[0:FF1, bass.ds(w_at, 1)], None, ALU.mult
                                                ).then_inc(S["hid_ready"], 1)

                    def add(b):
                        for t in range(2):
                            job = 2 * b + t
                            dve.wait_ge(S["out_ready"], job + 1)
                            xt = r.x[:, bass.ds(i * ROUND_BATCHES * 2 + job, 1), :].rearrange("p a d -> p (a d)")
                            nc.vector.tensor_tensor(xt, xt, ps[:, OUT[job % 2], 0:HID], ALU.add
                                                    ).then_inc(S["added"], 1)

                    for b in range(ROUND_BATCHES + 1):
                        if b < ROUND_BATCHES:
                            for k in range(TOP):
                                weighted(b * TOP + k)
                        if b >= 1:
                            add(b - 1)
            end_of_round(nc, list(S.values()) + slot_loaded)


def build(nc, a, out):
    with ExitStack() as ctx:
        r = Resident(nc, ctx)
        setup(nc, a["hidden"], r)
        attention(nc, r, a["A_q"], a["A_k"], a["A_v"], a["A_o"], a["A_bo"])
        experts(nc, r, a["B_g"], a["B_u"], a["B_d"], a["B_ga"], a["B_gb"], a["B_ua"], a["B_ub"], a["B_da"],
                a["B_db"], a["B_r"], a["B_temp"])
        delta(nc, r, a["C_q"], a["C_k"], a["C_v"], a["C_a"], a["C_b"], a["C_g"], a["C_o"], a["C_cq"], a["C_ck"],
              a["C_cv"], a["C_alog"], a["C_dt"], a["C_nw"])
        routed(nc, r, a["D_packed"], a["D_gate"], out)


def kernel(**inputs):
    import numpy as np
    import concourse.bacc as bacc
    from concourse.bass_utils import run_bass_kernel_spmd

    def layer(prefix):
        return {k[len(prefix):]: np.asarray(v) for k, v in inputs.items() if k.startswith(prefix)}

    A, B, C, D = layer("L0_attn_"), layer("L0_ffn_"), layer("L1_attn_"), layer("L1_ffn_")
    packed = np.zeros((EXPERTS, P, PACKED), D["W1"].dtype)
    for c in range(DC):
        packed[:, :, c * FF:(c + 1) * FF] = D["W1"][:, c * P:(c + 1) * P, :]
    packed[:, :, W2_AT:W2_AT + HID] = D["W2"][:, 0:P, :]
    packed[:, 0:FF1, W2_AT + HID:W2_AT + 2 * HID] = D["W2"][:, P:FF, :]
    packed[:, BIAS_ROW, W2_AT + HID:W2_AT + 2 * HID] = D["b2"]
    packed[:, :, B1_AT] = D["b1"][:, 0:P]
    packed[:, 0:FF1, B1_AT + 1] = D["b1"][:, P:FF]
    arrays = {
        "hidden": A["hidden_states"],
        "A_q": A["Wq"].T, "A_k": A["Wk"].T, "A_v": A["Wv"].T, "A_o": A["Wo"].T, "A_bo": A["bo"],
        "B_g": B["Wg"], "B_u": B["Wu"], "B_d": B["Wd"],
        "B_ga": B["Ga"].transpose(0, 2, 1), "B_gb": B["Gb"], "B_ua": B["Ua"].transpose(0, 2, 1), "B_ub": B["Ub"],
        "B_da": B["Da"].transpose(0, 2, 1), "B_db": B["Db"], "B_r": B["Wr"], "B_temp": B["temperature"],
        "C_q": C["Wq"], "C_k": C["Wk"], "C_v": C["Wv"], "C_a": C["Wa"], "C_b": C["Wb"], "C_g": C["Wg"],
        "C_o": C["Wo"], "C_cq": C["conv_wq"], "C_ck": C["conv_wk"], "C_cv": C["conv_wv"], "C_alog": C["A_log"],
        "C_dt": C["dt_bias"], "C_nw": C["norm_weight"],
        "D_packed": packed, "D_gate": D["gate_W"].T,
    }
    nc = bacc.Bacc("TRN2", target_bir_lowering=False, num_devices=1)
    arrays = {"in_" + k: np.ascontiguousarray(v) for k, v in arrays.items()}
    dram = {k[3:]: nc.dram_tensor(k, v.shape, mybir.dt.from_np(v.dtype), kind="ExternalInput").ap()
            for k, v in arrays.items()}
    out = nc.dram_tensor("out", (BATCH, SEQ, HID), F32, kind="ExternalOutput").ap()
    build(nc, dram, out)
    return run_bass_kernel_spmd(nc, [arrays], core_ids=[0]).results[0]["out"]
```

```python
import math
from contextlib import ExitStack

import concourse.bass as bass
from concourse import mybir
from concourse.alu_op_type import AluOpType as ALU

ACT = mybir.ActivationFunctionType
F32 = mybir.dt.float32
BF16 = mybir.dt.bfloat16
F32R = mybir.dt.float32r
I32 = mybir.dt.int32
AX_X = mybir.AxisListType.X

P = 128
BATCH, SEQ, HID = 8, 256, 256
TOKENS = BATCH * SEQ
TILES = TOKENS // P
DC = HID // P
GROUP_TILES = 4
GROUP = GROUP_TILES * P
GROUPS = TOKENS // GROUP
GROUP_BATCHES = GROUP // SEQ
LN_EPS = 1e-5
NEG = -1e30


class Resident:

    def __init__(self, nc, ctx):
        def sb(name, shape, dt=F32):
            return ctx.enter_context(nc.sbuf_tensor(name, shape, dt))

        self.x = sb("x", [P, TILES, HID])
        self.ident = sb("ident", [P, P])
        self.ident_bf = sb("ident_bf", [P, P], BF16)
        self.causal_bf = sb("causal_bf", [P, 2, P], BF16)
        self.ones_row = sb("ones_row", [1, P])
        self.first_xnT = sb("first_xnT", [P, DC, GROUP])
        self.x_loaded = [ctx.enter_context(nc.semaphore(f"x_loaded{g}")) for g in range(GROUPS)]

    def load_group(self, sp, hidden, g):
        sp.dma_start(self.x[:, g * GROUP_TILES:(g + 1) * GROUP_TILES, :],
                     hidden[g * GROUP_BATCHES:(g + 1) * GROUP_BATCHES].rearrange("b (h p) d -> p (b h) d", p=P)
                     ).then_inc(self.x_loaded[g], 16)


def end_of_round(nc, sems):
    nums = sorted(s.num for s in sems)
    while nums:
        n = 1
        while n < len(nums) and nums[n] == nums[0] + n:
            n += 1
        nc.gpsimd.sem_clear(range(nums[0], nums[0] + n))
        nums = nums[n:]
    nc.all_engine_barrier()


def setup(nc, hidden, r):
    with ExitStack() as ctx:
        zeroed = ctx.enter_context(nc.semaphore("zeroed"))
        with nc.Block() as block:
            @block.sync
            def _(sp):
                r.load_group(sp, hidden, 0)

            @block.gpsimd
            def _(pool):
                nc.gpsimd.memset(r.ident[:], 0.0)
                nc.gpsimd.memset(r.ident_bf[:], 0.0)
                nc.gpsimd.memset(r.ones_row[:], 1.0)
                nc.gpsimd.memset(r.causal_bf[:], 0.0).then_inc(zeroed, 1)
                pool.wait_ge(zeroed, 1)
                for m in (r.ident, r.ident_bf):
                    nc.gpsimd.affine_select(out=m[:], in_=m[:], compare_op=ALU.not_equal, fill=1.0, base=0,
                                            pattern=[[-1, P]], channel_multiplier=1)
                nc.gpsimd.affine_select(out=r.causal_bf[:], in_=r.causal_bf[:], compare_op=ALU.is_ge, fill=NEG,
                                        base=0, pattern=[[0, 2], [-1, P]], channel_multiplier=1)
        end_of_round(nc, [zeroed])


class Ahead:

    NAMES = "ln_chain ln_var_ready ln_root_ready ln_xn_ready ln_turned ln_high_ready ln_taken"

    def __init__(self, nc, ctx, first_xnT):
        def sb(name, shape, dt=F32):
            return ctx.enter_context(nc.sbuf_tensor("ln_" + name, shape, dt))

        self.nc = nc
        self.stats = sb("stats", [P, GROUP_TILES, 6])
        self.mv = sb("mv", [P, GROUP_TILES, 2])
        self.veps, self.lnv, self.r0, self.t = [sb(x, [P, GROUP_TILES]) for x in ("veps", "lnv", "r0", "t")]
        self.xn = sb("xn", [P, GROUP_TILES, HID])
        self.xnT = [first_xnT]
        self.high, self.low = [[sb(x, [P, DC, GROUP], F32R)] for x in ("high", "low")]

    def add_slot(self, ctx):
        for parts, name, dt in ((self.xnT, "xnT1", F32), (self.high, "high1", F32R), (self.low, "low1", F32R)):
            parts.append(ctx.enter_context(self.nc.sbuf_tensor("ln_" + name, [P, DC, GROUP], dt)))

    def sems(self, sem):
        return {x: sem(x) for x in self.NAMES.split()}

    def statistics(self, dve, S, x_tile):
        nc = self.nc
        for t in range(GROUP_TILES):
            last = nc.vector.bn_stats(self.stats[:, t, :], x_tile(t))
        last.then_inc(S["ln_chain"], 1)
        dve.wait_ge(S["ln_chain"], 1)
        for t in range(GROUP_TILES):
            last = nc.vector.bn_aggr(self.mv[:, t, :], self.stats[:, t, :])
        last.then_inc(S["ln_chain"], 1)
        dve.wait_ge(S["ln_chain"], 2)
        nc.vector.tensor_scalar(self.veps[:], self.mv[:, :, 1], LN_EPS, None, ALU.add).then_inc(S["ln_var_ready"], 1)

    def root(self, act, S):
        nc = self.nc
        nc.scalar.preload_act_table_set("natural_log_exp_and_others")
        act.wait_ge(S["ln_var_ready"], 1)
        nc.scalar.activation(self.lnv[:], self.veps[:], ACT.Ln).then_inc(S["ln_root_ready"], 1)
        act.wait_ge(S["ln_root_ready"], 1)
        nc.scalar.activation(self.r0[:], self.lnv[:], ACT.Exp, scale=-0.5).then_inc(S["ln_root_ready"], 1)

    def normalise(self, dve, S, x_tile):
        nc, t = self.nc, self.t
        dve.wait_ge(S["ln_root_ready"], 2)
        nc.vector.tensor_tensor(t[:], self.r0[:], self.r0[:], ALU.mult).then_inc(S["ln_chain"], 1)
        dve.wait_ge(S["ln_chain"], 3)
        nc.vector.tensor_tensor(t[:], t[:], self.veps[:], ALU.mult).then_inc(S["ln_chain"], 1)
        dve.wait_ge(S["ln_chain"], 4)
        nc.vector.tensor_scalar(t[:], t[:], -0.5, 1.5, ALU.mult, ALU.add).then_inc(S["ln_chain"], 1)
        dve.wait_ge(S["ln_chain"], 5)
        nc.vector.tensor_tensor(t[:], t[:], self.r0[:], ALU.mult).then_inc(S["ln_chain"], 1)
        dve.wait_ge(S["ln_chain"], 6)
        for k in range(GROUP_TILES):
            nc.vector.tensor_scalar(self.xn[:, k, :], x_tile(k), self.mv[:, k, 0:1], t[:, k:k + 1],
                                    ALU.subtract, ALU.mult).then_inc(S["ln_xn_ready"], 1)

    def turn(self, pe, S, ident, bank, c):
        for t in range(GROUP_TILES):
            pe.wait_ge(S["ln_xn_ready"], t + 1)
            mm = self.nc.tensor.transpose(bank[:, t * P:(t + 1) * P], self.xn[:, t, c * P:(c + 1) * P], ident[:])
        mm.then_inc(S["ln_turned"], 1)

    def take_high(self, act, S, bank, c, slot):
        act.wait_ge(S["ln_turned"], c + 1)
        self.nc.scalar.copy(self.high[slot][:, c, :], bank).then_inc(S["ln_high_ready"], 1)
        self.nc.scalar.copy(self.xnT[slot][:, c, :], bank).then_inc(S["ln_high_ready"], 1)

    def take_low(self, dve, S, bank, c, slot):
        dve.wait_ge(S["ln_high_ready"], 2 * (c + 1))
        self.nc.vector.tensor_tensor(self.low[slot][:, c, :], bank, self.high[slot][:, c, :].bitcast(F32),
                                     ALU.subtract).then_inc(S["ln_taken"], 1)


def split_passes(a_high, a_low, b_high, b_low):
    return ((a_high, b_high), (a_high, b_low), (a_low, b_high))


NH, NKV, HD = 16, 4, 128
REP = NH // NKV
QW = 3 * P


def attention(nc, r, ahead, next_weights, hidden, w_q, w_k, w_v, w_o, b_o):
    with ExitStack() as ctx:
        def sb(name, shape, dt=F32):
            return ctx.enter_context(nc.sbuf_tensor("a_" + name, shape, dt))

        def sem(name):
            return ctx.enter_context(nc.semaphore("a_" + name))

        ps = ctx.enter_context(nc.psum_tensor("a_ps", [P, 8, 512], F32))
        PROJ, SC, PTB, OTB = (0, 1), (2, 3), (4, 5), (6, 7)

        QKV = NH * HD + 2 * NKV * HD
        K_AT, V_AT = NH * HD, NH * HD + NKV * HD
        w_high = sb("w_high", [P, DC, QKV], F32R)
        w_low = sb("w_low", [P, DC, QKV], F32R)
        wo_high, wo_low = sb("wo_high", [P, NH, HID], F32R), sb("wo_low", [P, NH, HID], F32R)
        wo = next_weights.raw[:, 1].rearrange("p e c f -> p (e c f)").rearrange("p (h n) -> p h n", n=HID)
        bo = sb("bo", [P, 1, HID])
        kT = sb("kT", [P, NKV, GROUP])
        qT = sb("qT", [P, 2, GROUP])
        v_rest = sb("v_rest", [P, GROUP_TILES // 2, NKV * HD])
        v_first = ahead.xn[:].rearrange("p t d -> p (t d)").rearrange("p (t n) -> p t n", n=NKV * HD)
        v = [half[:, t, :] for half in (v_first, v_rest) for t in range(GROUP_TILES // 2)]
        negmax = sb("negmax", [P, 2, GROUP_TILES])
        rowsum = sb("rowsum", [P, 2, GROUP_TILES])
        inv = sb("inv", [P, 2, GROUP_TILES])
        probs = sb("probs", [P, 2, GROUP_BATCHES, QW])
        pT = sb("pT", [P, 2, GROUP_BATCHES, QW])
        WCOLS = NKV * HD
        BLOCKS_AT = [K_AT, V_AT] + [j * WCOLS for j in range(NH // NKV)]

        w_loaded = [sem(f"w_loaded{j}") for j in range(len(BLOCKS_AT))]
        wo_loaded, bo_loaded, w_rounded, wo_rounded, wo_split = [
            sem(x) for x in ("wo_loaded", "bo_loaded", "w_rounded", "wo_rounded", "wo_split")]
        L = ahead.sems(sem)
        proj_ready, proj_taken = sem("proj_ready"), sem("proj_taken")
        scores_ready, max_ready, exp_ready, probs_ready = [
            sem(s) for s in ("scores_ready", "max_ready", "exp_ready", "probs_ready")]
        pT_ready, pT_copied, oT_ready, oT_copied = [
            sem(s) for s in ("pT_ready", "pT_copied", "oT_ready", "oT_copied")]
        bias_added, dve_done, oT_split = sem("bias_added"), sem("dve_done"), sem("oT_split")
        out_ready, out_taken = sem("out_ready"), sem("out_taken")
        round_sems = list(L.values()) + [proj_ready, proj_taken,
                      scores_ready, max_ready, exp_ready, probs_ready, pT_ready, pT_copied, oT_ready,
                      oT_copied, bias_added, dve_done, oT_split, out_ready, out_taken]

        def first_tile(t):
            return r.x[:, t, :]

        with nc.sbuf_tensor("a_raw", [P, len(BLOCKS_AT), DC, WCOLS], F32) as raw, nc.Block() as block:
            @block.sync
            def _(sp):
                for j, at in enumerate(BLOCKS_AT):
                    src, col = (w_k, 0) if at == K_AT else (w_v, 0) if at == V_AT else (w_q, at)
                    sp.dma_start(raw[:, j], src[:, col:col + WCOLS].rearrange("(c p) n -> p c n", p=P)
                                 ).then_inc(w_loaded[j], 16)
                for g in range(1, GROUPS):
                    r.load_group(sp, hidden, g)
                sp.dma_start(wo, w_o.rearrange("(h p) n -> p h n", p=P)).then_inc(wo_loaded, 16)
                sp.dma_start(bo[:, 0, :], b_o.rearrange("(a n) -> a n", a=1).to_broadcast([P, HID])
                             ).then_inc(bo_loaded, 16)
                next_weights.load(sp, 0)
                for g in range(GROUPS):
                    sp.wait_ge(r.x_loaded[g], 16)

            @block.vector
            def _(dve):
                dve.wait_ge(r.x_loaded[0], 16)
                ahead.statistics(dve, L, first_tile)
                ahead.normalise(dve, L, first_tile)
                for c in range(DC):
                    ahead.take_low(dve, L, ps[:, OTB[c], :], c, 0)
                for j, at in enumerate(BLOCKS_AT):
                    dve.wait_ge(w_rounded, j + 1)
                    nc.vector.tensor_tensor(w_low[:, :, at:at + WCOLS], raw[:, j],
                                            w_high[:, :, at:at + WCOLS].bitcast(F32), ALU.subtract)

            @block.scalar
            def _(act):
                ahead.root(act, L)
                for j in range(2):
                    act.wait_ge(w_loaded[j], 16)
                    nc.scalar.copy(w_high[:, :, BLOCKS_AT[j]:BLOCKS_AT[j] + WCOLS], raw[:, j]).then_inc(w_rounded, 1)
                for c in range(DC):
                    ahead.take_high(act, L, ps[:, OTB[c], :], c, 0)
                for j in range(2, len(BLOCKS_AT)):
                    act.wait_ge(w_loaded[j], 16)
                    nc.scalar.copy(w_high[:, :, BLOCKS_AT[j]:BLOCKS_AT[j] + WCOLS], raw[:, j]).then_inc(w_rounded, 1)

            @block.tensor
            def _(pe):
                for c in range(DC):
                    ahead.turn(pe, L, r.ident, ps[:, OTB[c], :], c)
        end_of_round(nc, list(L.values()) + w_loaded + [w_rounded])

        HALF = NH // 2
        oT = sb("oT", [P, 2, HALF, GROUP], F32R)
        KV_JOBS = NKV + GROUP_TILES

        def chunk(b, half):
            t = 2 * b + half
            return slice(t * P, (t + 1) * P)

        BETWEEN = HALF + 1
        SPLITS = 4
        SPLIT_HEADS = NH // SPLITS

        def round_(i, following, split_weights=False):
            with nc.Block() as block:
                @block.sync
                def _(sp):
                    if split_weights:
                        sp.wait_ge(wo_split, SPLITS)
                        next_weights.load(sp, 1)

                @block.vector
                def _(dve):
                    done = [0]

                    def link(ins):
                        done[0] += 1
                        ins.then_inc(dve_done, 1)
                        dve.wait_ge(dve_done, done[0])

                    def x_tile(t):
                        return r.x[:, bass.ds(i * GROUP_TILES + t, 1), :].rearrange("p a d -> p (a d)")

                    def next_tile(t):
                        return r.x[:, bass.ds(following * GROUP_TILES + t, 1), :].rearrange("p a d -> p (a d)")

                    def maxima(h):
                        for b in range(GROUP_BATCHES):
                            dve.wait_ge(scores_ready, 2 * h + b + 1)
                            nc.vector.tensor_reduce(negmax[:, h % 2, 2 * b:2 * b + 1], ps[:, SC[b], 0:P],
                                                    AX_X, ALU.max, negate=True)
                            nc.vector.tensor_reduce(negmax[:, h % 2, 2 * b + 1:2 * b + 2], ps[:, SC[b], P:QW],
                                                    AX_X, ALU.max, negate=True).then_inc(max_ready, 1)

                    def copy_pT(h):
                        for b in range(GROUP_BATCHES):
                            dve.wait_ge(pT_ready, 2 * h + b + 1)
                            if h >= 2:
                                dve.wait_ge(oT_ready, h - 1)
                            nc.vector.tensor_copy(pT[:, h % 2, b, :], ps[:, PTB[b], 0:QW]).then_inc(pT_copied, 1)

                    def normalise(h):
                        dve.wait_ge(exp_ready, 2 * h + 2)
                        link(nc.vector.reciprocal(inv[:, h % 2, :], rowsum[:, h % 2, :]))
                        for b in range(GROUP_BATCHES):
                            nc.vector.tensor_scalar(probs[:, h % 2, b, 0:P], probs[:, h % 2, b, 0:P],
                                                    inv[:, h % 2, 2 * b:2 * b + 1], None, ALU.mult)
                            nc.vector.tensor_scalar(probs[:, h % 2, b, P:QW], probs[:, h % 2, b, P:QW],
                                                    inv[:, h % 2, 2 * b + 1:2 * b + 2], None,
                                                    ALU.mult).then_inc(probs_ready, 1)

                    def split_oT(h):
                        dve.wait_ge(oT_copied, h + 1)
                        nc.vector.tensor_tensor(oT[:, 1, h % HALF, :], ps[:, OTB[h % 2], :],
                                                oT[:, 0, h % HALF, :].bitcast(F32), ALU.subtract).then_inc(oT_split, 1)

                    def add_out(job):
                        t = job % GROUP_TILES
                        dve.wait_ge(out_ready, job + 1)
                        if job >= GROUP_TILES:
                            dve.wait_ge(out_taken, t + 1)
                        nc.vector.tensor_tensor(x_tile(t), x_tile(t), ps[:, PROJ[t % 2], 0:HID],
                                                ALU.add).then_inc(out_taken, 1)

                    def weight_lows(k):
                        heads = slice(k * SPLIT_HEADS, (k + 1) * SPLIT_HEADS)
                        dve.wait_ge(wo_rounded, k + 1)
                        nc.vector.tensor_tensor(wo_low[:, heads, :], wo[:, heads, :],
                                                wo_high[:, heads, :].bitcast(F32), ALU.subtract).then_inc(wo_split, 1)

                    for h in range(NH):
                        maxima(h)
                        if h >= 1:
                            copy_pT(h - 1)
                        normalise(h)
                        if h >= 2:
                            split_oT(h - 2)
                        if split_weights and 0 <= h - 4 < SPLITS:
                            weight_lows(h - 4)
                        if h == BETWEEN:
                            dve.wait_ge(bias_added, 1)
                            for t in range(GROUP_TILES):
                                add_out(t)
                    split_oT(NH - 2)
                    copy_pT(NH - 1)
                    split_oT(NH - 1)
                    ahead.statistics(dve, L, next_tile)
                    ahead.normalise(dve, L, next_tile)
                    for t in range(GROUP_TILES):
                        if t == 2:
                            for c in range(DC):
                                ahead.take_low(dve, L, ps[:, SC[c], :], c, 0)
                        add_out(GROUP_TILES + t)

                @block.gpsimd
                def _(pool):
                    pool.wait_ge(bo_loaded, 16)
                    xg = r.x[:, bass.ds(i * GROUP_TILES, GROUP_TILES), :]
                    nc.gpsimd.tensor_tensor(xg, xg, bo[:].to_broadcast([P, GROUP_TILES, HID]),
                                            ALU.add).then_inc(bias_added, 1)

                @block.scalar
                def _(act):
                    def take(job, dst):
                        act.wait_ge(proj_ready, job + 1)
                        nc.scalar.copy(dst, ps[:, PROJ[job % 2], :]).then_inc(proj_taken, 1)

                    for g in range(NKV):
                        take(g, kT[:, g, :])
                    for t in range(GROUP_TILES):
                        take(NKV + t, v[t])
                    take(KV_JOBS, qT[:, 0, :])

                    def exps(h):
                        if h >= 2:
                            act.wait_ge(pT_ready, 2 * (h - 1))
                        for b in range(GROUP_BATCHES):
                            act.wait_ge(max_ready, 2 * h + b + 1)
                            nc.scalar.activation(probs[:, h % 2, b, 0:P], ps[:, SC[b], 0:P], ACT.Exp,
                                                 bias=negmax[:, h % 2, 2 * b:2 * b + 1],
                                                 accum_out=rowsum[:, h % 2, 2 * b:2 * b + 1])
                            nc.scalar.activation(probs[:, h % 2, b, P:QW], ps[:, SC[b], P:QW], ACT.Exp,
                                                 bias=negmax[:, h % 2, 2 * b + 1:2 * b + 2],
                                                 accum_out=rowsum[:, h % 2, 2 * b + 1:2 * b + 2]
                                                 ).then_inc(exp_ready, 1)

                    def copy_oT(h):
                        act.wait_ge(oT_ready, h + 1)
                        if h >= HALF:
                            act.wait_ge(out_ready, GROUP_TILES)
                        nc.scalar.copy(oT[:, 0, h % HALF, :], ps[:, OTB[h % 2], :]).then_inc(oT_copied, 1)

                    def weight_highs(k):
                        heads = slice(k * SPLIT_HEADS, (k + 1) * SPLIT_HEADS)
                        act.wait_ge(wo_loaded, 16)
                        nc.scalar.copy(wo_high[:, heads, :], wo[:, heads, :]).then_inc(wo_rounded, 1)

                    for h in range(NH):
                        exps(h)
                        if h + 1 < NH:
                            take(KV_JOBS + h + 1, qT[:, (h + 1) % 2, :])
                        if h >= 1:
                            copy_oT(h - 1)
                        if split_weights and 0 <= h - 3 < SPLITS:
                            weight_highs(h - 3)
                    copy_oT(NH - 1)
                    ahead.root(act, L)
                    for c in range(DC):
                        ahead.take_high(act, L, ps[:, SC[c], :], c, 0)

                @block.tensor
                def _(pe):
                    def bank_free(job):
                        if job >= 2:
                            pe.wait_ge(proj_taken, job - 1)

                    high, low = ahead.high[0], ahead.low[0]

                    def project(job, at):
                        bank_free(job)
                        cols = slice(at, at + P)
                        passes = [p for c in range(DC) for p in split_passes(
                            w_high[:, c, cols], w_low[:, c, cols], high[:, c, :], low[:, c, :])]
                        for j, (wpart, xpart) in enumerate(passes):
                            mm = nc.tensor.matmul(ps[:, PROJ[job % 2], :], wpart, xpart,
                                                  start=(j == 0), stop=(j == len(passes) - 1))
                        mm.then_inc(proj_ready, 1)

                    for g in range(NKV):
                        project(g, K_AT + g * HD)
                    for t in range(GROUP_TILES):
                        bank_free(NKV + t)
                        rows, cols = slice(t * P, (t + 1) * P), slice(V_AT, V_AT + NKV * HD)
                        passes = [p for c in range(DC) for p in split_passes(
                            high[:, c, rows], low[:, c, rows], w_high[:, c, cols], w_low[:, c, cols])]
                        for j, (xpart, wpart) in enumerate(passes):
                            mm = nc.tensor.matmul(ps[:, PROJ[(NKV + t) % 2], :], xpart, wpart,
                                                  start=(j == 0), stop=(j == len(passes) - 1))
                        mm.then_inc(proj_ready, 1)

                    def queries(h):
                        if h > BETWEEN:
                            pe.wait_ge(out_taken, min(GROUP_TILES, h - BETWEEN + 2))
                        project(KV_JOBS + h, h * HD)

                    def scores(h):
                        pe.wait_ge(proj_taken, KV_JOBS + h + 1)
                        for b in range(GROUP_BATCHES):
                            if h >= 1:
                                pe.wait_ge(exp_ready, 2 * (h - 1) + b + 1)
                            q, k = qT[:, h % 2, :], kT[:, h // REP, :]
                            diagonals = ps[:, SC[b], 0:4 * P].rearrange("p (s k) -> p s k", k=P)[:, 0:3:2, :]
                            nc.tensor.matmul(diagonals, r.ident_bf[:], r.causal_bf[:], start=True, stop=False,
                                             skip_group_check=True)
                            nc.tensor.matmul(ps[:, SC[b], 0:P], q[:, chunk(b, 0)], k[:, chunk(b, 0)],
                                             start=False, stop=True, skip_group_check=True)
                            nc.tensor.matmul(ps[:, SC[b], P:QW], q[:, chunk(b, 1)],
                                             k[:, 2 * b * P:(2 * b + 2) * P], start=False, stop=True,
                                             skip_group_check=True).then_inc(scores_ready, 1)

                    def turn(h):
                        for b in range(GROUP_BATCHES):
                            pe.wait_ge(probs_ready, 2 * h + b + 1)
                            if h >= 1:
                                pe.wait_ge(pT_copied, 2 * (h - 1) + b + 1)
                            for s in range(3):
                                mm = nc.tensor.transpose(ps[:, PTB[b], s * P:(s + 1) * P],
                                                         probs[:, h % 2, b, s * P:(s + 1) * P], r.ident[:])
                            mm.then_inc(pT_ready, 1)

                    def values(h):
                        if h >= 2:
                            pe.wait_ge(oT_split, h - 1)
                        g = slice((h // REP) * HD, (h // REP + 1) * HD)
                        for b in range(GROUP_BATCHES):
                            pe.wait_ge(pT_copied, 2 * h + b + 1)
                            out = ps[:, OTB[h % 2], 2 * b * P:(2 * b + 2) * P]
                            nc.tensor.matmul(out, v[2 * b][:, g], pT[:, h % 2, b, 0:2 * P], start=True, stop=False)
                            mm = nc.tensor.matmul(out[:, P:2 * P], v[2 * b + 1][:, g], pT[:, h % 2, b, 2 * P:QW],
                                                  start=False, stop=True)
                        mm.then_inc(oT_ready, 1)

                    def project_out(job):
                        t, first_head = job % GROUP_TILES, job // GROUP_TILES * HALF
                        if t >= 2:
                            pe.wait_ge(out_taken, job - 1)
                        rows = slice(t * P, (t + 1) * P)
                        for k in range(HALF):
                            pe.wait_ge(oT_split, first_head + k + 1)
                            passes = split_passes(oT[:, 0, k, rows], oT[:, 1, k, rows],
                                                  wo_high[:, first_head + k, :], wo_low[:, first_head + k, :])
                            for j, (opart, wpart) in enumerate(passes):
                                mm = nc.tensor.matmul(ps[:, PROJ[t % 2], 0:HID], opart, wpart,
                                                      start=(k == 0 and j == 0),
                                                      stop=(k == HALF - 1 and j == len(passes) - 1))
                        mm.then_inc(out_ready, 1)

                    queries(0)
                    scores(0)
                    queries(1)
                    for h in range(1, NH):
                        scores(h)
                        turn(h - 1)
                        if h == BETWEEN:
                            pe.wait_ge(wo_split, SPLITS)
                            for t in range(GROUP_TILES):
                                project_out(t)
                        if h + 1 < NH:
                            queries(h + 1)
                        values(h - 1)
                    turn(NH - 1)
                    values(NH - 1)
                    for t in range(GROUP_TILES):
                        if t == 2:
                            pe.wait_ge(exp_ready, 2 * NH)
                            for c in range(DC):
                                ahead.turn(pe, L, r.ident, ps[:, SC[c], :], c)
                        project_out(GROUP_TILES + t)
            end_of_round(nc, round_sems)

        round_(0, 1, split_weights=True)
        with nc.Fori(1, GROUPS - 1) as i:
            round_(i, i + 1)
        round_(GROUPS - 1, 0)
        end_of_round(nc, [wo_loaded, bo_loaded, wo_rounded, wo_split])


NE, FE, RANK, NLORA = 8, 256, 64, 2
FC = FE // P
GOLDEN_CENTER = 1.0 / math.e
GOLDEN_LOWER = 0.5 - math.log(4.0 / 3.0)
ZONE_LOW = math.log(GOLDEN_LOWER / (1.0 - GOLDEN_LOWER))
ZONE_HIGH = 1e-7


class GateUpWeights:

    def __init__(self, nc, ctx, Wg, Wu):
        self.sources = (Wg, Wu)
        self.raw = ctx.enter_context(nc.sbuf_tensor("gate_up_raw", [P, 2, NE, DC, FE], F32))
        self.loaded = [ctx.enter_context(nc.semaphore(f"gate_up_loaded{k}")) for k in range(2)]

    def load(self, sp, k):
        sp.dma_start(self.raw[:, k], self.sources[k].rearrange("e (c p) f -> p e c f", p=P)
                     ).then_inc(self.loaded[k], 16)


def experts(nc, r, ahead, gate_up_weights, Wd, Ga, Gb, Ua, Ub, Da, Db, Wr, temperature):
    with ExitStack() as ctx:
        def sb(name, shape, dt=F32):
            return ctx.enter_context(nc.sbuf_tensor("b_" + name, shape, dt))

        def sem(name):
            return ctx.enter_context(nc.semaphore("b_" + name))

        ps = ctx.enter_context(nc.psum_tensor("b_ps", [P, 8, 512], F32))
        GATE, UP, DOWN, TURN = (0, 1), (2, 3), (4, 5, 6), 7

        ahead.add_slot(ctx)
        raw = gate_up_weights.raw
        high = sb("high", [P, 2, NE, DC, FE], F32R)
        low = sb("low", [P, 2, NE, DC, FE], F32R)
        wd_high, wd_low = [sb(x, [P, NE, FC, HID], F32R) for x in ("wd_high", "wd_low")]
        wr = sb("wr", [P, DC, NE])
        temp = sb("temp", [P, 1])
        inv_temp = sb("inv_temp", [P, 1])
        rank_of = sb("rank_of", [P, NE])
        silu, product = [
            raw[:, 0].rearrange("p e c f -> p (e c f)")[:, k * FC * GROUP:(k + 1) * FC * GROUP].rearrange(
                "p (m t) -> p m t", t=GROUP) for k in range(2)]
        TE = [P, GROUP_TILES, NE]
        z, zone, ez, dist, zw, fb = [sb(s, TE) for s in ("z", "zone", "ez", "dist", "zw", "fb")]
        eq, key, first, second, rest, raw_w = [sb(s, TE) for s in ("eq", "key", "first", "second", "rest", "raw_w")]
        w = sb("w", [P, 2, GROUP_TILES, NE])
        top, best, total, none = [sb(s, [P, GROUP_TILES, 1]) for s in ("top", "best", "total", "none")]

        router_loaded, loaded, wd_loaded = sem("router_loaded"), sem("loaded"), sem("wd_loaded")
        lora_ready, lora_taken, split_done, setup_done, zeroed = [
            sem(s) for s in ("lora_ready", "lora_taken", "split_done", "setup_done", "zeroed")]
        L = ahead.sems(sem)
        R = {x: sem(x) for x in "logits_ready z_ready ez_ready dist_ready exps_ready route_chain".split()}
        gate_ready, up_ready, silu_ready, product_ready, mid_high_ready, mid_ready, down_ready, added = [
            sem(s) for s in ("gate_ready", "up_ready", "silu_ready", "product_ready", "mid_high_ready", "mid_ready",
                             "down_ready", "added")]
        round_sems = list(L.values()) + list(R.values()) + [gate_ready, up_ready, silu_ready, product_ready, mid_high_ready, mid_ready,
                                                            down_ready, added]

        class Router:

            def __init__(self, slot):
                self.slot, self.done = slot, 0

            def logits(self, pe):
                for t in range(GROUP_TILES):
                    for c in range(DC):
                        mm = nc.tensor.matmul(ps[:, TURN, t * NE:(t + 1) * NE],
                                              ahead.xnT[self.slot][:, c, t * P:(t + 1) * P], wr[:, c, :],
                                              start=(c == 0), stop=(c == DC - 1))
                mm.then_inc(R["logits_ready"], 1)

            def sigmoid(self, act):
                act.wait_ge(R["z_ready"], 1)
                nc.scalar.activation(ez[:], z[:], ACT.Exp, scale=-1.0).then_inc(R["ez_ready"], 1)

            def weightings(self, act):
                act.wait_ge(R["dist_ready"], 1)
                nc.scalar.activation(zw[:], dist[:], ACT.Exp, scale=-1.0 / 0.1).then_inc(R["exps_ready"], 1)
                nc.scalar.activation(fb[:], dist[:], ACT.Exp, scale=-1.0 / 0.3).then_inc(R["exps_ready"], 1)

            def link(self, dve, ins):
                self.done += 1
                ins.then_inc(R["route_chain"], 1)
                dve.wait_ge(R["route_chain"], self.done)

            def zones(self, dve):
                dve.wait_ge(R["logits_ready"], 1)
                self.link(dve, nc.vector.tensor_scalar(z[:].rearrange("p t e -> p (t e)"),
                                                       ps[:, TURN, 0:GROUP_TILES * NE], inv_temp[:, 0:1], None,
                                                       ALU.mult))
                nc.vector.tensor_scalar(zone[:], z[:], ZONE_LOW, None, ALU.is_ge).then_inc(R["z_ready"], 1)
                self.link(dve, nc.vector.tensor_scalar(eq[:], z[:], ZONE_HIGH, None, ALU.is_le))
                self.link(dve, nc.vector.tensor_tensor(zone[:], zone[:], eq[:], ALU.mult))

            def distances(self, dve):
                dve.wait_ge(R["ez_ready"], 1)
                self.link(dve, nc.vector.tensor_scalar(ez[:], ez[:], 1.0, None, ALU.add))
                self.link(dve, nc.vector.reciprocal(ez[:], ez[:]))
                self.link(dve, nc.vector.tensor_scalar(ez[:], ez[:], -GOLDEN_CENTER, None, ALU.add))
                nc.vector.scalar_tensor_tensor(dist[:], ez[:], -1.0, ez[:], ALU.mult, ALU.max
                                               ).then_inc(R["dist_ready"], 1)

            def in_zone(self, dve):
                dve.wait_ge(R["exps_ready"], 2)
                self.link(dve, nc.vector.tensor_tensor(zw[:], zw[:], zone[:], ALU.mult))
                self.link(dve, nc.vector.reduce_sum(total[:], zw[:], AX_X))
                self.link(dve, nc.vector.tensor_scalar(none[:], total[:], 1e-8, None, ALU.is_lt))

            def pick(self, dve, values, chosen):
                self.link(dve, nc.vector.reduce_max(top[:], values[:], AX_X))
                self.link(dve, nc.vector.tensor_tensor(eq[:], values[:], top[:].to_broadcast(TE), ALU.is_equal))
                self.link(dve, nc.vector.tensor_tensor(
                    key[:], eq[:], rank_of[:].rearrange("p (a e) -> p a e", a=1).to_broadcast(TE), ALU.mult))
                self.link(dve, nc.vector.reduce_max(best[:], key[:], AX_X))
                self.link(dve, nc.vector.tensor_tensor(chosen[:], key[:], best[:].to_broadcast(TE), ALU.is_equal))

            def pick_first(self, dve):
                self.pick(dve, fb, first)
                self.link(dve, nc.vector.scalar_tensor_tensor(rest[:], first[:], -4.0, fb[:], ALU.mult, ALU.add))

            def pick_second(self, dve):
                self.pick(dve, rest, second)
                self.link(dve, nc.vector.tensor_tensor(first[:], first[:], second[:], ALU.add))
                self.link(dve, nc.vector.tensor_tensor(fb[:], fb[:], first[:], ALU.mult))

            def normalised(self, dve, dst, a):
                self.link(dve, nc.vector.reduce_sum(total[:], a[:], AX_X))
                self.link(dve, nc.vector.tensor_scalar(total[:], total[:], 1e-8, None, ALU.max))
                self.link(dve, nc.vector.reciprocal(best[:], total[:]))
                self.link(dve, nc.vector.tensor_tensor(dst, a[:], best[:].to_broadcast(TE), ALU.mult))

            def fallback(self, dve):
                self.normalised(dve, fb[:], fb)
                self.link(dve, nc.vector.tensor_tensor(fb[:], fb[:], zw[:], ALU.subtract))
                self.link(dve, nc.vector.tensor_tensor(fb[:], fb[:], none[:].to_broadcast(TE), ALU.mult))
                self.link(dve, nc.vector.tensor_tensor(raw_w[:], zw[:], fb[:], ALU.add))

            def weights(self, dve):
                self.normalised(dve, w[:, self.slot], raw_w)

        first_router = Router(0)
        EXPERT_ORDER = list(range(NLORA, NE)) + list(range(NLORA))
        POOL_LOWS = 3

        def down_low(engine, eng, e):
            engine.wait_ge(split_done, 2 * NE + e + 1)
            eng.tensor_tensor(wd_low[:, EXPERT_ORDER[e]], wd[:, EXPERT_ORDER[e]],
                              wd_high[:, EXPERT_ORDER[e]].bitcast(F32), ALU.subtract)

        before_rounds = ExitStack()
        wd = before_rounds.enter_context(nc.sbuf_tensor("b_wd", [P, NE, FC, HID], F32))
        lora_a, lora_b = [before_rounds.enter_context(nc.sbuf_tensor("b_" + x, [RANK, 3, NLORA, FE], F32))
                          for x in ("lora_a", "lora_b")]
        with before_rounds, nc.Block() as block:
            @block.sync
            def _(sp):
                sp.dma_start(temp[:], temperature.rearrange("(a n) -> a n", a=1).to_broadcast([P, 1])
                             ).then_inc(router_loaded, 16)
                sp.dma_start(wr[:], Wr.rearrange("(c p) e -> p c e", p=P)).then_inc(router_loaded, 16)
                for k, (a, b) in enumerate(((Ga, Gb), (Ua, Ub), (Da, Db))):
                    sp.dma_start(lora_a[:, k], a.rearrange("l r d -> r l d")).then_inc(loaded, 16)
                    sp.dma_start(lora_b[:, k], b.rearrange("l r f -> r l f")).then_inc(loaded, 16)
                sp.dma_start(wd[:], Wd.rearrange("e (c p) f -> p e c f", p=P)).then_inc(wd_loaded, 16)

            @block.gpsimd
            def _(pool):
                nc.gpsimd.iota(rank_of[:], pattern=[[-1, NE]], base=NE, channel_multiplier=0,
                               allow_small_or_imprecise_dtypes=True).then_inc(setup_done, 1)
                for e in range(POOL_LOWS):
                    down_low(pool, nc.gpsimd, e)

            @block.tensor
            def _(pe):
                pe.wait_ge(router_loaded, 16 * 2)
                first_router.logits(pe)
                pe.wait_ge(loaded, 16 * 6)
                for k in range(3):
                    for e in range(NLORA):
                        job = k * NLORA + e
                        for c in range(DC):
                            mm = nc.tensor.matmul(ps[:, job, c * FE:(c + 1) * FE],
                                                  lora_a[:, k, e, c * P:(c + 1) * P], lora_b[:, k, e, :],
                                                  start=True, stop=True)
                        mm.then_inc(lora_ready, 1)

            @block.vector
            def _(dve):
                def lows(k, e):
                    dve.wait_ge(split_done, k * NE + e + 1)
                    nc.vector.tensor_tensor(low[:, k, EXPERT_ORDER[e]], raw[:, k, EXPERT_ORDER[e]],
                                            high[:, k, EXPERT_ORDER[e]].bitcast(F32), ALU.subtract)

                def add_low_rank(k):
                    dve.wait_ge(gate_up_weights.loaded[k], 16)
                    for e in range(NLORA):
                        dve.wait_ge(lora_ready, k * NLORA + e + 1)
                        dst = raw[:, k, e].rearrange("p c f -> p (c f)")
                        nc.vector.tensor_tensor(dst, dst, ps[:, k * NLORA + e, :], ALU.add).then_inc(lora_taken, 1)

                dve.wait_ge(router_loaded, 16 * 2)
                nc.vector.reciprocal(inv_temp[:], temp[:]).then_inc(setup_done, 1)
                dve.wait_ge(setup_done, 2)
                first_router.zones(dve)
                lows(0, 0)
                lows(0, 1)
                first_router.distances(dve)
                add_low_rank(0)
                lows(0, 2)
                lows(0, 3)
                first_router.in_zone(dve)
                first_router.pick_first(dve)
                for e in range(4, NE):
                    lows(0, e)
                first_router.pick_second(dve)
                add_low_rank(1)
                lows(1, 0)
                lows(1, 1)
                first_router.fallback(dve)
                lows(1, 2)
                lows(1, 3)
                first_router.weights(dve)
                for e in range(4, NE):
                    lows(1, e)
                dve.wait_ge(wd_loaded, 16)
                for e in range(NLORA):
                    dve.wait_ge(lora_ready, 2 * NLORA + e + 1)
                    dst = wd[:, e].rearrange("p c f -> p (c f)")
                    nc.vector.tensor_tensor(dst, dst, ps[:, 2 * NLORA + e, :], ALU.add).then_inc(lora_taken, 1)
                for e in range(POOL_LOWS, NE):
                    down_low(dve, nc.vector, e)

            @block.scalar
            def _(act):
                def highs(k, e):
                    if EXPERT_ORDER[e] < NLORA:
                        act.wait_ge(lora_taken, NLORA * (k + 1))
                    dst, src = (wd_high, wd) if k == 2 else (high[:, k], raw[:, k])
                    nc.scalar.copy(dst[:, EXPERT_ORDER[e]], src[:, EXPERT_ORDER[e]]).then_inc(split_done, 1)

                act.wait_ge(gate_up_weights.loaded[0], 16)
                highs(0, 0)
                highs(0, 1)
                first_router.sigmoid(act)
                highs(0, 2)
                highs(0, 3)
                first_router.weightings(act)
                for e in range(4, NE):
                    highs(0, e)
                act.wait_ge(gate_up_weights.loaded[1], 16)
                for e in range(NE):
                    highs(1, e)
                act.wait_ge(wd_loaded, 16)
                for e in range(NE):
                    highs(2, e)
        end_of_round(nc, list(R.values()) + [router_loaded, loaded, wd_loaded, lora_ready, lora_taken, split_done, setup_done]
                     + gate_up_weights.loaded)

        mid = sb("mid", [P, 2, 2, FC, GROUP], F32R)

        def round_(i, slot, following):
            router = Router(1 - slot)
            with nc.Block() as block:
                @block.vector
                def _(dve):
                    def x_tile(t):
                        return r.x[:, bass.ds(i * GROUP_TILES + t, 1), :].rearrange("p a d -> p (a d)")

                    def next_tile(t):
                        return r.x[:, bass.ds(following * GROUP_TILES + t, 1), :].rearrange("p a d -> p (a d)")

                    def mids(e):
                        for m in range(FC):
                            dve.wait_ge(silu_ready, FC * e + m + 1)
                            dve.wait_ge(up_ready, FC * e + m + 1)
                            if e >= 1:
                                dve.wait_ge(mid_ready, FC * (e - 1) + m + 1)
                            nc.vector.tensor_tensor(product[:, m, :], silu[:, m, :], ps[:, UP[m], :],
                                                    ALU.mult).then_inc(product_ready, 1)
                        for m in range(FC):
                            dve.wait_ge(mid_high_ready, FC * e + m + 1)
                            nc.vector.tensor_tensor(mid[:, 1, e % 2, m, :], product[:, m, :],
                                                    mid[:, 0, e % 2, m, :].bitcast(F32), ALU.subtract
                                                    ).then_inc(mid_ready, 1)

                    def add(e):
                        for t in range(GROUP_TILES):
                            q = 2 * e + t // 2
                            dve.wait_ge(down_ready, q + 1)
                            if e >= 1:
                                dve.wait_ge(added, GROUP_TILES * (e - 1) + t + 1)
                            at = (t % 2) * HID
                            nc.vector.scalar_tensor_tensor(x_tile(t), ps[:, DOWN[q % 3], at:at + HID],
                                                           w[:, slot, t, e:e + 1], x_tile(t), ALU.mult, ALU.add
                                                           ).then_inc(added, 1)

                    mids(0)
                    ahead.statistics(dve, L, next_tile)
                    mids(1)
                    ahead.normalise(dve, L, next_tile)
                    add(0)
                    mids(2)
                    add(1)
                    ahead.take_low(dve, L, ps[:, TURN, :], 0, 1 - slot)
                    mids(3)
                    add(2)
                    ahead.take_low(dve, L, ps[:, TURN, :], 1, 1 - slot)
                    mids(4)
                    add(3)
                    router.zones(dve)
                    router.distances(dve)
                    mids(5)
                    add(4)
                    router.in_zone(dve)
                    router.pick_first(dve)
                    mids(6)
                    add(5)
                    router.pick_second(dve)
                    router.fallback(dve)
                    mids(7)
                    router.weights(dve)
                    add(6)
                    add(7)

                @block.scalar
                def _(act):
                    def silus(e):
                        for m in range(FC):
                            act.wait_ge(gate_ready, FC * e + m + 1)
                            if e >= 1:
                                act.wait_ge(product_ready, FC * (e - 1) + m + 1)
                            nc.scalar.activation(silu[:, m, :], ps[:, GATE[m], :], ACT.Silu).then_inc(silu_ready, 1)

                    def mid_highs(e):
                        if e >= 2:
                            act.wait_ge(down_ready, 2 * (e - 1))
                        for m in range(FC):
                            act.wait_ge(product_ready, FC * e + m + 1)
                            nc.scalar.copy(mid[:, 0, e % 2, m, :], product[:, m, :]).then_inc(mid_high_ready, 1)

                    silus(0)
                    mid_highs(0)
                    ahead.root(act, L)
                    silus(1)
                    mid_highs(1)
                    silus(2)
                    mid_highs(2)
                    ahead.take_high(act, L, ps[:, TURN, :], 0, 1 - slot)
                    silus(3)
                    mid_highs(3)
                    ahead.take_high(act, L, ps[:, TURN, :], 1, 1 - slot)
                    silus(4)
                    mid_highs(4)
                    router.sigmoid(act)
                    router.weightings(act)
                    silus(5)
                    mid_highs(5)
                    silus(6)
                    mid_highs(6)
                    silus(7)
                    mid_highs(7)

                @block.tensor
                def _(pe):
                    def hidden_product(bank, k, e, m, ready):
                        cols = slice(m * P, (m + 1) * P)
                        passes = [p for c in range(DC) for p in split_passes(
                            high[:, k, e, c, cols], low[:, k, e, c, cols], ahead.high[slot][:, c, :],
                            ahead.low[slot][:, c, :])]
                        for j, (wpart, xpart) in enumerate(passes):
                            mm = nc.tensor.matmul(ps[:, bank, :], wpart, xpart,
                                                  start=(j == 0), stop=(j == len(passes) - 1))
                        mm.then_inc(ready, 1)

                    def gate_up(e):
                        for m in range(FC):
                            if e >= 1:
                                pe.wait_ge(silu_ready, FC * (e - 1) + m + 1)
                            hidden_product(GATE[m], 0, e, m, gate_ready)
                            if e >= 1:
                                pe.wait_ge(product_ready, FC * (e - 1) + m + 1)
                            hidden_product(UP[m], 1, e, m, up_ready)

                    def down(e):
                        pe.wait_ge(mid_ready, FC * (e + 1))
                        for pair in range(2):
                            q = 2 * e + pair
                            if q >= 3:
                                pe.wait_ge(added, 2 * (q - 2))
                            for t in (2 * pair, 2 * pair + 1):
                                at = (t % 2) * HID
                                rows = slice(t * P, (t + 1) * P)
                                passes = [p for m in range(FC) for p in split_passes(
                                    mid[:, 0, e % 2, m, rows], mid[:, 1, e % 2, m, rows],
                                    wd_high[:, e, m, :], wd_low[:, e, m, :])]
                                for j, (midpart, wpart) in enumerate(passes):
                                    mm = nc.tensor.matmul(ps[:, DOWN[q % 3], at:at + HID], midpart, wpart,
                                                          start=(j == 0), stop=(j == len(passes) - 1))
                            mm.then_inc(down_ready, 1)

                    gate_up(0)
                    gate_up(1)
                    down(0)
                    gate_up(2)
                    ahead.turn(pe, L, r.ident, ps[:, TURN, :], 0)
                    down(1)
                    gate_up(3)
                    pe.wait_ge(L["ln_taken"], 1)
                    ahead.turn(pe, L, r.ident, ps[:, TURN, :], 1)
                    down(2)
                    gate_up(4)
                    pe.wait_ge(L["ln_taken"], 2)
                    router.logits(pe)
                    down(3)
                    gate_up(5)
                    down(4)
                    gate_up(6)
                    down(5)
                    gate_up(7)
                    down(6)
                    down(7)
            end_of_round(nc, round_sems)

        with nc.Fori(0, GROUPS // 2) as i:
            round_(i * 2, 0, i * 2 + 1)
            round_(i * 2 + 1, 1, i * -2 + 2)


DH, DK, DV = 6, 32, 64
KEYS, VALS = DH * DK, DH * DV
TAPS = 4
SUB = 16
BLOCKS = P // SUB
HALVES = SEQ // P
UNITS = DH * HALVES
SET0 = 4 * DV
GATES = VALS + 2 * DH
RMS_EPS = 1e-5
JOBS = ((0, P), (KEYS, P), (P, KEYS - P), (KEYS + P, KEYS - P),
        (2 * KEYS, P), (2 * KEYS + P, P), (2 * KEYS + 2 * P, P))
QK_JOBS = 4
ATANH_TERMS = 8


class NormAll:

    RING = 8
    NAMES = "ln_chained ln_var_ready ln_r0_ready ln_xn_ready ln_turned ln_copied ln_summed"

    def __init__(self, nc, ctx):
        def sb(name, shape):
            return ctx.enter_context(nc.sbuf_tensor("all_" + name, shape, F32))

        self.nc, self.start = nc, 0
        self.stats = sb("ln_stats", [P, TILES, 6])
        self.mv = sb("ln_mv", [P, TILES, 2])
        self.veps = sb("ln_veps", [P, TILES])
        self.lnv = sb("ln_lnv", [P, TILES])
        self.r0 = sb("ln_r0", [P, TILES])
        self.t = sb("ln_t", [P, TILES])
        self.xn = sb("ln_xn", [P, self.RING, HID])
        self.xnT = sb("xnT", [P, DC, TOKENS])
        self.sums = sb("ln_sums", [P, DC, BATCH])
        self.sems = [ctx.enter_context(nc.semaphore("all_" + s)) for s in self.NAMES.split()]
        (self.chained, self.var_ready, self.r0_ready, self.xn_ready, self.turned, self.copied,
         self.summed) = self.sems

    def statistics(self, dve, x, part, first, end):
        nc, links = self.nc, 6 * part
        for t in range(first, end):
            last = nc.vector.bn_stats(self.stats[:, t, :], x[:, t, :])
        last.then_inc(self.chained, 1)
        dve.wait_ge(self.chained, links + 1)
        for t in range(first, end):
            last = nc.vector.bn_aggr(self.mv[:, t, :], self.stats[:, t, :])
        last.then_inc(self.chained, 1)
        dve.wait_ge(self.chained, links + 2)
        nc.vector.tensor_scalar(self.veps[:, first:end], self.mv[:, first:end, 1], LN_EPS, None, ALU.add
                                ).then_inc(self.var_ready, 1)

    def newton(self, dve, part, first, end):
        nc, links = self.nc, 6 * part
        r0, veps, t = self.r0[:, first:end], self.veps[:, first:end], self.t[:, first:end]
        dve.wait_ge(self.r0_ready, 2 * part + 2)
        nc.vector.tensor_tensor(t, r0, r0, ALU.mult).then_inc(self.chained, 1)
        dve.wait_ge(self.chained, links + 3)
        nc.vector.tensor_tensor(t, t, veps, ALU.mult).then_inc(self.chained, 1)
        dve.wait_ge(self.chained, links + 4)
        nc.vector.tensor_scalar(t, t, -0.5, 1.5, ALU.mult, ALU.add).then_inc(self.chained, 1)
        dve.wait_ge(self.chained, links + 5)
        nc.vector.tensor_tensor(t, t, r0, ALU.mult).then_inc(self.chained, 1)
        dve.wait_ge(self.chained, links + 6)

    def normalise(self, dve, x, first, end):
        for t in range(first, end):
            nth = t - self.start
            if nth >= self.RING:
                dve.wait_ge(self.turned, nth - self.RING + 1)
            self.nc.vector.tensor_scalar(self.xn[:, nth % self.RING, :], x[:, t, :], self.mv[:, t, 0:1],
                                         self.t[:, t:t + 1], ALU.subtract, ALU.mult).then_inc(self.xn_ready, 1)

    def root(self, act, part, first, end):
        nc = self.nc
        act.wait_ge(self.var_ready, part + 1)
        nc.scalar.activation(self.lnv[:, first:end], self.veps[:, first:end], ACT.Ln).then_inc(self.r0_ready, 1)
        act.wait_ge(self.r0_ready, 2 * part + 1)
        nc.scalar.activation(self.r0[:, first:end], self.lnv[:, first:end], ACT.Exp, scale=-0.5
                             ).then_inc(self.r0_ready, 1)

    def bank(self, g, c):
        return (g % 2) * DC + c

    def turn(self, pe, ps, ident, g):
        if g >= 2:
            pe.wait_ge(self.copied, DC * (g - 1))
        for t in range(g * GROUP_TILES, (g + 1) * GROUP_TILES):
            nth = t - self.start
            pe.wait_ge(self.xn_ready, nth + 1)
            for c in range(DC):
                at = (t % GROUP_TILES) * P
                mm = self.nc.tensor.transpose(ps[:, self.bank(g, c), at:at + P],
                                              self.xn[:, nth % self.RING, c * P:(c + 1) * P], ident[:])
            mm.then_inc(self.turned, 1)

    def copy(self, act, ps, g):
        act.wait_ge(self.turned, GROUP_TILES * (g + 1) - self.start)
        for c in range(DC):
            self.nc.scalar.copy(self.xnT[:, c, g * GROUP:(g + 1) * GROUP], ps[:, self.bank(g, c), :]
                                ).then_inc(self.copied, 1)

    def copy_first(self, act, first_xnT):
        for c in range(DC):
            self.nc.scalar.copy(self.xnT[:, c, 0:GROUP], first_xnT[:, c, :]).then_inc(self.copied, 1)

    def sum_batches(self, dve, g):
        dve.wait_ge(self.copied, DC * (g + 1))
        self.nc.vector.reduce_sum(self.sums[:, :, g * GROUP_BATCHES:(g + 1) * GROUP_BATCHES],
                                  self.xnT[:, :, g * GROUP:(g + 1) * GROUP].rearrange(
                                      "p c (b t) -> p c b t", b=GROUP_BATCHES), AX_X).then_inc(self.summed, 1)


EARLY_TILES = 3 * GROUP_TILES


def delta(nc, r, n, w_q, w_k, w_v, w_a, w_b, w_g, w_o, conv_q, conv_k, conv_v, a_log, dt_bias, norm_weight):
    with ExitStack() as ctx:
        def sb(name, shape, dt=F32):
            return ctx.enter_context(nc.sbuf_tensor("c_" + name, shape, dt))

        def sem(name):
            return ctx.enter_context(nc.semaphore("c_" + name))

        ps = ctx.enter_context(nc.psum_tensor("c_ps", [P, 8, 512], F32))
        win = sb("win", [P, DC, 2 * KEYS + VALS])
        wgate = sb("wgate", [P, DC, VALS])
        wab = sb("wab", [P, DC, 2 * DH])
        wo = sb("wo", [P, VALS // P, HID])
        taps = sb("taps", [P, len(JOBS), TAPS])
        dtb = sb("dtb", [P, 1, DH])
        neg_rate = sb("neg_rate", [P, 1, DH])
        normw = sb("normw", [P, 1, DV])
        blocks = sb("blocks", [P, BLOCKS])
        even_neg, odd_neg = sb("even_neg", [P, 1]), sb("odd_neg", [P, 1])
        off_blocks = sb("off_blocks", [P, 1, P])
        head_ones = sb("head_ones", [P, P])
        own = sb("own", [P, DH, DV])
        ident2 = sb("ident2", [P, HALVES, P])
        urep = sb("urep", [P, SUB, UNITS, SUB])
        inv = sb("inv", [P, UNITS, SUB + 1])
        xnT = n.xnT
        beta = sb("beta", [P, TILES, DH])
        a_dram = nc.dram_tensor("a_scratch", [BATCH, DH * SEQ], F32).ap()
        g_dram = nc.dram_tensor("g_scratch", [BATCH, DH * P], F32).ap()
        state = sb("state", [P, VALS])
        chan = sb("chan", [P, len(JOBS), SEQ])
        square = sb("square", [P, QK_JOBS, SEQ])
        a_all = sb("a_all", [P, DH, SEQ])
        kq = sb("kq", [P, 2, 2, SEQ])
        g_all = sb("g_all", [P, 2, P])

        gates_loaded, loaded, masks, spread = [sem(x) for x in ("gates_loaded", "loaded", "masks", "spread")]

        def load_weights(sp):
            def row(a, m):
                return a.rearrange("(a n) -> a n", a=1).to_broadcast([P, m])

            for dst, src in ((wab[:, :, 0:DH], w_a.rearrange("(c p) n -> p c n", p=P)),
                             (wab[:, :, DH:], w_b.rearrange("(c p) n -> p c n", p=P)),
                             (dtb[:, 0, :], row(dt_bias, DH)), (neg_rate[:, 0, :], row(a_log, DH))):
                sp.dma_start(dst, src).then_inc(gates_loaded, 16)
            loads = [(win[:, :, 0:KEYS], w_q.rearrange("(c p) n -> p c n", p=P)),
                     (win[:, :, KEYS:2 * KEYS], w_k.rearrange("(c p) n -> p c n", p=P)),
                     (win[:, :, 2 * KEYS:], w_v.rearrange("(c p) n -> p c n", p=P)),
                     (taps[:, 0, :], conv_q[0:P, :]), (taps[:, 1, :], conv_k[0:P, :]),
                     (taps[0:KEYS - P, 2, :], conv_q[P:KEYS, :]), (taps[0:KEYS - P, 3, :], conv_k[P:KEYS, :]),
                     (taps[:, QK_JOBS:, :], conv_v.rearrange("(j p) n -> p j n", p=P)),
                     (wgate[:], w_g.rearrange("(c p) n -> p c n", p=P)),
                     (wo[:], w_o.rearrange("(c p) n -> p c n", p=P)), (normw[:, 0, :], row(norm_weight, DV))]
            for dst, src in loads:
                sp.dma_start(dst, src).then_inc(loaded, 16)
            assert len(loads) == LOADS

        def make_masks(pool):
            nc.gpsimd.memset(blocks[:], 1.0)
            nc.gpsimd.memset(head_ones[:], 1.0)
            nc.gpsimd.memset(kq[:], 0.0)
            nc.gpsimd.memset(g_all[:], 0.0)
            nc.gpsimd.memset(state[:], 0.0)
            nc.gpsimd.memset(inv[:, :, 0:1], 1.0).then_inc(masks, 1)
            pool.wait_ge(masks, 1)
            nc.gpsimd.affine_select(out=blocks[:], in_=blocks[:], compare_op=ALU.is_ge, fill=0.0, base=0,
                                    pattern=[[-SUB, BLOCKS]], channel_multiplier=1)
            nc.gpsimd.affine_select(out=head_ones[:], in_=head_ones[:], compare_op=ALU.is_ge, fill=0.0, base=0,
                                    pattern=[[-DK, P // DK], [0, DK]], channel_multiplier=1).then_inc(masks, 1)
            pool.wait_ge(masks, 2)
            nc.gpsimd.affine_select(out=blocks[:], in_=blocks[:], compare_op=ALU.is_ge, fill=0.0, base=SUB - 1,
                                    pattern=[[SUB, BLOCKS]], channel_multiplier=-1)
            nc.gpsimd.affine_select(out=head_ones[:], in_=head_ones[:], compare_op=ALU.is_ge, fill=0.0,
                                    base=DK - 1, pattern=[[DK, P // DK], [0, DK]],
                                    channel_multiplier=-1).then_inc(masks, 1)

        decays(nc, r, n, ps, win, taps, chan, square, a_all, g_all, xnT, wab, dtb, neg_rate, beta, a_dram, g_dram, gates_loaded, loaded, masks,
               spread, load_weights, make_masks, (blocks, even_neg, odd_neg, off_blocks, head_ones, own, ident2, urep, inv))
        batches(nc, r, n, ps, win, wgate, wo, taps, normw, blocks, even_neg, odd_neg, off_blocks, head_ones, own,
                ident2, urep, inv, xnT, beta, a_dram, g_dram, spread, state, chan, square, kq, a_all, g_all)


def spread_decays(nc, sp, a_dram, g_dram, a_all, g_all, batch, signal):
    sp.dma_start(a_all[:].rearrange("p h t -> p (h t)"), a_dram[batch].to_broadcast([P, DH * SEQ])
                 ).then_inc(signal, 16)
    for h in range(DH):
        rows = slice((h % 4) * DK, (h % 4 + 1) * DK)
        cols = slice(h * P, (h + 1) * P)
        sp.dma_start(g_all[rows, h // 4, :], g_dram[batch, cols].to_broadcast([DK, P])).then_inc(signal, 16)


SPREADS = 16 * (1 + DH)


class Channels:

    def __init__(self, nc, sems, ps, banks, win, taps, chan, square, xnT):
        self.nc, self.S, self.ps, self.banks = nc, sems, ps, banks
        self.win, self.taps, self.chan, self.square, self.xnT = win, taps, chan, square, xnT

    NAMES = "tap_ready job_ready conv_step silu_done square_ready"

    def place(self, j):
        at = (j % 2) * SEQ
        return self.ps[0:JOBS[j][1], self.banks[j // 2], at:at + SEQ]

    def through(self, j):
        return min(j // 2 * 2 + 2, len(JOBS))

    def job(self, pe, j, tokens):
        nc, S = self.nc, self.S
        col, m = JOBS[j]
        if self.banks[j // 2] in self.banks[0:j // 2]:
            pe.wait_ge(S["conv_step"], (TAPS - 1) * 2 * (self.banks.index(self.banks[j // 2]) + 1))
        for c in range(DC):
            mm = nc.tensor.matmul(self.place(j), self.win[:, c, col:col + m], self.xnT[:, c, tokens],
                                  start=(c == 0), stop=(c == DC - 1))
        mm.then_inc(S["job_ready"], 1)

    def tap(self, act, j):
        m = JOBS[j][1]
        act.wait_ge(self.S["job_ready"], self.through(j))
        self.nc.scalar.activation(self.chan[0:m, j, :], self.place(j), ACT.Copy,
                                  scale=self.taps[0:m, j, TAPS - 1:TAPS]).then_inc(self.S["tap_ready"], 1)

    def conv(self, dve, q):
        j, k = q // (TAPS - 1), 1 + q % (TAPS - 1)
        m = JOBS[j][1]
        if k == 1:
            dve.wait_ge(self.S["tap_ready"], self.through(j))
        else:
            dve.wait_ge(self.S["conv_step"], q)
        self.nc.vector.scalar_tensor_tensor(self.chan[0:m, j, k:], self.place(j)[:, 0:SEQ - k],
                                            self.taps[0:m, j, TAPS - 1 - k:TAPS - k], self.chan[0:m, j, k:],
                                            ALU.mult, ALU.add).then_inc(self.S["conv_step"], 1)

    def silu(self, act, j):
        m = JOBS[j][1]
        act.wait_ge(self.S["conv_step"], (TAPS - 1) * (j + 1))
        self.nc.scalar.activation(self.chan[0:m, j, :], self.chan[0:m, j, :], ACT.Silu
                                  ).then_inc(self.S["silu_done"], 1)

    def squares(self, pool, j):
        m = JOBS[j][1]
        pool.wait_ge(self.S["silu_done"], j + 1)
        self.nc.gpsimd.tensor_tensor(self.square[0:m, j, :], self.chan[0:m, j, :], self.chan[0:m, j, :], ALU.mult
                                     ).then_inc(self.S["square_ready"], 1)


LOADS, GATE_LOADS = 11, 4
CONVS = len(JOBS) * (TAPS - 1)


def decays(nc, r, n, ps, win, taps, chan, square, a_all, g_all, xnT, wab, dtb, neg_rate, beta_all, a_dram, g_dram, gates_loaded, loaded, masks,
           spread, load_weights, make_masks, consts):
    blocks, even_neg, odd_neg, off_blocks, head_ones, own, ident2, urep, inv = consts
    with ExitStack() as ctx:
        def sb(name, shape, dt=F32):
            return ctx.enter_context(nc.sbuf_tensor("cd_" + name, shape, dt))

        def sem(name):
            return ctx.enter_context(nc.semaphore("cd_" + name))

        n.start = GROUP_TILES
        TH = [P, TILES, DH]
        ab = sb("ab", [P, TILES, 2 * DH])
        u, s, s2, poly, decay = [sb(x, TH) for x in ("u", "s", "s2", "poly", "decay")]
        aT = sb("aT", [DH, TILES, P])
        gT = sb("gT", [DH, BATCH, P])
        zeros_row = sb("zeros_row", [DH, P])
        mine = sb("mine", [P, 1, SUB])
        ab_ready, a_pre, exps_ready, a_in, a_ready, aT_ready, chained, scanned, stored, rate = [
            sem(x) for x in ("ab_ready", "a_pre", "exps_ready", "a_in", "a_ready", "aT_ready", "chained", "scanned",
                             "stored", "rate")]
        AB, ROWS = 4, (0, 1, 2, 3)
        first = Channels(nc, {x: sem(x) for x in Channels.NAMES.split()}, ps, (5, 6, 7, 5), win, taps, chan, square, xnT)

        with nc.Block() as block:
            @block.sync
            def _(sp):
                load_weights(sp)
                sp.wait_ge(scanned, BATCH + 1)
                sp.dma_start(a_dram.rearrange("b (h t) -> h b t", h=DH),
                             aT[:].rearrange("h (b k) p -> h b (k p)", b=BATCH)).then_inc(stored, 16)
                sp.dma_start(g_dram.rearrange("b (h t) -> h b t", h=DH), gT[:]).then_inc(stored, 16)
                sp.wait_ge(stored, 32)
                spread_decays(nc, sp, a_dram, g_dram, a_all, g_all, slice(0, 1), spread)
                sp.wait_ge(loaded, 16 * LOADS)

            @block.scalar
            def _(act):
                nc.scalar.preload_act_table_set("natural_log_exp_and_others")
                n.copy_first(act, r.first_xnT)
                n.root(act, 0, n.start, TILES)
                act.wait_ge(gates_loaded, 16 * GATE_LOADS)
                nc.scalar.activation(neg_rate[:], neg_rate[:], ACT.Exp).then_inc(rate, 1)
                act.wait_ge(rate, 1)
                nc.scalar.mul(neg_rate[:], neg_rate[:], -1.0).then_inc(rate, 1)
                for g in range(1, GROUPS):
                    n.copy(act, ps, g)
                act.wait_ge(a_pre, 1)
                nc.scalar.activation(u[:], u[:], ACT.Exp, scale=-1.0).then_inc(exps_ready, 1)
                nc.scalar.activation(beta_all[:], ab[:, :, DH:], ACT.Exp, scale=-1.0).then_inc(exps_ready, 1)
                act.wait_ge(loaded, 16 * LOADS)
                for j in range(len(JOBS) - 1):
                    first.tap(act, j)
                act.wait_ge(a_in, 1)
                nc.scalar.activation(decay[:], poly[:], ACT.Exp).then_inc(a_ready, 1)
                first.silu(act, 0)
                first.silu(act, 1)
                first.tap(act, len(JOBS) - 1)
                for j in range(2, len(JOBS)):
                    first.silu(act, j)

            @block.gpsimd
            def _(pool):
                make_masks(pool)
                for j in range(QK_JOBS):
                    first.squares(pool, j)

            @block.tensor
            def _(pe):
                pe.wait_ge(gates_loaded, 16 * GATE_LOADS)
                for g in range(GROUPS):
                    pe.wait_ge(n.copied, DC * (g + 1))
                    for t in range(g * GROUP_TILES, (g + 1) * GROUP_TILES):
                        for c in range(DC):
                            mm = nc.tensor.matmul(ps[:, AB, t * 2 * DH:(t + 1) * 2 * DH],
                                                  xnT[:, c, t * P:(t + 1) * P], wab[:, c, :],
                                                  start=(c == 0), stop=(c == DC - 1))
                    if g == 0:
                        n.turn(pe, ps, r.ident, 1)
                    if g + 2 < GROUPS:
                        n.turn(pe, ps, r.ident, g + 2)
                mm.then_inc(ab_ready, 1)
                pe.wait_ge(loaded, 16 * LOADS)
                for j in range(len(JOBS) - 1):
                    first.job(pe, j, slice(0, SEQ))
                pe.wait_ge(a_ready, 1)
                for t in range(TILES):
                    at = (t % GROUP_TILES) * P
                    mm = nc.tensor.transpose(ps[0:DH, ROWS[t // GROUP_TILES], at:at + P], decay[:, t, :], r.ident[:])
                mm.then_inc(aT_ready, 1)
                first.job(pe, len(JOBS) - 1, slice(0, SEQ))

            @block.vector
            def _(dve):
                done = [0]

                def link(ins):
                    done[0] += 1
                    ins.then_inc(chained, 1)
                    dve.wait_ge(chained, done[0])

                n.statistics(dve, r.x, 0, n.start, TILES)
                n.newton(dve, 0, n.start, TILES)
                n.normalise(dve, r.x, n.start, TILES)
                nc.vector.memset(zeros_row[:], 0.0)
                for k in range(HALVES):
                    nc.vector.tensor_copy(ident2[:, k, :], r.ident[:])
                dve.wait_ge(masks, 3)
                pairs = blocks[:].rearrange("p (b h) -> p h b", h=2)
                nc.vector.tensor_reduce(even_neg[:], pairs[:, 0:1, :], AX_X, ALU.add, negate=True)
                nc.vector.tensor_reduce(odd_neg[:], pairs[:, 1:2, :], AX_X, ALU.add, negate=True)
                wide = blocks[:].rearrange("p (b o) -> p b o", o=1).to_broadcast([P, BLOCKS, SUB])
                nc.vector.tensor_scalar(off_blocks[:, 0, :].rearrange("p (b t) -> p b t", b=BLOCKS), wide,
                                        -1.0, 1.0, ALU.mult, ALU.add)
                for h in range(DH):
                    nc.vector.tensor_copy(own[:, h, :],
                                          head_ones[:, (h % 4) * DK:(h % 4) * DK + 1].to_broadcast([P, DV]))
                link(nc.vector.tensor_reduce(mine[:, 0, :], r.ident[:].rearrange("p (b t) -> p t b", b=BLOCKS),
                                             AX_X, ALU.add))
                nc.vector.tensor_copy(urep[:, 0, :, :], mine[:].to_broadcast([P, UNITS, SUB]))
                nc.vector.tensor_copy(inv[:, :, 1:2], mine[:, :, 0:1].to_broadcast([P, UNITS, 1]))

                dve.wait_ge(ab_ready, 1)
                link(nc.vector.tensor_copy(ab[:].rearrange("p t h -> p (t h)"), ps[:, AB, 0:TILES * 2 * DH]))
                link(nc.vector.tensor_tensor(ab[:, :, 0:DH], ab[:, :, 0:DH], dtb[:].to_broadcast(TH), ALU.add))
                nc.vector.scalar_tensor_tensor(u[:], ab[:, :, 0:DH], -1.0, ab[:, :, 0:DH], ALU.mult,
                                               ALU.max).then_inc(a_pre, 1)
                dve.wait_ge(exps_ready, 2)
                link(nc.vector.tensor_scalar(beta_all[:], beta_all[:], 1.0, None, ALU.add))
                nc.vector.reciprocal(beta_all[:], beta_all[:])
                link(nc.vector.tensor_scalar(s[:], u[:], 2.0, None, ALU.add))
                link(nc.vector.reciprocal(s[:], s[:]))
                link(nc.vector.tensor_tensor(s[:], s[:], u[:], ALU.mult))
                link(nc.vector.tensor_tensor(s2[:], s[:], s[:], ALU.mult))
                link(nc.vector.tensor_scalar(poly[:], s2[:], 1.0 / (2 * ATANH_TERMS + 1), None, ALU.mult))
                for k in range(ATANH_TERMS - 1, 0, -1):
                    link(nc.vector.scalar_tensor_tensor(poly[:], poly[:], 1.0 / (2 * k + 1), s2[:], ALU.add, ALU.mult))
                link(nc.vector.scalar_tensor_tensor(poly[:], poly[:], 1.0, s[:], ALU.add, ALU.mult))
                link(nc.vector.tensor_scalar(ab[:, :, 0:DH], ab[:, :, 0:DH], 0.0, None, ALU.max))
                link(nc.vector.scalar_tensor_tensor(poly[:], poly[:], 2.0, ab[:, :, 0:DH], ALU.mult, ALU.add))
                dve.wait_ge(rate, 2)
                nc.vector.tensor_tensor(poly[:], poly[:], neg_rate[:].to_broadcast(TH), ALU.mult).then_inc(a_in, 1)
                for q in range(CONVS // 2):
                    first.conv(dve, q)
                dve.wait_ge(aT_ready, 1)
                for g in range(GROUPS):
                    ins = nc.vector.tensor_copy(
                        aT[:, g * GROUP_TILES:(g + 1) * GROUP_TILES, :].rearrange("h t p -> h (t p)"),
                        ps[0:DH, ROWS[g], :])
                link(ins)
                for b in range(BATCH):
                    nc.vector.tensor_tensor_scan(gT[:, b, :], aT[:, HALVES * b + 1, :], zeros_row[:], 1.0,
                                                 ALU.mult, ALU.add).then_inc(scanned, 1)
                dve.wait_ge(scanned, BATCH)
                nc.vector.memset(aT[:, :, 0:1], 0.0).then_inc(scanned, 1)
                for q in range(CONVS // 2, CONVS):
                    first.conv(dve, q)
        end_of_round(nc, [gates_loaded, loaded, masks, ab_ready, a_pre, exps_ready, a_in, a_ready, aT_ready, chained, scanned,
                          stored, rate] + list(n.sems) + list(first.S.values()))


def batches(nc, r, n, ps, win, wgate, wo, taps, normw, blocks, even_neg, odd_neg, off_blocks, head_ones, own,
            ident2, urep, inv, xnT, beta, a_dram, g_dram, spread, state, chan, square, kq, a_all, g_all):
    with ExitStack() as ctx:
        def sb(name, shape, dt=F32):
            return ctx.enter_context(nc.sbuf_tensor("cb_" + name, shape, dt))

        def sem(name):
            return ctx.enter_context(nc.semaphore("cb_" + name))

        WIDE = DV + DK
        SET = VALS + WIDE
        WIDES = (DH - 1) * WIDE
        xb = sb("xb", [P, DC, SEQ])
        bb = sb("bb", [P, HALVES, DH])
        rnorm = sb("rnorm", [P, QK_JOBS, SEQ])
        E = sb("E", [P, DH, HALVES, P])
        klast = sb("klast", [P, DH, 1])
        diag = sb("diag", [P, UNITS, SUB])
        prod = sb("prod", [P, UNITS, SUB])
        kqg = sb("kqg", [P, 2, 2, 2, P])
        ktok = sb("ktok", [P, 2, DH, DK])
        right = sb("right", [P, 2, HALVES, SET])
        gate = sb("gate", [P, 2, HALVES, DH, DV])
        aq = sb("aq", [P, 2, UNITS, 2, P])
        low = sb("low", [P, 2, UNITS, P])
        tdT = sb("tdT", [P, UNITS, P])
        nN, nT, n2T = [sb(x, [P, UNITS, P]) for x in ("nN", "nT", "n2T")]
        y, z = [sb(x, [P, HALVES, SET]) for x in ("y", "z")]
        wk = sb("wk", [P, KEYS])
        wkT = sb("wkT", [P, 2, P])
        x1 = sb("x1", [P, VALS])
        osq = sb("osq", [P, DH, DV])
        o = sb("o", [P, HALVES, DH, DV])
        ms = sb("ms", [P, HALVES, DH, 1])
        oT = r.first_xnT[:].rearrange("p c t -> p (c t)")[:, 0:HALVES * VALS].rearrange(
            "p (k c t) -> p k c t", k=HALVES, t=P)

        names = (Channels.NAMES + " xb_ready a_spread norms_ready ln_ready rnorm_ready kq_pool kq_vector kqg_ready "
                 "gates_ready gate_taken gated vT_ready v_ready kT_ready ktok_ready kg_ready "
                 "e_ready klast_ready scores_ready aq_ready lT_ready l_ready folded inv_step td_pool td_vector "
                 "n_ready n_copied y_ready y_copied step_ready step_done state_ready state_copied wk_ready wkT_ready "
                 "wkT_copied ks_ready x1_ready o_ready osq_ready "
                 "summed saved root_ready o_done oT_ready oT_copied out_ready out_added").split()
        S = {x: sem(x) for x in names}
        round_sems = [S[x] for x in names]

        n.start = 0
        NORM_BANKS, N_BANKS, SCORE_BANKS, K_BANK, V_BANKS = (0, 1), (2, 3, 4), (0, 1), 2, (3, 4)
        L_BANKS, SET_BANKS, O_BANKS, JOB_BANKS, GATE_BANKS = (0, 1, 2), (5, 6), (3, 5), (7, 7, 4, 0), (1, 2)
        PAIRS = DH // 2
        TURNED_BANKS, DONE_BANK = (5, 6), 7
        STEPS = 4

        channels = Channels(nc, S, ps, JOB_BANKS, win, taps, chan, square, xnT)

        def head_cols(h):
            return slice(h * DV, (h + 1) * DV)

        def half_cols(k):
            return slice(k * P, (k + 1) * P)

        def wide(h):
            return (1, h * WIDE) if h < DH - 1 else (0, VALS)

        def rights(s):
            if s:
                return [(h, 1, slice(h * WIDE, (h + 1) * WIDE)) for h in range(DH - 1)]
            return [(h, 0, head_cols(h)) for h in range(DH)] + [(DH - 1, 1, slice(VALS, SET))]

        WIDTHS = (SET, WIDES)
        HEAD_SETS = ((0, slice(0, SET0)), (1, slice(SET0, VALS)))

        def wides(t):
            return t[:, 0:WIDES].rearrange("p (h w) -> p h w", w=WIDE)

        def stage(first, middle, ms_, last, ls, done, ds_):
            C_, M_, S_, D_ = first is not None, middle is not None, last is not None, done is not None
            N1_, N2_ = S_ and not M_, D_ and not S_
            with nc.Block() as block:
                @block.sync
                def _(sp):
                    if C_:
                        sp.wait_ge(S["e_ready"], DH)
                        sp.wait_ge(S["kqg_ready"], 2)
                        spread_decays(nc, sp, a_dram, g_dram, a_all, g_all, bass.ds(first, 1), S["a_spread"])
                        sp.wait_ge(S["a_spread"], SPREADS)

                def normalise_channels(engine, eng, j, sem_name):
                    m = JOBS[j][1]
                    engine.wait_ge(S["rnorm_ready"], j + 1)
                    eng.tensor_tensor(kq[0:m, j // 2, 1 - j % 2, :], chan[0:m, j, :], rnorm[0:m, j, :],
                                      ALU.mult).then_inc(S[sem_name], 1)

                def spread_inverse(eng, p, sem_name):
                    us = slice(p * 2 * HALVES, (p + 1) * 2 * HALVES)
                    eng.tensor_tensor(
                        tdT[:, us, :].rearrange("p u (b t) -> p u b t", b=BLOCKS),
                        inv[:, us, 1:SUB + 1].rearrange("p u (o t) -> p u o t", o=1).to_broadcast(
                            [P, 2 * HALVES, BLOCKS, SUB]),
                        blocks[:].rearrange("p (o b k) -> p o b k", o=1, k=1).to_broadcast(
                            [P, 2 * HALVES, BLOCKS, SUB]), ALU.mult).then_inc(S[sem_name], 1)

                @block.gpsimd
                def _(pool):
                    if M_:
                        nc.gpsimd.tensor_copy(bb[:], beta[:, bass.ds(middle * HALVES, HALVES), :]
                                              ).then_inc(S["xb_ready"], 1)
                    if D_:
                        for k in range(HALVES):
                            nc.gpsimd.tensor_tensor(gate[:, ds_, k], gate[:, ds_, k],
                                                    normw[:].to_broadcast([P, DH, DV]), ALU.mult
                                                    ).then_inc(S["gated"], 1)
                    if M_:
                        for j in (0, 2):
                            normalise_channels(pool, nc.gpsimd, j, "kq_pool")
                        pool.wait_ge(S["kq_pool"], 2)
                        pool.wait_ge(S["kq_vector"], 2)
                        if M_ and not S_:
                            pool.wait_ge(spread, SPREADS)
                        for hs in range(2):
                            nc.gpsimd.tensor_tensor(kqg[:, ms_, hs], kq[:, hs, :, P:SEQ],
                                                    g_all[:, hs:hs + 1, :].to_broadcast([P, 2, P]), ALU.mult
                                                    ).then_inc(S["kqg_ready"], 1)
                        nc.gpsimd.tensor_copy(xb[:], xnT[:, :, bass.ds(middle * SEQ, SEQ)]).then_inc(S["xb_ready"], 1)
                    if D_:
                        pool.wait_ge(S["gated"], HALVES)
                        nc.gpsimd.tensor_tensor(o[:], o[:], gate[:, ds_], ALU.mult).then_inc(S["gated"], 1)
                        pool.wait_ge(S["root_ready"], 2)
                        pool.wait_ge(S["gated"], HALVES + 1)
                        nc.gpsimd.tensor_tensor(o[:], o[:], ms[:].to_broadcast([P, HALVES, DH, DV]), ALU.mult
                                                ).then_inc(S["o_done"], 1)
                    if C_:
                        pool.wait_ge(S["norms_ready"], QK_JOBS)
                        for j in range(QK_JOBS):
                            channels.squares(pool, j)
                    if M_:
                        pool.wait_ge(S["inv_step"], 2 * (SUB - 1))
                        if S_:
                            pool.wait_ge(S["y_ready"], 2)
                        for p in range(1, PAIRS):
                            spread_inverse(nc.gpsimd, p, "td_pool")

                @block.vector
                def _(dve):
                    def scan(h):
                        if M_ and not S_:
                            dve.wait_ge(spread, SPREADS)
                        nc.vector.tensor_tensor_scan(E[:, h].rearrange("p t k -> p (t k)"), a_all[:, h, :],
                                                     ident2[:].rearrange("p t k -> p (t k)"), 0.0,
                                                     ALU.mult, ALU.add).then_inc(S["e_ready"], 1)

                    def last_decays():
                        dve.wait_ge(S["e_ready"], DH)
                        dve.wait_ge(S["xb_ready"], 1)
                        nc.vector.tensor_tensor(klast[:], E[:, :, 0, P - 1:P],
                                                bb[:, 0, :].rearrange("p (h o) -> p h o", o=1), ALU.mult
                                                ).then_inc(S["klast_ready"], 1)

                    def keys_by_token():
                        dve.wait_ge(S["klast_ready"], 1)
                        dve.wait_ge(S["kg_ready"], 2)
                        nc.vector.tensor_tensor(ktok[:, ms_], ps[:, K_BANK, 0:KEYS].rearrange("p (h k) -> p h k", h=DH),
                                                klast[:].to_broadcast([P, DH, DK]), ALU.mult
                                                ).then_inc(S["ktok_ready"], 1)

                    def products(h):
                        dve.wait_ge(S["scores_ready"], h + 1)
                        for k in range(HALVES):
                            src = ps[:, SCORE_BANKS[h % 2], k * 2 * P:(k + 1) * 2 * P].rearrange("p (c t) -> p c t", c=2)
                            nc.vector.scalar_tensor_tensor(aq[:, ms_, h * HALVES + k], src, bb[:, k, h:h + 1],
                                                           E[:, h, k:k + 1, :].to_broadcast([P, 2, P]),
                                                           ALU.mult, ALU.mult).then_inc(S["aq_ready"], 1)

                    def off_diagonal(p):
                        dve.wait_ge(S["lT_ready"], p + 1)
                        nc.vector.tensor_tensor(low[:, ms_, p * 2 * HALVES:(p + 1) * 2 * HALVES, :],
                                                ps[:, L_BANKS[p], :].rearrange("p (t k) -> p t k", k=P),
                                                off_blocks[:].to_broadcast([P, 2 * HALVES, P]), ALU.mult
                                                ).then_inc(S["l_ready"], 1)

                    def fold_even():
                        dve.wait_ge(S["aq_ready"], UNITS)
                        for q in range(P // 32):
                            rows = slice(32 * q, 32 * q + 32)
                            ins = nc.vector.tensor_scalar(diag[rows], aq[rows, ms_, :, 0, 32 * q:32 * q + SUB],
                                                          even_neg[rows], None, ALU.mult)
                        ins.then_inc(S["folded"], 1)

                    def fold_odd():
                        dve.wait_ge(S["folded"], 1)
                        for q in range(P // 32):
                            rows = slice(32 * q, 32 * q + 32)
                            ins = nc.vector.scalar_tensor_tensor(diag[rows],
                                                                 aq[rows, ms_, :, 0, 32 * q + SUB:32 * q + 32],
                                                                 odd_neg[rows], diag[rows], ALU.mult, ALU.add)
                        ins.then_inc(S["folded"], 1)

                    def shuffle(k):
                        if k == 0:
                            dve.wait_ge(S["folded"], 2)
                        ins = nc.vector.stream_shuffle(urep[:, 1 + k, :, k + 1:SUB], diag[:, :, k + 1:SUB],
                                                       [k] * SUB + [SUB + k] * SUB)
                        if k == SUB - 2:
                            ins.then_inc(S["folded"], 1)

                    def column_product(t):
                        if t == 1:
                            dve.wait_ge(S["folded"], 3)
                        else:
                            dve.wait_ge(S["inv_step"], 2 * (t - 1))
                        nc.vector.tensor_tensor(prod[:, :, 0:t + 1], inv[:, :, 0:t + 1],
                                                urep[:, 0:t + 1, :, t].rearrange("p k u -> p u k"), ALU.mult
                                                ).then_inc(S["inv_step"], 1)

                    def column_sum(t):
                        dve.wait_ge(S["inv_step"], 2 * t - 1)
                        nc.vector.reduce_sum(inv[:, :, 1 + t:2 + t], prod[:, :, 0:t + 1], AX_X
                                             ).then_inc(S["inv_step"], 1)

                    def step(k, s):
                        dve.wait_ge(S["step_ready"], 2 * k + s + 1)
                        w = WIDTHS[s]
                        if k == 0:
                            dve.wait_ge(S["y_copied"], s + 1)
                        dst, base = (z, y) if k == 0 else (y, z)
                        nc.vector.tensor_tensor(dst[:, s, 0:w], base[:, s, 0:w], ps[:, SET_BANKS[s], 0:w], ALU.add
                                                ).then_inc(S["step_done"], 1)

                    def keep_state():
                        dve.wait_ge(S["state_ready"], 1)
                        nc.vector.tensor_tensor(state[:, 0:SET0], ps[:, SET_BANKS[0], 0:SET0],
                                                own[:, 0:4, :].rearrange("p h v -> p (h v)"), ALU.mult)
                        rows = slice(0, KEYS - P)
                        nc.vector.tensor_tensor(state[rows, SET0:VALS], ps[rows, SET_BANKS[0], SET0:VALS],
                                                own[rows, 4:DH, :].rearrange("p h v -> p (h v)"), ALU.mult
                                                ).then_inc(S["state_copied"], 1)

                    def second_values():
                        dve.wait_ge(S["ks_ready"], 1)
                        dve.wait_ge(S["step_done"], 2 * STEPS)
                        nc.vector.tensor_tensor(x1[:, 0:(DH - 1) * DV].rearrange("p (h v) -> p h v", v=DV),
                                                wides(y[:, 1])[:, :, 0:DV],
                                                ps[:, SET_BANKS[1], 0:(DH - 1) * DV].rearrange("p (h v) -> p h v", v=DV),
                                                ALU.subtract)
                        nc.vector.tensor_tensor(x1[:, (DH - 1) * DV:], y[:, 0, VALS:VALS + DV],
                                                ps[:, SET_BANKS[1], (DH - 1) * DV:VALS], ALU.subtract
                                                ).then_inc(S["x1_ready"], 1)

                    def mean_square(half):
                        dve.wait_ge(S["osq_ready"], half + 1)
                        if D_:
                            dve.wait_ge(S["o_done"], 1)
                        nc.vector.reduce_sum(ms[:, half], osq[:], AX_X).then_inc(S["summed"], 1)

                    def add_epsilon():
                        dve.wait_ge(S["summed"], HALVES)
                        nc.vector.tensor_scalar(ms[:], ms[:], 1.0 / DV, RMS_EPS, ALU.mult, ALU.add)

                    def add_out(half):
                        dve.wait_ge(S["out_ready"], HALVES)
                        xt = r.x[:, bass.ds(done * HALVES + half, 1), :].rearrange("p a d -> p (a d)")
                        nc.vector.tensor_tensor(xt, xt, ps[:, DONE_BANK, half * HID:(half + 1) * HID],
                                                ALU.add
                                                ).then_inc(S["out_added"], 1)

                    def run(on, f, *args):
                        if on:
                            f(*args)

                    def convolve(q, to):
                        for q in range(q, to):
                            run(C_, channels.conv, dve, q)

                    def convolve(q, to):
                        for q in range(q, to):
                            run(C_, channels.conv, dve, q)

                    for h in range(DH):
                        run(M_, scan, h)
                    run(N1_, n.statistics, dve, r.x, 0, 0, EARLY_TILES)
                    run(N1_, n.newton, dve, 0, 0, EARLY_TILES)
                    run(N1_, n.normalise, dve, r.x, 0, n.RING)
                    run(N2_, n.normalise, dve, r.x, n.RING, EARLY_TILES)
                    run(N2_, n.sum_batches, dve, 0)
                    run(N2_, n.sum_batches, dve, 1)
                    run(M_, last_decays)
                    for j in (1, 3):
                        run(M_, normalise_channels, dve, nc.vector, j, "kq_vector")
                    run(M_, products, 0)
                    convolve(0, 1)
                    run(M_, products, 1)
                    convolve(1, 3)
                    run(M_, products, 2)
                    convolve(3, 4)
                    run(M_, products, 3)
                    convolve(4, 5)
                    run(M_, products, 4)
                    convolve(5, 6)
                    run(M_, products, 5)
                    run(M_, fold_even)
                    run(M_, fold_odd)
                    for k in range(SUB - 1):
                        run(M_, shuffle, k)
                    run(M_, column_product, 1)
                    run(M_, keys_by_token)
                    run(M_, column_sum, 1)
                    convolve(6, 7)
                    run(M_, column_product, 2)
                    run(S_, step, 0, 0)
                    run(M_, column_sum, 2)
                    convolve(7, 8)
                    run(M_, column_product, 3)
                    run(S_, step, 0, 1)
                    run(M_, column_sum, 3)
                    convolve(8, 9)
                    run(M_, column_product, 4)
                    run(S_, step, 1, 0)
                    run(M_, column_sum, 4)
                    convolve(9, 10)
                    run(M_, column_product, 5)
                    run(S_, step, 1, 1)
                    run(M_, column_sum, 5)
                    run(M_, off_diagonal, 0)
                    run(M_, column_product, 6)
                    run(S_, step, 2, 0)
                    run(M_, column_sum, 6)
                    run(M_, off_diagonal, 1)
                    run(M_, column_product, 7)
                    run(S_, step, 2, 1)
                    run(M_, column_sum, 7)
                    run(M_, off_diagonal, 2)
                    run(M_, column_product, 8)
                    convolve(10, 11)
                    run(M_, column_sum, 8)
                    run(S_, step, 3, 0)
                    run(M_, column_product, 9)
                    convolve(11, 12)
                    run(M_, column_sum, 9)
                    run(S_, step, 3, 1)
                    run(M_, column_product, 10)
                    convolve(12, 13)
                    run(M_, column_sum, 10)
                    run(S_, keep_state)
                    run(M_, column_product, 11)
                    convolve(13, 14)
                    run(M_, column_sum, 11)
                    convolve(14, 15)
                    run(M_, column_product, 12)
                    run(S_, second_values)
                    run(M_, column_sum, 12)
                    run(S_, mean_square, 0)
                    run(M_, column_product, 13)
                    convolve(15, 16)
                    run(M_, column_sum, 13)
                    convolve(16, 17)
                    run(M_, column_product, 14)
                    convolve(17, 18)
                    run(M_, column_sum, 14)
                    convolve(18, 19)
                    run(M_, column_product, 15)
                    run(S_, mean_square, 1)
                    run(M_, column_sum, 15)
                    convolve(19, 21)
                    if M_:
                        dve.wait_ge(S["inv_step"], 2 * (SUB - 1))
                        if S_:
                            dve.wait_ge(S["y_ready"], 2)
                    run(M_, spread_inverse, nc.vector, 0, "td_vector")
                    run(S_, add_epsilon)
                    run(D_, add_out, 0)
                    run(D_, add_out, 1)
                    run(N2_, n.sum_batches, dve, 2)

                @block.scalar
                def _(act):
                    def gate_silu(k):
                        act.wait_ge(S["gates_ready"], k + 1)
                        if D_:
                            act.wait_ge(S["gated"], HALVES + 1)
                        nc.scalar.activation(gate[:, ms_, k].rearrange("p h v -> p (h v)"),
                                             ps[:, GATE_BANKS[k], 0:VALS], ACT.Silu).then_inc(S["gate_taken"], 1)

                    def norm_ln(j):
                        m = JOBS[j][1]
                        act.wait_ge(S["norms_ready"], 2 * (j // 2) + 2)
                        nc.scalar.activation(rnorm[0:m, j, :], ps[0:m, NORM_BANKS[j // 2], (j % 2) * SEQ:(j % 2 + 1) * SEQ],
                                             ACT.Ln, scale=float(DK) if j % 2 == 0 else 1.0).then_inc(S["ln_ready"], 1)

                    def norm_exp(j):
                        m = JOBS[j][1]
                        act.wait_ge(S["ln_ready"], j + 1)
                        nc.scalar.activation(rnorm[0:m, j, :], rnorm[0:m, j, :], ACT.Exp, scale=-0.5
                                             ).then_inc(S["rnorm_ready"], 1)

                    def values_by_token(k):
                        act.wait_ge(S["vT_ready"], k + 1)
                        if k == 0:
                            nc.scalar.copy(right[:, ms_, 0, 0:VALS], ps[:, V_BANKS[0], 0:VALS]
                                           ).then_inc(S["v_ready"], 1)
                        else:
                            w = (DH - 1) * DV
                            nc.scalar.copy(wides(right[:, ms_, 1])[:, :, 0:DV],
                                           ps[:, V_BANKS[1], 0:w].rearrange("p (h v) -> p h v", v=DV)
                                           ).then_inc(S["v_ready"], 1)
                            nc.scalar.copy(right[:, ms_, 0, VALS:VALS + DV], ps[:, V_BANKS[1], w:VALS]
                                           ).then_inc(S["v_ready"], 1)

                    def second_keys():
                        act.wait_ge(S["kT_ready"], 1)
                        w = (DH - 1) * DK
                        nc.scalar.copy(wides(right[:, ms_, 1])[:, :, DV:WIDE],
                                       ps[:, K_BANK, KEYS:KEYS + w].rearrange("p (h k) -> p h k", k=DK)
                                       ).then_inc(S["kg_ready"], 1)
                        nc.scalar.copy(right[:, ms_, 0, VALS + DV:SET], ps[:, K_BANK, KEYS + w:2 * KEYS]
                                       ).then_inc(S["kg_ready"], 1)

                    def copy_n(q):
                        dst, scale = ((nT, -1.0), (nN, 1.0), (n2T, -1.0))[q // PAIRS]
                        p = q % PAIRS
                        act.wait_ge(S["n_ready"], q + 1)
                        nc.scalar.mul(dst[:, p * 2 * HALVES:(p + 1) * 2 * HALVES, :].rearrange("p u t -> p (u t)"),
                                      ps[:, N_BANKS[q % 3], :], scale).then_inc(S["n_copied"], 1)

                    def copy_y(s):
                        act.wait_ge(S["y_ready"], s + 1)
                        nc.scalar.copy(y[:, s, 0:WIDTHS[s]], ps[:, SET_BANKS[s], 0:WIDTHS[s]]
                                       ).then_inc(S["y_copied"], 1)

                    def solved_keys():
                        act.wait_ge(S["step_done"], 2 * STEPS)
                        w = (DH - 1) * DK
                        nc.scalar.copy(wk[:, 0:w].rearrange("p (h k) -> p h k", k=DK), wides(y[:, 1])[:, :, DV:WIDE]
                                       ).then_inc(S["wk_ready"], 1)
                        nc.scalar.copy(wk[:, w:KEYS], y[:, 0, VALS + DV:SET]).then_inc(S["wk_ready"], 1)

                    def copy_wkT():
                        act.wait_ge(S["wkT_ready"], 1)
                        nc.scalar.copy(wkT[:, 0, :], ps[:, SET_BANKS[1], 0:P]).then_inc(S["wkT_copied"], 1)
                        nc.scalar.copy(wkT[0:KEYS - P, 1, :], ps[0:KEYS - P, SET_BANKS[1], P:2 * P]
                                       ).then_inc(S["wkT_copied"], 1)

                    def squares(half):
                        act.wait_ge(S["o_ready"], half + 1)
                        if half:
                            act.wait_ge(S["summed"], 1)
                        nc.scalar.activation(osq[:].rearrange("p h v -> p (h v)"), ps[:, O_BANKS[half], 0:VALS],
                                             ACT.Square).then_inc(S["osq_ready"], 1)

                    def save_output(half):
                        if D_:
                            act.wait_ge(S["oT_ready"], HALVES)
                        nc.scalar.copy(o[:, half].rearrange("p h v -> p (h v)"), ps[:, O_BANKS[half], 0:VALS]
                                       ).then_inc(S["saved"], 1)

                    def root():
                        nc.scalar.activation(ms[:], ms[:], ACT.Ln).then_inc(S["root_ready"], 1)
                        act.wait_ge(S["root_ready"], 1)
                        nc.scalar.activation(ms[:], ms[:], ACT.Exp, scale=-0.5).then_inc(S["root_ready"], 1)

                    def copy_oT(half):
                        act.wait_ge(S["oT_ready"], half + 1)
                        nc.scalar.copy(oT[:, half].rearrange("p c t -> p (c t)"), ps[:, TURNED_BANKS[half], 0:VALS]
                                       ).then_inc(S["oT_copied"], 1)

                    def run(on, f, *args):
                        if on:
                            f(*args)

                    nc.scalar.preload_act_table_set("natural_log_exp_and_others")
                    run(D_, root)
                    for j in range(QK_JOBS):
                        run(M_, norm_ln, j)
                    for j in range(QK_JOBS):
                        run(M_, norm_exp, j)
                    if M_ and C_:
                        act.wait_ge(S["kq_pool"], 2)
                        act.wait_ge(S["kq_vector"], 2)
                    run(C_, channels.tap, act, 0)
                    run(C_, channels.tap, act, 1)
                    run(S_, copy_n, 0)
                    run(S_, copy_n, 1)
                    for q in range(2, PAIRS + 1):
                        run(S_, copy_n, q)
                    run(N2_, n.copy, act, ps, 0)
                    run(D_, copy_oT, 0)
                    run(D_, copy_oT, 1)
                    run(N1_, n.root, act, 0, 0, EARLY_TILES)
                    run(N2_, n.copy, act, ps, 1)
                    run(N2_, n.copy, act, ps, 2)
                    for q in range(PAIRS + 1, 3 * PAIRS):
                        run(S_, copy_n, q)
                    run(S_, copy_y, 0)
                    run(C_, channels.tap, act, 2)
                    run(C_, channels.tap, act, 3)
                    run(S_, copy_y, 1)
                    run(M_, second_keys)
                    run(M_, values_by_token, 0)
                    run(M_, values_by_token, 1)
                    run(C_, channels.silu, act, 0)
                    run(C_, channels.silu, act, 1)
                    run(C_, channels.tap, act, 4)
                    run(C_, channels.tap, act, 5)
                    run(S_, solved_keys)
                    run(S_, copy_wkT)
                    run(S_, squares, 0)
                    run(S_, save_output, 0)
                    run(C_, channels.tap, act, 6)
                    run(C_, channels.silu, act, 2)
                    run(C_, channels.silu, act, 3)
                    run(S_, squares, 1)
                    run(S_, save_output, 1)
                    run(C_, channels.silu, act, 4)
                    run(M_, gate_silu, 0)
                    run(C_, channels.silu, act, 5)
                    run(C_, channels.silu, act, 6)
                    run(M_, gate_silu, 1)

                @block.tensor
                def _(pe):
                    def norms(j):
                        m = JOBS[j][1]
                        nc.tensor.matmul(ps[0:m, NORM_BANKS[j // 2], (j % 2) * SEQ:(j % 2 + 1) * SEQ],
                                         head_ones[0:m, 0:m], square[0:m, j, :], start=True, stop=True
                                         ).then_inc(S["norms_ready"], 1)

                    def scores(h):
                        rows = slice((h % 4) * DK, (h % 4 + 1) * DK)
                        if h == 0:
                            pe.wait_ge(S["kq_pool"], 2)
                            pe.wait_ge(S["kq_vector"], 2)
                        if h >= 2:
                            pe.wait_ge(S["aq_ready"], HALVES * (h - 1))
                        for k in range(HALVES):
                            mm = nc.tensor.matmul(ps[:, SCORE_BANKS[h % 2], k * 2 * P:(k + 1) * 2 * P],
                                                  kq[rows, h // 4, 0, half_cols(k)], kq[rows, h // 4, :, half_cols(k)],
                                                  start=True, stop=True)
                        mm.then_inc(S["scores_ready"], 1)

                    def turn_keys():
                        pe.wait_ge(S["kqg_ready"], 2)
                        if S_:
                            pe.wait_ge(S["n_copied"], 7)
                        m = KEYS - P
                        nc.tensor.transpose(ps[:, K_BANK, 0:P], kq[:, 0, 0, 0:P], r.ident[:])
                        nc.tensor.transpose(ps[:, K_BANK, P:KEYS], kq[0:m, 1, 0, 0:P], r.ident[0:m, 0:m])
                        nc.tensor.transpose(ps[:, K_BANK, KEYS:KEYS + P], kqg[:, ms_, 0, 0, :], r.ident[:])
                        nc.tensor.transpose(ps[:, K_BANK, KEYS + P:2 * KEYS], kqg[0:m, ms_, 1, 0, :],
                                            r.ident[0:m, 0:m]).then_inc(S["kT_ready"], 1)

                    def turn_values(k):
                        if S_:
                            pe.wait_ge(S["n_copied"], 8 + k)
                        for c in range(VALS // P):
                            mm = nc.tensor.transpose(ps[:, V_BANKS[k], c * P:(c + 1) * P],
                                                     chan[:, QK_JOBS + c, half_cols(k)], r.ident[:])
                        mm.then_inc(S["vT_ready"], 1)

                    def turn_low(p):
                        pe.wait_ge(S["aq_ready"], (10, 12, 12)[p])
                        if p == 2:
                            pe.wait_ge(S["ktok_ready"], 1)
                        for u in range(2 * HALVES):
                            mm = nc.tensor.transpose(ps[:, L_BANKS[p], u * P:(u + 1) * P],
                                                     aq[:, ms_, p * 2 * HALVES + u, 0, :], r.ident[:])
                        mm.then_inc(S["lT_ready"], 1)

                    def gates(k):
                        pe.wait_ge(S["xb_ready"], 2)
                        pe.wait_ge(S["l_ready"], k + 2)
                        for c in range(DC):
                            mm = nc.tensor.matmul(ps[:, GATE_BANKS[k], 0:VALS], xb[:, c, half_cols(k)], wgate[:, c, :],
                                                  start=(c == 0), stop=(c == DC - 1))
                        mm.then_inc(S["gates_ready"], 1)

                    def job(j):
                        if M_ and j == 4:
                            pe.wait_ge(S["v_ready"], 3)
                        if M_ and j == 6:
                            pe.wait_ge(S["l_ready"], 1)
                        channels.job(pe, j, bass.ds(first * SEQ, SEQ))

                    def n_product(q):
                        kind, p = divmod(q, PAIRS)
                        if kind:
                            pe.wait_ge(S["n_copied"], q - 2)
                        if kind == 2:
                            pe.wait_ge(S["n_copied"], PAIRS + p + 1)
                        for k in range(2 * HALVES):
                            u = p * 2 * HALVES + k
                            lhsT, rhs_ = ((low[:, ls, u, :], tdT[:, u, :]), (tdT[:, u, :], low[:, ls, u, :]),
                                          (nN[:, u, :], nT[:, u, :]))[kind]
                            mm = nc.tensor.matmul(ps[:, N_BANKS[q % 3], k * P:(k + 1) * P], lhsT, rhs_,
                                                  start=True, stop=True)
                        mm.then_inc(S["n_ready"], 1)

                    def multiply(s, mat, src, signal):
                        for h, half, cols in rights(s):
                            mm = nc.tensor.matmul(ps[:, SET_BANKS[s], cols], mat[:, h * HALVES + half, :],
                                                  src[:, cols], start=True, stop=True)
                        mm.then_inc(S[signal], 1)

                    def solve_blocks(s):
                        if D_:
                            pe.wait_ge(S["oT_copied"], s + 1)
                        multiply(s, tdT, right[:, ls, s], "y_ready")

                    def step(k, s):
                        if k == 0:
                            pe.wait_ge(S["y_copied"], s + 1)
                            pe.wait_ge(S["n_copied"], PAIRS)
                        else:
                            pe.wait_ge(S["step_done"], 2 * (k - 1) + s + 1)
                            pe.wait_ge(S["n_copied"], 3 * PAIRS)
                        multiply(s, nT if k == 0 else n2T, (z if k == 1 else y)[:, s], "step_ready")

                    def new_state():
                        pe.wait_ge(S["step_done"], 2 * (STEPS - 1) + 1)
                        nc.tensor.matmul(ps[:, SET_BANKS[0], 0:SET0], ktok[:, ls, 0:4, :].rearrange("p h k -> p (h k)"),
                                         y[:, 0, 0:SET0], start=True, stop=True)
                        nc.tensor.matmul(ps[0:KEYS - P, SET_BANKS[0], SET0:VALS],
                                         ktok[:, ls, 4:DH, :].rearrange("p h k -> p (h k)"),
                                         y[:, 0, SET0:VALS], start=True, stop=True).then_inc(S["state_ready"], 1)

                    def turn_solved_keys():
                        pe.wait_ge(S["wk_ready"], 2)
                        nc.tensor.transpose(ps[:, SET_BANKS[1], 0:P], wk[:, 0:P], r.ident[:])
                        nc.tensor.transpose(ps[0:KEYS - P, SET_BANKS[1], P:2 * P], wk[:, P:KEYS], r.ident[:]
                                            ).then_inc(S["wkT_ready"], 1)

                    def known():
                        pe.wait_ge(S["state_copied"], 1)
                        pe.wait_ge(S["wkT_copied"], 2)
                        m = KEYS - P
                        nc.tensor.matmul(ps[:, SET_BANKS[1], 0:SET0], wkT[:, 0, :], state[:, 0:SET0],
                                         start=True, stop=True)
                        nc.tensor.matmul(ps[:, SET_BANKS[1], SET0:VALS], wkT[0:m, 1, :], state[0:m, SET0:VALS],
                                         start=True, stop=True).then_inc(S["ks_ready"], 1)

                    def outputs(half):
                        if M_ and not half:
                            pe.wait_ge(S["v_ready"], 1)
                        if half:
                            for hs, cols in HEAD_SETS:
                                nc.tensor.matmul(ps[:, O_BANKS[1], cols], kqg[:, ls, hs, 1, :], state[:, cols],
                                                 start=(hs == 0), stop=False, skip_group_check=True)
                            pe.wait_ge(S["x1_ready"], 1)
                        for h in range(DH):
                            src = x1[:, head_cols(h)] if half else y[:, 0, head_cols(h)]
                            mm = nc.tensor.matmul(ps[:, O_BANKS[half], head_cols(h)],
                                                  aq[:, ls, h * HALVES + half, 1, :], src, start=not half, stop=True,
                                                  skip_group_check=bool(half))
                        mm.then_inc(S["o_ready"], 1)

                    def turn_out(half):
                        pe.wait_ge(S["o_done"], 1)
                        of = o[:, half].rearrange("p h v -> p (h v)")
                        for c in range(VALS // P):
                            mm = nc.tensor.transpose(ps[:, TURNED_BANKS[half], c * P:(c + 1) * P],
                                                     of[:, c * P:(c + 1) * P], r.ident[:])
                        mm.then_inc(S["oT_ready"], 1)

                    def project_out(half):
                        pe.wait_ge(S["oT_copied"], half + 1)
                        if C_:
                            pe.wait_ge(S["conv_step"], (TAPS - 1) * QK_JOBS)
                        for c in range(VALS // P):
                            mm = nc.tensor.matmul(ps[:, DONE_BANK, half * HID:(half + 1) * HID], oT[:, half, c, :], wo[:, c, :],
                                                  start=(c == 0), stop=(c == VALS // P - 1))
                        mm.then_inc(S["out_ready"], 1)

                    def run(on, f, *args):
                        if on:
                            f(*args)

                    for j in range(QK_JOBS):
                        run(M_, norms, j)
                    run(C_, job, 0)
                    run(C_, job, 1)
                    run(S_, n_product, 0)
                    run(M_, scores, 0)
                    run(S_, n_product, 1)
                    run(M_, scores, 1)
                    run(S_, n_product, 2)
                    run(M_, scores, 2)
                    run(S_, n_product, 3)
                    run(M_, scores, 3)
                    run(N2_, n.turn, pe, ps, r.ident, 0)
                    run(N2_, n.turn, pe, ps, r.ident, 1)
                    run(D_, turn_out, 0)
                    run(D_, turn_out, 1)
                    run(N2_, n.turn, pe, ps, r.ident, 2)
                    run(S_, n_product, 4)
                    run(M_, scores, 4)
                    run(S_, n_product, 5)
                    run(M_, scores, 5)
                    for q in range(2 * PAIRS, 3 * PAIRS):
                        run(S_, n_product, q)
                    run(S_, solve_blocks, 0)
                    run(C_, job, 2)
                    run(C_, job, 3)
                    run(S_, solve_blocks, 1)
                    run(M_, turn_keys)
                    run(S_, step, 0, 0)
                    run(M_, turn_values, 0)
                    run(S_, step, 0, 1)
                    run(M_, turn_values, 1)
                    run(S_, step, 1, 0)
                    run(M_, turn_low, 0)
                    run(S_, step, 1, 1)
                    run(M_, turn_low, 1)
                    run(S_, step, 2, 0)
                    run(M_, turn_low, 2)
                    run(S_, step, 2, 1)
                    run(C_, job, 4)
                    run(S_, step, 3, 0)
                    run(C_, job, 5)
                    run(S_, step, 3, 1)
                    run(S_, new_state)
                    run(D_, project_out, 0)
                    run(S_, turn_solved_keys)
                    run(S_, outputs, 0)
                    run(S_, known)
                    run(C_, job, 6)
                    run(D_, project_out, 1)
                    run(S_, outputs, 1)
                    run(M_, gates, 0)
                    run(M_, gates, 1)
            end_of_round(nc, round_sems)

        stage(1, 0, 0, None, None, None, None)
        stage(2, 1, 1, 0, 0, None, None)
        with nc.Fori(0, BATCH // 2 - 2) as i:
            stage(i * 2 + 3, i * 2 + 2, 0, i * 2 + 1, 1, i * 2, 0)
            stage(i * 2 + 4, i * 2 + 3, 1, i * 2 + 2, 0, i * 2 + 1, 1)
        stage(BATCH - 1, BATCH - 2, 0, BATCH - 3, 1, BATCH - 4, 0)
        stage(None, BATCH - 1, 1, BATCH - 2, 0, BATCH - 3, 1)
        stage(None, None, None, BATCH - 1, 1, BATCH - 2, 0)
        stage(None, None, None, None, None, BATCH - 1, 1)
        end_of_round(nc, [spread])


EXPERTS, FF, TOP = 6, 176, 2
FF1 = FF - P
BIAS_ROW = 64
W1_AT, W2_AT, B1_AT = 0, DC * FF, DC * FF + 2 * HID
PACKED = B1_AT + 2
ROUND_BATCHES = 4


def routed(nc, r, n, packed, w_gate, out):
    with ExitStack() as ctx:
        def sb(name, shape, dt=F32):
            return ctx.enter_context(nc.sbuf_tensor("d_" + name, shape, dt))

        def sem(name):
            return ctx.enter_context(nc.semaphore("d_" + name))

        ps = ctx.enter_context(nc.psum_tensor("d_ps", [P, 8, 512], F32))
        HIDDEN, OUT = (0, 1, 2, 3), (4, 5)
        gate_w = sb("gate_w", [P, DC, EXPERTS])
        xnT, sums = n.xnT, n.sums
        BE = [1, BATCH, EXPERTS]
        rank_of, index_of = sb("rank_of", [1, 1, EXPERTS]), sb("index_of", [1, 1, EXPERTS])
        prob, eq, key, picked, rest, part = [sb(x, BE) for x in ("prob", "eq", "key", "picked", "rest", "part")]
        top, best, total = [sb(x, [1, BATCH, 1]) for x in ("top", "best", "total")]
        chosen, chosen_f = sb("chosen", [1, BATCH * TOP], I32), sb("chosen_f", [1, BATCH, TOP])
        weight = sb("weight", [1, BATCH, TOP])
        weights = sb("weights", [P, BATCH * TOP])
        slots = sb("slots", [P, ROUND_BATCHES * TOP, PACKED])
        gelu = sb("gelu", [P, 2, 2, SEQ])
        hid = sb("hid", [P, 2 * TOP, 2, SEQ])

        gate_loaded, zeroed = sem("gate_loaded"), sem("zeroed")
        logits_ready, exp_ready, shifted, weight_ready, spread_ready, route_done = [
            sem(x) for x in ("logits_ready", "exp_ready", "shifted", "weight_ready", "spread_ready", "route_done")]
        names = ("hidden_ready gelu_done hid_ready out_ready added stored").split()
        S = {x: sem(x) for x in names}
        slot_loaded = [sem(f"slot_loaded{j}") for j in range(ROUND_BATCHES * TOP)]

        LOGITS, SPREAD = 4, 5
        with nc.Block() as block:
            @block.sync
            def _(sp):
                sp.dma_start(gate_w[:], w_gate.rearrange("(c p) e -> p c e", p=P)).then_inc(gate_loaded, 16)

            @block.tensor
            def _(pe):
                n.turn(pe, ps, r.ident, GROUPS - 1)
                pe.wait_ge(n.summed, GROUPS)
                pe.wait_ge(gate_loaded, 16)
                for b in range(BATCH):
                    for c in range(DC):
                        mm = nc.tensor.matmul(ps[0:1, LOGITS, b * EXPERTS:(b + 1) * EXPERTS], sums[:, c, b:b + 1],
                                              gate_w[:, c, :], start=(c == 0), stop=(c == DC - 1))
                mm.then_inc(logits_ready, 1)
                pe.wait_ge(weight_ready, 1)
                nc.tensor.matmul(ps[:, SPREAD, 0:BATCH * TOP], r.ones_row[:], weight[:].rearrange("o b k -> o (b k)"),
                                 start=True, stop=True).then_inc(spread_ready, 1)

            @block.scalar
            def _(act):
                nc.scalar.preload_act_table_set("natural_log_exp_and_others")
                n.root(act, 1, EARLY_TILES, TILES)
                n.copy(act, ps, GROUPS - 1)
                act.wait_ge(shifted, 1)
                nc.scalar.activation(prob[:], prob[:], ACT.Exp, scale=1.0 / SEQ).then_inc(exp_ready, 1)

            @block.gpsimd
            def _(pool):
                nc.gpsimd.memset(hid[:], 0.0)
                nc.gpsimd.iota(index_of[:], pattern=[[1, EXPERTS]], base=0, channel_multiplier=0,
                               allow_small_or_imprecise_dtypes=True)
                nc.gpsimd.iota(rank_of[:], pattern=[[-1, EXPERTS]], base=EXPERTS, channel_multiplier=0,
                               allow_small_or_imprecise_dtypes=True).then_inc(zeroed, 1)

            @block.vector
            def _(dve):
                done = [0]

                def link(ins):
                    done[0] += 1
                    ins.then_inc(route_done, 1)
                    dve.wait_ge(route_done, done[0])

                n.statistics(dve, r.x, 1, EARLY_TILES, TILES)
                n.newton(dve, 1, EARLY_TILES, TILES)
                n.normalise(dve, r.x, EARLY_TILES, TILES)
                n.sum_batches(dve, GROUPS - 1)
                dve.wait_ge(logits_ready, 1)
                dve.wait_ge(zeroed, 1)
                logits = ps[0:1, LOGITS, 0:BATCH * EXPERTS].rearrange("o (b e) -> o b e", b=BATCH)
                link(nc.vector.reduce_max(top[:], logits, AX_X))
                nc.vector.tensor_tensor(prob[:], logits, top[:].to_broadcast(BE), ALU.subtract).then_inc(shifted, 1)
                dve.wait_ge(exp_ready, 1)
                link(nc.vector.reduce_sum(total[:], prob[:], AX_X))
                link(nc.vector.reciprocal(total[:], total[:]))
                link(nc.vector.tensor_tensor(prob[:], prob[:], total[:].to_broadcast(BE), ALU.mult))

                def pick(values, k):
                    link(nc.vector.reduce_max(top[:], values[:], AX_X))
                    link(nc.vector.tensor_tensor(eq[:], values[:], top[:].to_broadcast(BE), ALU.is_equal))
                    link(nc.vector.tensor_tensor(key[:], eq[:], rank_of[:].to_broadcast(BE), ALU.mult))
                    link(nc.vector.reduce_max(best[:], key[:], AX_X))
                    link(nc.vector.tensor_tensor(picked[:], key[:], best[:].to_broadcast(BE), ALU.is_equal))
                    link(nc.vector.tensor_tensor(part[:], picked[:], index_of[:].to_broadcast(BE), ALU.mult))
                    link(nc.vector.reduce_sum(chosen_f[:, :, k:k + 1], part[:], AX_X))
                    link(nc.vector.tensor_copy(weight[:, :, k:k + 1], top[:]))

                pick(prob, 0)
                link(nc.vector.scalar_tensor_tensor(rest[:], picked[:], -4.0, prob[:], ALU.mult, ALU.add))
                pick(rest, 1)
                link(nc.vector.reduce_sum(total[:], weight[:], AX_X))
                link(nc.vector.reciprocal(total[:], total[:]))
                nc.vector.tensor_tensor(weight[:], weight[:], total[:].to_broadcast([1, BATCH, TOP]),
                                        ALU.mult).then_inc(weight_ready, 1)
                nc.vector.tensor_copy(chosen[:], chosen_f[:].rearrange("o b k -> o (b k)"))
                dve.wait_ge(spread_ready, 1)
                nc.vector.tensor_copy(weights[:], ps[:, SPREAD, 0:BATCH * TOP])

        with nc.Fori(0, BATCH // ROUND_BATCHES) as i:
            with nc.Block() as block:
                @block.sync
                def _(sp):
                    for j in range(ROUND_BATCHES * TOP):
                        e = sp.value_load(chosen[0:1, bass.ds(i * ROUND_BATCHES * TOP + j, 1)],
                                          min_val=0, max_val=EXPERTS - 1)
                        sp.dma_start(slots[:, j, :], packed[bass.ds(e, 1)].rearrange("e p n -> p (e n)")
                                     ).then_inc(slot_loaded[j], 16)
                    for b in range(ROUND_BATCHES):
                        sp.wait_ge(S["added"], 2 * (b + 1))
                        sp.dma_start(out[bass.ds(i * ROUND_BATCHES + b, 1)].rearrange("b (h p) d -> p (b h) d", p=P),
                                     r.x[:, bass.ds(i * ROUND_BATCHES * 2 + 2 * b, 2), :]).then_inc(S["stored"], 16)
                    sp.wait_ge(S["stored"], 16 * ROUND_BATCHES)

                @block.tensor
                def _(pe):
                    def hidden(j):
                        pe.wait_ge(slot_loaded[j], 16)
                        if j >= 4:
                            pe.wait_ge(S["gelu_done"], 2 * (j - 3))
                        for m, rows in enumerate((P, FF1)):
                            for c in range(DC):
                                mm = nc.tensor.matmul(
                                    ps[0:rows, HIDDEN[j % 4], m * SEQ:(m + 1) * SEQ],
                                    slots[:, j, c * FF + m * P:c * FF + m * P + rows],
                                    xnT[:, c, bass.ds((i * ROUND_BATCHES + j // TOP) * SEQ, SEQ)],
                                    start=(c == 0), stop=(c == DC - 1))
                        mm.then_inc(S["hidden_ready"], 1)

                    def down(b):
                        pe.wait_ge(S["hid_ready"], TOP * (b + 1))
                        for t in range(2):
                            job = 2 * b + t
                            if job >= 2:
                                pe.wait_ge(S["added"], job - 1)
                            for k in range(TOP):
                                j = b * TOP + k
                                cols = slice(t * P, (t + 1) * P)
                                nc.tensor.matmul(ps[:, OUT[job % 2], 0:HID], hid[:, j % 4, 0, cols],
                                                 slots[:, j, W2_AT:W2_AT + HID], start=(k == 0), stop=False)
                                mm = nc.tensor.matmul(ps[:, OUT[job % 2], 0:HID], hid[:, j % 4, 1, cols],
                                                      slots[:, j, W2_AT + HID:W2_AT + 2 * HID],
                                                      start=False, stop=(k == TOP - 1))
                            mm.then_inc(S["out_ready"], 1)

                    for b in range(ROUND_BATCHES + 1):
                        if b < ROUND_BATCHES:
                            for k in range(TOP):
                                hidden(b * TOP + k)
                        if b >= 1:
                            down(b - 1)

                @block.scalar
                def _(act):
                    for j in range(ROUND_BATCHES * TOP):
                        act.wait_ge(S["hidden_ready"], j + 1)
                        if j >= 2:
                            act.wait_ge(S["hid_ready"], j - 1)
                        for m, rows in enumerate((P, FF1)):
                            nc.scalar.activation(gelu[0:rows, j % 2, m, :], ps[0:rows, HIDDEN[j % 4], m * SEQ:(m + 1) * SEQ],
                                                 ACT.Gelu, bias=slots[0:rows, j, B1_AT + m:B1_AT + m + 1]
                                                 ).then_inc(S["gelu_done"], 1)

                @block.vector
                def _(dve):
                    def weighted(j):
                        dve.wait_ge(S["gelu_done"], 2 * (j + 1))
                        if j >= 4:
                            dve.wait_ge(S["out_ready"], 2 * ((j - 4) // TOP + 1))
                        w_at = i * ROUND_BATCHES * TOP + j
                        nc.vector.tensor_scalar(hid[:, j % 4, 0, :], gelu[:, j % 2, 0, :],
                                                weights[:, bass.ds(w_at, 1)], None, ALU.mult)
                        nc.vector.tensor_copy(hid[BIAS_ROW:BIAS_ROW + 1, j % 4, 1, :],
                                              weights[BIAS_ROW:BIAS_ROW + 1, bass.ds(w_at, 1)].to_broadcast([1, SEQ]))
                        nc.vector.tensor_scalar(hid[0:FF1, j % 4, 1, :], gelu[0:FF1, j % 2, 1, :],
                                                weights[0:FF1, bass.ds(w_at, 1)], None, ALU.mult
                                                ).then_inc(S["hid_ready"], 1)

                    def add(b):
                        for t in range(2):
                            job = 2 * b + t
                            dve.wait_ge(S["out_ready"], job + 1)
                            xt = r.x[:, bass.ds(i * ROUND_BATCHES * 2 + job, 1), :].rearrange("p a d -> p (a d)")
                            nc.vector.tensor_tensor(xt, xt, ps[:, OUT[job % 2], 0:HID], ALU.add
                                                    ).then_inc(S["added"], 1)

                    for b in range(ROUND_BATCHES + 1):
                        if b < ROUND_BATCHES:
                            for k in range(TOP):
                                weighted(b * TOP + k)
                        if b >= 1:
                            add(b - 1)
            end_of_round(nc, list(S.values()) + slot_loaded)


def build(nc, a, out):
    with ExitStack() as ctx:
        r = Resident(nc, ctx)
        setup(nc, a["hidden"], r)
        with ExitStack() as first_layer:
            ahead = Ahead(nc, first_layer, r.first_xnT)
            gate_up = GateUpWeights(nc, first_layer, a["B_g"], a["B_u"])
            attention(nc, r, ahead, gate_up, a["hidden"], a["A_q"], a["A_k"], a["A_v"], a["A_o"], a["A_bo"])
            experts(nc, r, ahead, gate_up, a["B_d"], a["B_ga"], a["B_gb"], a["B_ua"], a["B_ub"], a["B_da"],
                    a["B_db"], a["B_r"], a["B_temp"])
        n = NormAll(nc, ctx)
        delta(nc, r, n, a["C_q"], a["C_k"], a["C_v"], a["C_a"], a["C_b"], a["C_g"], a["C_o"], a["C_cq"], a["C_ck"],
              a["C_cv"], a["C_alog"], a["C_dt"], a["C_nw"])
        routed(nc, r, n, a["D_packed"], a["D_gate"], out)


def kernel(**inputs):
    import numpy as np
    import concourse.bacc as bacc
    from concourse.bass_utils import run_bass_kernel_spmd

    def layer(prefix):
        return {k[len(prefix):]: np.asarray(v) for k, v in inputs.items() if k.startswith(prefix)}

    A, B, C, D = layer("L0_attn_"), layer("L0_ffn_"), layer("L1_attn_"), layer("L1_ffn_")
    packed = np.zeros((EXPERTS, P, PACKED), D["W1"].dtype)
    for c in range(DC):
        packed[:, :, c * FF:(c + 1) * FF] = D["W1"][:, c * P:(c + 1) * P, :]
    packed[:, :, W2_AT:W2_AT + HID] = D["W2"][:, 0:P, :]
    packed[:, 0:FF1, W2_AT + HID:W2_AT + 2 * HID] = D["W2"][:, P:FF, :]
    packed[:, BIAS_ROW, W2_AT + HID:W2_AT + 2 * HID] = D["b2"]
    packed[:, :, B1_AT] = D["b1"][:, 0:P]
    packed[:, 0:FF1, B1_AT + 1] = D["b1"][:, P:FF]
    arrays = {
        "hidden": A["hidden_states"],
        "A_q": A["Wq"].T, "A_k": A["Wk"].T, "A_v": A["Wv"].T, "A_o": A["Wo"].T, "A_bo": A["bo"],
        "B_g": B["Wg"], "B_u": B["Wu"], "B_d": B["Wd"],
        "B_ga": B["Ga"].transpose(0, 2, 1), "B_gb": B["Gb"], "B_ua": B["Ua"].transpose(0, 2, 1), "B_ub": B["Ub"],
        "B_da": B["Da"].transpose(0, 2, 1), "B_db": B["Db"], "B_r": B["Wr"], "B_temp": B["temperature"],
        "C_q": C["Wq"], "C_k": C["Wk"], "C_v": C["Wv"], "C_a": C["Wa"], "C_b": C["Wb"], "C_g": C["Wg"],
        "C_o": C["Wo"], "C_cq": C["conv_wq"], "C_ck": C["conv_wk"], "C_cv": C["conv_wv"], "C_alog": C["A_log"],
        "C_dt": C["dt_bias"], "C_nw": C["norm_weight"],
        "D_packed": packed, "D_gate": D["gate_W"].T,
    }
    nc = bacc.Bacc("TRN2", target_bir_lowering=False, num_devices=1)
    arrays = {"in_" + k: np.ascontiguousarray(v) for k, v in arrays.items()}
    dram = {k[3:]: nc.dram_tensor(k, v.shape, mybir.dt.from_np(v.dtype), kind="ExternalInput").ap()
            for k, v in arrays.items()}
    out = nc.dram_tensor("out", (BATCH, SEQ, HID), F32, kind="ExternalOutput").ap()
    build(nc, dram, out)
    return run_bass_kernel_spmd(nc, [arrays], core_ids=[0]).results[0]["out"]
```
